# Optimizing a Trainium2 kernel written in Bass

```python
import numpy as np
import jax
import jax.numpy as jnp

def _softmax(x, axis=-1):
    return jax.nn.softmax(x, axis=axis)

def _gelu(x):
    return jax.nn.gelu(x, approximate=True)

def _silu(x):
    return jax.nn.silu(x)

def _sigmoid(x):
    return jax.nn.sigmoid(x)

def _layernorm(x, axis=-1, eps=1e-05):
    m = jnp.mean(x, axis=axis, keepdims=True)
    v = jnp.var(x, axis=axis, keepdims=True)
    return (x - m) / jnp.sqrt(v + eps)

def _scatter_add(tgt, idx, src, axis=0):
    return tgt.at[idx].add(src)

def _segment_sum(src, seg, n):
    return jax.ops.segment_sum(src, seg, n)
kernel_name = 'mk_decoder_preln_d2_seqx_r8_722e11'

def setup_inputs(seed: int=0):
    np.random.seed(seed)
    _w = jnp.asarray

    def _rec_inputs():
        import jax
        import jax.numpy as jnp
        _rk = jax.random.key(seed)
        x = 0.002226 + 0.9996 * jax.random.normal(jax.random.fold_in(_rk, 1), (2, 512, 128), jnp.float32)
        _lenS = 512 - jax.random.randint(jax.random.fold_in(_rk, 7), (2,), 0, max(1, 512 // 4) + 1, jnp.int32)
        _lenS2 = 77 - jax.random.randint(jax.random.fold_in(_rk, 8), (2,), 0, max(1, 77 // 4) + 1, jnp.int32)
        _ctx_1024P = jax.random.normal(jax.random.fold_in(_rk, 11), (2, 16, 128), jnp.float32)
        _ctx_1024c = jax.random.dirichlet(jax.random.fold_in(_rk, 511), 0.3 * jnp.ones((16,), jnp.float32), (2, 77))
        _ctx_1024t = jnp.einsum('bsk,bkd->bsd', _ctx_1024c, _ctx_1024P)
        _ctx_1024t = _ctx_1024t * jax.lax.rsqrt(jnp.mean(jnp.square(_ctx_1024t)) + 1e-12) * 0.953939
        ctx_1024 = -0.000125008 + 0.999885 * (_ctx_1024t + 0.3 * jax.random.normal(jax.random.fold_in(_rk, 611), (2, 77, 128), jnp.float32))
        _validS = jnp.arange(512)[None, :] < _lenS[:, None]
        _validS2 = jnp.arange(77)[None, :] < _lenS2[:, None]
        _causal = jnp.tril(jnp.ones((512, 512), dtype=bool))
        mask_BxSxS2_ik1 = jnp.where(jnp.broadcast_to(_validS2[:, None, :], (2, 512, 77)), 1, 0).astype(jnp.int32)
        return (x, ctx_1024, mask_BxSxS2_ik1)
    x, ctx_1024, mask_BxSxS2_ik1 = _rec_inputs()

    def _L0_attn_setup():
        import jax, jax.numpy as jnp
        import numpy as np
        DIM = 128
        HEADS = 16
        EPS = 1e-12
        key = jax.random.key(seed)
        ks = jax.random.split(key, 6)
        b, n, dim, h = (2, 256, DIM, HEADS)
        x = jax.random.normal(ks[0], (b, n, dim), dtype=jnp.float32)
        w_qkv = jax.random.normal(ks[1], (3 * dim, dim), dtype=jnp.float32) / np.sqrt(dim)
        w_out = jax.random.normal(ks[2], (dim, dim), dtype=jnp.float32) / np.sqrt(dim)
        b_out = jax.random.normal(ks[3], (dim,), dtype=jnp.float32) * 0.02
        norm_g = jnp.ones((1, h, 1, 1), dtype=jnp.float32)
        norm_b = jnp.zeros((1, h, 1, 1), dtype=jnp.float32)
        return {'x': x, 'w_qkv': w_qkv, 'w_out': w_out, 'b_out': b_out, 'norm_g': norm_g, 'norm_b': norm_b}
    _L0_attn_all = _L0_attn_setup()
    _L0_attn_in = {k: v for k, v in _L0_attn_all.items() if k in ('w_qkv', 'w_out', 'b_out', 'norm_g', 'norm_b')}
    del _L0_attn_all

    def _L0_xattn_setup():
        import jax, jax.numpy as jnp
        import numpy as np
        B, M, N, DIM, DH, H = (8, 512, 64, 128, 128, 8)
        INNER = DH * H
        EPS = 1e-05

        def _layernorm(x, g, b):
            mu = jnp.mean(x, axis=-1, keepdims=True)
            var = jnp.var(x, axis=-1, keepdims=True)
            return (x - mu) * jax.lax.rsqrt(var + EPS) * g + b
        key = jax.random.key(seed)
        ks = jax.random.split(key, 8)
        sd = 0.02
        return {'x': jax.random.normal(ks[0], (B, M, DIM), jnp.float32), 'latents': jax.random.normal(ks[1], (B, N, DIM), jnp.float32), 'gamma_media': jnp.ones((DIM,), jnp.float32), 'beta_media': jnp.zeros((DIM,), jnp.float32), 'gamma_lat': jnp.ones((DIM,), jnp.float32), 'beta_lat': jnp.zeros((DIM,), jnp.float32), 'Wq': jax.random.normal(ks[2], (DIM, INNER), jnp.float32) * sd, 'bq': jnp.zeros((INNER,), jnp.float32), 'Wkv': jax.random.normal(ks[3], (DIM, 2 * INNER), jnp.float32) * sd, 'bkv': jnp.zeros((2 * INNER,), jnp.float32), 'Wo': jax.random.normal(ks[4], (INNER, DIM), jnp.float32) * sd, 'bo': jnp.zeros((DIM,), jnp.float32)}
    _L0_xattn_all = _L0_xattn_setup()
    _L0_xattn_in = {k: v for k, v in _L0_xattn_all.items() if k in ('gamma_media', 'beta_media', 'gamma_lat', 'beta_lat', 'Wq', 'bq', 'Wkv', 'bkv', 'Wo', 'bo')}
    del _L0_xattn_all

    def _L0_ffn_setup():
        import jax, jax.numpy as jnp
        import numpy as np
        from jax import lax
        B, N, D, H, E, K = (16, 128, 128, 512, 8, 2)
        key = jax.random.key(seed)
        ks = jax.random.split(key, 12)
        s = 0.02
        return {'x': jax.random.normal(ks[0], (B, N, D), jnp.float32), 'alpha': jnp.asarray(0.9, jnp.float32), 'w_gate': jax.random.normal(ks[1], (D, E), jnp.float32) * s, 'b_gate': jnp.zeros((E,), jnp.float32), 'W1m': jax.random.normal(ks[2], (D, H), jnp.float32) * s, 'b1m': jnp.zeros((H,), jnp.float32), 'W2m': jax.random.normal(ks[3], (H, D), jnp.float32) * s, 'b2m': jnp.zeros((D,), jnp.float32), 'W1e': jax.random.normal(ks[4], (E, D, H), jnp.float32) * s, 'b1e': jnp.zeros((E, H), jnp.float32), 'W2e': jax.random.normal(ks[5], (E, H, D), jnp.float32) * s, 'b2e': jnp.zeros((E, D), jnp.float32)}
    _L0_ffn_all = _L0_ffn_setup()
    _L0_ffn_in = {k: v for k, v in _L0_ffn_all.items() if k in ('alpha', 'w_gate', 'b_gate', 'W1m', 'b1m', 'W2m', 'b2m', 'W1e', 'b1e', 'W2e', 'b2e')}
    del _L0_ffn_all

    def _L1_attn_setup():
        import jax, jax.numpy as jnp
        import numpy as np
        import math
        NUM_HEADS = 8
        EMB = 128
        HEAD_DIM = 128
        B, T = (1, 512)

        def sinusoidal_pe(T, d, dtype=jnp.float32):
            pos = jnp.arange(T, dtype=dtype)[:, None]
            inv_freq = jnp.exp(-math.log(10000.0) * jnp.arange(0, d, 2, dtype=dtype) / d)
            ang = pos * inv_freq[None, :]
            pe = jnp.zeros((T, d), dtype=dtype)
            pe = pe.at[:, 0::2].set(jnp.sin(ang))
            pe = pe.at[:, 1::2].set(jnp.cos(ang))
            return pe
        key = jax.random.key(seed)
        ks = jax.random.split(key, 6)
        s = lambda fan_in: 1.0 / math.sqrt(fan_in)
        x = jax.random.normal(ks[0], (B, T, EMB), dtype=jnp.float32)
        Wq = jax.random.normal(ks[1], (EMB, NUM_HEADS * HEAD_DIM), dtype=jnp.float32) * s(EMB)
        bq = jax.random.normal(ks[2], (NUM_HEADS * HEAD_DIM,), dtype=jnp.float32) * s(EMB)
        Wkv = jax.random.normal(ks[3], (EMB, 2 * HEAD_DIM), dtype=jnp.float32) * s(EMB)
        bkv = jax.random.normal(ks[4], (2 * HEAD_DIM,), dtype=jnp.float32) * s(EMB)
        Wo = jax.random.normal(ks[5], (NUM_HEADS * HEAD_DIM, EMB), dtype=jnp.float32) * s(NUM_HEADS * HEAD_DIM)
        return {'x': x, 'Wq': Wq, 'bq': bq, 'Wkv': Wkv, 'bkv': bkv, 'Wo': Wo}
    _L1_attn_all = _L1_attn_setup()
    _L1_attn_in = {k: v for k, v in _L1_attn_all.items() if k in ('Wq', 'bq', 'Wkv', 'bkv', 'Wo')}
    del _L1_attn_all

    def _L1_xattn_setup():
        import jax, jax.numpy as jnp
        import numpy as np
        B, L, H = (8, 256, 128)
        SCALE = float(np.sqrt(H))
        EPS = 1e-05
        key = jax.random.key(seed)
        ks = jax.random.split(key, 12)
        s = 1.0 / np.sqrt(H)
        return {'queries': jax.random.normal(ks[0], (B, L, H), jnp.float32), 'keys': jax.random.normal(ks[1], (B, L, H), jnp.float32), 'values': jax.random.normal(ks[2], (B, L, H), jnp.float32), 'mask': jax.random.randint(ks[3], (B, L, L), 0, 2, jnp.int32), 'Wq': jax.random.normal(ks[4], (H, H), jnp.float32) * s, 'bq': jnp.zeros((H,), jnp.float32), 'Wk': jax.random.normal(ks[5], (H, H), jnp.float32) * s, 'bk': jnp.zeros((H,), jnp.float32), 'Wv': jax.random.normal(ks[6], (H, H), jnp.float32) * s, 'bv': jnp.zeros((H,), jnp.float32), 'ln_gamma': jnp.ones((H,), jnp.float32), 'ln_beta': jnp.zeros((H,), jnp.float32)}
    _L1_xattn_all = _L1_xattn_setup()
    _L1_xattn_in = {k: v for k, v in _L1_xattn_all.items() if k in ('Wq', 'bq', 'Wk', 'bk', 'Wv', 'bv', 'ln_gamma', 'ln_beta')}
    del _L1_xattn_all

    def _L1_ffn_setup():
        import jax, jax.numpy as jnp
        import numpy as np
        NUM_EXPERTS = 8
        NUM_LANGS = 4
        TOP_K = 2
        D_MODEL = 128
        EXPERT_SIZE = 512
        B, S = (2, 256)
        key = jax.random.key(seed)
        ks = jax.random.split(key, 6)

        def xavier(k, shape, fan_in, fan_out):
            a = float(np.sqrt(6.0 / (fan_in + fan_out)))
            return jax.random.uniform(k, shape, jnp.float32, -a, a)
        return {'x': jax.random.normal(ks[0], (B, S, D_MODEL), jnp.float32), 'router_w': xavier(ks[1], (NUM_EXPERTS, D_MODEL), D_MODEL, NUM_EXPERTS), 'router_b': jnp.zeros((NUM_EXPERTS,), jnp.float32), 'lang_w': xavier(ks[2], (NUM_LANGS, D_MODEL), D_MODEL, NUM_LANGS), 'lang_b': jnp.zeros((NUM_LANGS,), jnp.float32), 'w1': xavier(ks[3], (NUM_EXPERTS, D_MODEL, EXPERT_SIZE), D_MODEL, EXPERT_SIZE), 'b1': jnp.zeros((NUM_EXPERTS, EXPERT_SIZE), jnp.float32), 'w2': xavier(ks[4], (NUM_EXPERTS, EXPERT_SIZE, D_MODEL), EXPERT_SIZE, D_MODEL), 'b2': jnp.zeros((NUM_EXPERTS, D_MODEL), jnp.float32)}
    _L1_ffn_all = _L1_ffn_setup()
    _L1_ffn_in = {k: v for k, v in _L1_ffn_all.items() if k in ('router_w', 'router_b', 'lang_w', 'lang_b', 'w1', 'b1', 'w2', 'b2')}
    del _L1_ffn_all
    return {'x': x, 'ctx_1024': ctx_1024, 'mask_BxSxS2_ik1': mask_BxSxS2_ik1, 'L0_attn_w_qkv': _L0_attn_in['w_qkv'], 'L0_attn_w_out': _L0_attn_in['w_out'], 'L0_attn_b_out': _L0_attn_in['b_out'], 'L0_attn_norm_g': _L0_attn_in['norm_g'], 'L0_attn_norm_b': _L0_attn_in['norm_b'], 'L0_xattn_gamma_media': _L0_xattn_in['gamma_media'], 'L0_xattn_beta_media': _L0_xattn_in['beta_media'], 'L0_xattn_gamma_lat': _L0_xattn_in['gamma_lat'], 'L0_xattn_beta_lat': _L0_xattn_in['beta_lat'], 'L0_xattn_Wq': _L0_xattn_in['Wq'], 'L0_xattn_bq': _L0_xattn_in['bq'], 'L0_xattn_Wkv': _L0_xattn_in['Wkv'], 'L0_xattn_bkv': _L0_xattn_in['bkv'], 'L0_xattn_Wo': _L0_xattn_in['Wo'], 'L0_xattn_bo': _L0_xattn_in['bo'], 'L0_ffn_alpha': _L0_ffn_in['alpha'], 'L0_ffn_w_gate': _L0_ffn_in['w_gate'], 'L0_ffn_b_gate': _L0_ffn_in['b_gate'], 'L0_ffn_W1m': _L0_ffn_in['W1m'], 'L0_ffn_b1m': _L0_ffn_in['b1m'], 'L0_ffn_W2m': _L0_ffn_in['W2m'], 'L0_ffn_b2m': _L0_ffn_in['b2m'], 'L0_ffn_W1e': _L0_ffn_in['W1e'], 'L0_ffn_b1e': _L0_ffn_in['b1e'], 'L0_ffn_W2e': _L0_ffn_in['W2e'], 'L0_ffn_b2e': _L0_ffn_in['b2e'], 'L1_attn_Wq': _L1_attn_in['Wq'], 'L1_attn_bq': _L1_attn_in['bq'], 'L1_attn_Wkv': _L1_attn_in['Wkv'], 'L1_attn_bkv': _L1_attn_in['bkv'], 'L1_attn_Wo': _L1_attn_in['Wo'], 'L1_xattn_Wq': _L1_xattn_in['Wq'], 'L1_xattn_bq': _L1_xattn_in['bq'], 'L1_xattn_Wk': _L1_xattn_in['Wk'], 'L1_xattn_bk': _L1_xattn_in['bk'], 'L1_xattn_Wv': _L1_xattn_in['Wv'], 'L1_xattn_bv': _L1_xattn_in['bv'], 'L1_xattn_ln_gamma': _L1_xattn_in['ln_gamma'], 'L1_xattn_ln_beta': _L1_xattn_in['ln_beta'], 'L1_ffn_router_w': _L1_ffn_in['router_w'], 'L1_ffn_router_b': _L1_ffn_in['router_b'], 'L1_ffn_lang_w': _L1_ffn_in['lang_w'], 'L1_ffn_lang_b': _L1_ffn_in['lang_b'], 'L1_ffn_w1': _L1_ffn_in['w1'], 'L1_ffn_b1': _L1_ffn_in['b1'], 'L1_ffn_w2': _L1_ffn_in['w2'], 'L1_ffn_b2': _L1_ffn_in['b2']}

def reference(x, ctx_1024, mask_BxSxS2_ik1, L0_attn_w_qkv, L0_attn_w_out, L0_attn_b_out, L0_attn_norm_g, L0_attn_norm_b, L0_xattn_gamma_media, L0_xattn_beta_media, L0_xattn_gamma_lat, L0_xattn_beta_lat, L0_xattn_Wq, L0_xattn_bq, L0_xattn_Wkv, L0_xattn_bkv, L0_xattn_Wo, L0_xattn_bo, L0_ffn_alpha, L0_ffn_w_gate, L0_ffn_b_gate, L0_ffn_W1m, L0_ffn_b1m, L0_ffn_W2m, L0_ffn_b2m, L0_ffn_W1e, L0_ffn_b1e, L0_ffn_W2e, L0_ffn_b2e, L1_attn_Wq, L1_attn_bq, L1_attn_Wkv, L1_attn_bkv, L1_attn_Wo, L1_xattn_Wq, L1_xattn_bq, L1_xattn_Wk, L1_xattn_bk, L1_xattn_Wv, L1_xattn_bv, L1_xattn_ln_gamma, L1_xattn_ln_beta, L1_ffn_router_w, L1_ffn_router_b, L1_ffn_lang_w, L1_ffn_lang_b, L1_ffn_w1, L1_ffn_b1, L1_ffn_w2, L1_ffn_b2):
    import jax
    import jax.numpy as jnp

    def _L0_attn_ref(x, w_qkv, w_out, b_out, norm_g, norm_b):
        import jax, jax.numpy as jnp
        import numpy as np
        DIM = 128
        HEADS = 16
        EPS = 1e-12
        b, n, dim = x.shape
        h = HEADS
        d = dim // h
        qkv = jnp.einsum('bnm,om->bno', x, w_qkv)
        qkv = qkv.reshape(b, n, 3, h, d)
        q, k, v = [jnp.transpose(qkv[:, :, i], (0, 2, 1, 3)) for i in range(3)]
        dots = jnp.einsum('bhid,bhjd->bhij', q, k)
        norm = jnp.sqrt(jnp.sum(dots * dots, axis=-1, keepdims=True))
        attn = dots / jnp.maximum(norm, EPS) * norm_g + norm_b
        out = jnp.einsum('bhij,bhjd->bhid', attn, v)
        out = jnp.transpose(out, (0, 2, 1, 3)).reshape(b, n, dim)
        return jnp.einsum('bnm,om->bno', out, w_out) + b_out

    def _L0_xattn_ref(x, latents, gamma_media, beta_media, gamma_lat, beta_lat, Wq, bq, Wkv, bkv, Wo, bo):
        import jax, jax.numpy as jnp
        import numpy as np
        B, M, N, DIM, DH, H = (8, 512, 64, 128, 128, 8)
        INNER = DH * H
        EPS = 1e-05

        def _layernorm(x, g, b):
            mu = jnp.mean(x, axis=-1, keepdims=True)
            var = jnp.var(x, axis=-1, keepdims=True)
            return (x - mu) * jax.lax.rsqrt(var + EPS) * g + b
        b = x.shape[0]
        xn = _layernorm(x, gamma_media, beta_media)
        ln = _layernorm(latents, gamma_lat, beta_lat)
        q = ln @ Wq + bq
        kv_input = jnp.concatenate([xn, ln], axis=1)
        kv = kv_input @ Wkv + bkv
        k, v = jnp.split(kv, 2, axis=-1)

        def to_heads(t):
            return t.reshape(b, t.shape[1], H, DH).transpose(0, 2, 1, 3)
        q, k, v = (to_heads(q), to_heads(k), to_heads(v))
        q = q * DH ** (-0.5)
        sim = jnp.einsum('bhid,bhjd->bhij', q, k)
        attn = jax.nn.softmax(sim, axis=-1)
        out = jnp.einsum('bhij,bhjd->bhid', attn, v)
        out = out.transpose(0, 2, 1, 3).reshape(b, -1, INNER)
        return out @ Wo + bo

    def _L0_ffn_ref(x, alpha, w_gate, b_gate, W1m, b1m, W2m, b2m, W1e, b1e, W2e, b2e):
        import jax, jax.numpy as jnp
        import numpy as np
        from jax import lax
        B, N, D, H, E, K = (16, 128, 128, 512, 8, 2)
        main = jax.nn.gelu(x @ W1m + b1m) @ W2m + b2m
        logits = jnp.mean(x, axis=1) @ w_gate + b_gate
        probs = jax.nn.softmax(logits, axis=-1)
        top_vals, top_idx = lax.top_k(probs, K)
        gate_w = top_vals / jnp.sum(top_vals, axis=-1, keepdims=True)
        W1g = W1e[top_idx]
        b1g = b1e[top_idx]
        W2g = W2e[top_idx]
        b2g = b2e[top_idx]
        h = jax.nn.gelu(jnp.einsum('bnd,bkdh->bknh', x, W1g) + b1g[:, :, None, :])
        eo = jnp.einsum('bknh,bkhd->bknd', h, W2g) + b2g[:, :, None, :]
        expert_out = jnp.einsum('bk,bknd->bnd', gate_w, eo)
        a = jnp.clip(alpha, 0.1, 1.0)
        return a * main + (1.0 - a) * expert_out

    def _L1_attn_ref(x, Wq, bq, Wkv, bkv, Wo):
        import jax, jax.numpy as jnp
        import numpy as np
        import math
        NUM_HEADS = 8
        EMB = 128
        HEAD_DIM = 128
        B, T = (1, 512)

        def sinusoidal_pe(T, d, dtype=jnp.float32):
            pos = jnp.arange(T, dtype=dtype)[:, None]
            inv_freq = jnp.exp(-math.log(10000.0) * jnp.arange(0, d, 2, dtype=dtype) / d)
            ang = pos * inv_freq[None, :]
            pe = jnp.zeros((T, d), dtype=dtype)
            pe = pe.at[:, 0::2].set(jnp.sin(ang))
            pe = pe.at[:, 1::2].set(jnp.cos(ang))
            return pe
        Bsz, Tlen, E = x.shape
        q = (x @ Wq + bq).reshape(Bsz, Tlen, NUM_HEADS, HEAD_DIM)
        kv = x @ Wkv + bkv
        k, v = (kv[..., :HEAD_DIM], kv[..., HEAD_DIM:])
        q = jnp.transpose(q, (0, 2, 1, 3))
        pe = sinusoidal_pe(Tlen, HEAD_DIM, x.dtype)
        q = q + pe[None, None, :, :]
        k = k + pe[None, :, :]
        scale = 1.0 / math.sqrt(HEAD_DIM)
        scores = jnp.einsum('bhqd,bkd->bhqk', q, k) * scale
        causal = jnp.tril(jnp.ones((Tlen, Tlen), dtype=bool))
        scores = jnp.where(causal[None, None, :, :], scores, jnp.finfo(scores.dtype).min)
        probs = jax.nn.softmax(scores, axis=-1)
        attn = jnp.einsum('bhqk,bkd->bhqd', probs, v)
        out = jnp.transpose(attn, (0, 2, 1, 3)).reshape(Bsz, Tlen, NUM_HEADS * HEAD_DIM)
        return out @ Wo

    def _L1_xattn_ref(queries, keys, values, mask, Wq, bq, Wk, bk, Wv, bv, ln_gamma, ln_beta):
        import jax, jax.numpy as jnp
        import numpy as np
        B, L, H = (8, 256, 128)
        SCALE = float(np.sqrt(H))
        EPS = 1e-05
        Q = queries @ Wq + bq
        K = keys @ Wk + bk
        V = values @ Wv + bv
        scores = jnp.einsum('bik,bjk->bij', Q, K) / SCALE
        scores = jnp.where(mask == 0, -jnp.inf, scores)
        probs = jax.nn.softmax(scores, axis=-1)
        context = jnp.einsum('bij,bjk->bik', probs, V)
        mu = jnp.mean(context, axis=-1, keepdims=True)
        var = jnp.var(context, axis=-1, keepdims=True)
        normed = (context - mu) * jax.lax.rsqrt(var + EPS)
        return normed * ln_gamma + ln_beta

    def _L1_ffn_ref(x, router_w, router_b, lang_w, lang_b, w1, b1, w2, b2):
        import jax, jax.numpy as jnp
        import numpy as np
        NUM_EXPERTS = 8
        NUM_LANGS = 4
        TOP_K = 2
        D_MODEL = 128
        EXPERT_SIZE = 512
        B, S = (2, 256)
        lang_logits = x @ lang_w.T + lang_b
        lang_probs = jax.nn.softmax(lang_logits, axis=-1)
        lp_pad = jnp.pad(lang_probs, ((0, 0), (0, 0), (0, 1)))
        idx = jnp.arange(NUM_EXPERTS) % NUM_LANGS
        expert_weights = lp_pad[..., idx] + lp_pad[..., idx + 1]
        router_logits = x @ router_w.T + router_b + 0.1 * expert_weights
        router_probs = jax.nn.softmax(router_logits, axis=-1)
        top_p, top_i = jax.lax.top_k(router_probs, TOP_K)
        top_p = top_p / top_p.sum(axis=-1, keepdims=True)
        h = jax.nn.gelu(jnp.einsum('bsd,edh->bseh', x, w1) + b1, approximate=False)
        expert_out = jnp.einsum('bseh,ehd->bsed', h, w2) + b2
        sel = jnp.take_along_axis(expert_out, top_i[..., None], axis=2)
        return (top_p[..., None] * sel).sum(axis=2)
    x = x + _L0_attn_ref(_layernorm(x, axis=-1), L0_attn_w_qkv, L0_attn_w_out, L0_attn_b_out, L0_attn_norm_g, L0_attn_norm_b)
    x = x + _L0_xattn_ref(ctx_1024, _layernorm(x, axis=-1), L0_xattn_gamma_media, L0_xattn_beta_media, L0_xattn_gamma_lat, L0_xattn_beta_lat, L0_xattn_Wq, L0_xattn_bq, L0_xattn_Wkv, L0_xattn_bkv, L0_xattn_Wo, L0_xattn_bo)
    x = x + _L0_ffn_ref(_layernorm(x, axis=-1), L0_ffn_alpha, L0_ffn_w_gate, L0_ffn_b_gate, L0_ffn_W1m, L0_ffn_b1m, L0_ffn_W2m, L0_ffn_b2m, L0_ffn_W1e, L0_ffn_b1e, L0_ffn_W2e, L0_ffn_b2e)
    x = x + _L1_attn_ref(_layernorm(x, axis=-1), L1_attn_Wq, L1_attn_bq, L1_attn_Wkv, L1_attn_bkv, L1_attn_Wo)
    x = x + _L1_xattn_ref(_layernorm(x, axis=-1), ctx_1024, ctx_1024, mask_BxSxS2_ik1, L1_xattn_Wq, L1_xattn_bq, L1_xattn_Wk, L1_xattn_bk, L1_xattn_Wv, L1_xattn_bv, L1_xattn_ln_gamma, L1_xattn_ln_beta)
    x = x + _L1_ffn_ref(_layernorm(x, axis=-1), L1_ffn_router_w, L1_ffn_router_b, L1_ffn_lang_w, L1_ffn_lang_b, L1_ffn_w1, L1_ffn_b1, L1_ffn_w2, L1_ffn_b2)
    return x

_drawn_inputs = setup_inputs


def setup_inputs(seed=0):
    import zlib

    import numpy as np

    out = dict(_drawn_inputs(seed))
    spreads = {'L0_attn_norm_g': (1.0, 0.2),
     'L0_attn_norm_b': (0.0, 0.1),
     'L0_xattn_gamma_media': (1.0, 0.6),
     'L0_xattn_beta_media': (0.0, 0.8),
     'L0_xattn_gamma_lat': (1.0, 0.6),
     'L0_xattn_beta_lat': (0.0, 0.8),
     'L0_xattn_bq': (0.0, 0.8),
     'L0_xattn_bkv': (0.0, 0.357),
     'L0_xattn_bo': (0.0, 0.1),
     'L0_ffn_b_gate': (0.0, 0.8),
     'L0_ffn_b1m': (0.0, 0.8),
     'L0_ffn_b2m': (0.0, 0.269),
     'L0_ffn_b1e': (0.0, 0.8),
     'L0_ffn_b2e': (0.0, 2.0),
     'L1_xattn_bq': (0.0, 0.633),
     'L1_xattn_bk': (0.0, 2.0),
     'L1_xattn_bv': (0.0, 0.1),
     'L1_xattn_ln_gamma': (1.0, 0.2),
     'L1_xattn_ln_beta': (0.0, 0.282),
     'L1_ffn_router_b': (0.0, 0.42),
     'L1_ffn_lang_b': (0.0, 2.0),
     'L1_ffn_b1': (0.0, 0.524),
     'L1_ffn_b2': (0.0, 0.405)}
    factors = {'L0_attn_b_out': 8.0,
     'L0_xattn_Wq': 8.0,
     'L0_xattn_Wkv': 2.817,
     'L0_ffn_w_gate': 8.0,
     'L0_ffn_W1m': 3.905,
     'L0_ffn_W2m': 3.76,
     'L0_ffn_W1e': 8.0,
     'L0_ffn_W2e': 8.0,
     'L1_attn_bq': 8.0,
     'L1_ffn_lang_w': 28.918}
    for name, (base, spread) in spreads.items():
        noise = np.random.default_rng([zlib.crc32(name.encode()), seed]).standard_normal(out[name].shape)
        drawn = base * np.exp(spread * noise) if base else spread * noise
        out[name] = jnp.asarray(drawn.astype(out[name].dtype))
    for name, factor in factors.items():
        out[name] = (out[name] * factor).astype(out[name].dtype)
    return out
```

```python
from contextlib import ExitStack

import numpy as np

import concourse.bass as bass
from concourse import mybir

P = 128
B = 2
S = 512
NT = S // P
C = 77
H = 8
HA = 16
HID = 512
NM = HID // P
NE = 8
NL = 4
LN_EPS = 1e-5
NORM_EPS = 1e-12
SCALE = P ** -0.5
BIG = 3e38
NEG = -1e30

F32 = mybir.dt.float32
BF16 = mybir.dt.bfloat16
I32 = mybir.dt.int32
U32 = mybir.dt.uint32
ALU = mybir.AluOpType
ACT = mybir.ActivationFunctionType
AX = mybir.AxisListType.X


def offsets(parts):
    at, out = 0, {}
    for name, n in parts:
        out[name] = at
        at += n
    return out, at


COLS, N_COLS = offsets([
    ("norm_b", 1), ("gamma_media", 1), ("beta_media", 1), ("gamma_lat", 1), ("beta_lat", 1),
    ("X_bq", H), ("X_bv", H), ("F_b1m", NM), ("D_bq", H), ("D_bk", 1), ("D_bv", 1),
    ("E_bq", 1), ("E_bk", 1)])
ROWS, N_ROWS = offsets([
    ("norm_g", P), ("A_b_out", P), ("X_bo", P), ("F_b_gate", NE), ("F_b2m", P), ("alpha", 1),
    ("E_bv", P), ("ln_gamma", P), ("ln_beta", P), ("M_bias", NE + NL)])
CONSTS, N_CONSTS = offsets([
    ("ident", P), ("blocks", 2 * P), ("head_sum", HA), ("causal", P), ("iota", NE), ("ones", 1), ("peT", S)])

STAGES = "AXFDEM"
W_A_BIAS, W_A, W_X_BIAS = 1, 2, 3
W_F_BIAS, W_F = W_X_BIAS + 1, W_X_BIAS + 2
W_E = W_F + 1
W_M_BIAS = W_E + 1
W_M = W_M_BIAS + NE
READ_BY_LN = {"X": W_A, "D": W_F, "M": W_E}


def build(nc, t):
    ctx = ExitStack()
    with ctx:
        def sb(name, shape, dt=F32):
            return ctx.enter_context(nc.sbuf_tensor(name, shape, dt))

        def sem(name):
            return ctx.enter_context(nc.semaphore(name))

        cols, rows, consts = sb("cols", [P, N_COLS]), sb("rows", [P, N_ROWS]), sb("consts", [P, N_CONSTS])
        x = [sb(f"x{b}", [P, NT, P]) for b in range(B)]
        ctx_tok = sb("ctx_tok", [C, B, P])
        ctxT = sb("ctxT", [P, B, C])
        mask = sb("mask", [P, B, NT, C], I32)
        A_wqkvT, A_woutT = sb("A_wqkvT", [P, 3 * P]), sb("A_woutT", [P, P])
        X_WqT, X_WkT, X_WvT = (sb(f"X_W{n}T", [P, H, P]) for n in "qkv")
        X_Wo = sb("X_Wo", [P, H, P])
        F_w_gate, F_W1m, F_W2m = sb("F_w_gate", [P, NE]), sb("F_W1m", [P, HID]), sb("F_W2m", [P, NM, P])
        packed = [[X_WqT, X_WkT], [X_WvT, X_Wo]]
        F_W1e = [[w[:, 0:NM, :].rearrange("p h k -> p (h k)") for w in pair] for pair in packed]
        F_W2e = [[w[:, NM:2 * NM, :] for w in pair] for pair in packed]
        F_b1e = [[sb(f"F_b1e{b}{k}", [P, NM]) for k in range(2)] for b in range(B)]
        F_b2e = [[sb(f"F_b2e{b}{k}", [P, P]) for k in range(2)] for b in range(B)]
        D_Wq, D_Wkv, D_Wo = sb("D_Wq", [P, H, P]), sb("D_Wkv", [P, 2 * P]), sb("D_Wo", [P, H, P])
        E_Wq, E_Wk, E_Wv = (sb(f"E_W{n}", [P, P]) for n in "qkv")
        M_w, M_b2 = sb("M_w", [P, NE + NL]), sb("M_b2", [NE, P])
        M_b1 = [sb(f"M_b1{s}", [P, NM]) for s in range(2)]
        M_w1 = [sb(f"M_w1{s}", [P, HID]) for s in range(2)]
        M_w2 = [sb(f"M_w2{s}", [P, NM, P]) for s in range(2)]

        def col(name, n=1, at=0):
            return cols[:, COLS[name] + at:COLS[name] + at + n]

        def row(name, n=P):
            return rows[:, ROWS[name]:ROWS[name] + n]

        def const(name, n):
            return consts[:, CONSTS[name]:CONSTS[name] + n]

        ident = const("ident", P)

        bn = sb("bn", [P, B, NT, 6])
        mv = sb("mv", [P, B, NT, 2])
        var_eps, rstd = sb("var_eps", [P, B, NT]), sb("rstd", [P, B, NT])
        rstd1 = sb("rstd1", [P, B, NT])
        minus_half = sb("minus_half", [P, NT])
        xhat = [sb(f"xhat{b}", [P, NT, P]) for b in range(B)]
        xT = [sb(f"xT{b}", [P, S]) for b in range(B)]
        a_mask = sb("a_mask", [P, 2 * P])
        qT, kv = ([sb(f"{n}{b}", [P, w]) for b in range(B)] for n, w in (("qT", S), ("kv", NT * 2 * P)))
        gm, t1 = ([sb(f"{n}{b}", [P, w]) for b in range(B)] for n, w in (("gm", 2 * P), ("t1", S)))
        vsum = sb("vsum", [P, B])
        norm2, norm, rnorm = (sb(n, [P, B, NT * HA]) for n in ("norm2", "norm", "rnorm"))
        c_bn, c_mv, c_var = sb("c_bn", [C, B, 6]), sb("c_mv", [C, B, 2]), sb("c_var", [C, B])
        c_rstd, c_hat = sb("c_rstd", [C, B]), sb("c_hat", [C, B, P])
        czT, czkT = sb("czT", [P, B, C]), sb("czkT", [P, B, C])
        X_A, X_V = sb("X_A", [P, H, P]), sb("X_V", [P, H, P])
        X_r0 = sb("X_r0", [P, H])
        X_bias = sb("X_bias", [P, P])
        X_vc = sb("X_vc", [C, B, H * P])
        keysT = [sb(f"keysT{b}", [P, S]) for b in range(B)]
        valuesT = [sb(f"valuesT{b}", [P, S]) for b in range(B)]
        w_head = [sb(f"w_head{p}", [P, P]) for p in range(2)]
        rT = [sb(f"rT{p}", [P, S]) for p in range(2)]
        vw = [sb(f"vw{p}", [P, NT, P]) for p in range(2)]
        probs = [sb(f"probs{p}", [P, NT, S + C]) for p in range(2)]
        pT = sb("pT", [P, NT + 1, S])
        neg_cmax, neg_max = sb("neg_cmax", [P, 2, NT]), sb("neg_max", [P, 2, NT])
        sum_x, sum_c = sb("sum_x", [P, 2, NT]), sb("sum_c", [P, 2, NT])
        denom, rdenom = sb("denom", [P, 2, NT]), sb("rdenom", [P, 2, NT])
        spill = sb("spill", [P, NT, S], BF16)
        ident_bf, causal_bf = sb("ident_bf", [P, P], BF16), sb("causal_bf", [P, P], BF16)
        xsum, mean_bc = sb("xsum", [P, B]), sb("mean_bc", [P, B, P])
        f_lg, f_max, f_idx = sb("f_lg", [P, B, NE]), sb("f_max", [P, B, 8]), sb("f_idx", [P, B, 8], U32)
        f_nmax, f_e, f_es = sb("f_nmax", [P, B]), sb("f_e", [P, B, 2]), sb("f_es", [P, B])
        f_ers, f_g = sb("f_ers", [P, B]), sb("f_g", [P, B, 2])
        f_a, f_1a = sb("f_a", [P, 1]), sb("f_1a", [P, 1])
        f_bias = sb("f_bias", [P, B, P])
        f_bias0, f_bias1 = sb("f_bias0", [P, P]), sb("f_bias1", [P, B, P])
        hT = [sb(f"hT{s}", [P, S]) for s in range(4)]
        e_lim, e_tmp = sb("e_lim", [P, B * NT * C]), sb("e_tmp", [P, B * NT * C])
        e_kT, e_v = sb("e_kT", [P, B, C]), sb("e_v", [C, B, P])
        e_s = [sb(f"e_s{b}", [P, NT, C]) for b in range(B)]
        e_p = [sb(f"e_p{b}", [P, NT, C]) for b in range(B)]
        e_pT = [sb(f"e_pT{b}", [C, S]) for b in range(B)]
        e_nmax, e_sum, e_rsum = (sb(n, [P, B, NT]) for n in ("e_nmax", "e_sum", "e_rsum"))
        tiles = "p (n d) -> p n d"
        e_qT = t1
        e_o = [kv[b][:, 0:S].rearrange(tiles, d=P) for b in range(B)]
        e_on = [kv[b][:, S:2 * S].rearrange(tiles, d=P) for b in range(B)]
        e_og = [qT[b][:].rearrange(tiles, d=P) for b in range(B)]
        m_lg = [sb(f"m_lg{b}", [P, NT, NE + NL]) for b in range(B)]
        m_lmax = sb("m_lmax", [P, B, NT])
        m_ld, m_le = sb("m_ld", [P, B, NT, NL]), sb("m_le", [P, B, NT, NL])
        m_ls, m_lr = sb("m_ls", [P, B, NT]), sb("m_lr", [P, B, NT])
        m_lp, m_ew = sb("m_lp", [P, B, NT, NL + 1]), sb("m_ew", [P, B, NT, NL])
        m_rl = [sb(f"m_rl{b}", [P, NT, NE]) for b in range(B)]
        m_max, m_idx = sb("m_max", [P, B, NT, 8]), sb("m_idx", [P, B, NT, 8], U32)
        m_idxf = sb("m_idxf", [P, B, NT, 2])
        m_d, m_e = sb("m_d", [P, B, NT]), sb("m_e", [P, B, NT])
        m_s, m_g0, m_g1 = (sb(n, [P, B, NT]) for n in ("m_s", "m_g0", "m_g1"))
        m_oh = sb("m_oh", [P, B, 2, NT, NE])
        m_og = sb("m_og", [P, B, 2, NT, NE])
        gates = [sb(f"gates{b}", [P, NT, NE]) for b in range(B)]
        gT = [e_pT[b][0:NE, :] for b in range(B)]

        bank = [ctx.enter_context(nc.psum_tensor(f"bank{i}", [P, S], F32)) for i in range(8)]
        S_BANK, C_BANK, T_BANK, R_BANK, V_BANK, O_BANK = (0, 1), 2, (3, 4), 5, 6, 7
        TR_BANK = {s: (6, 7) for s in "XFDEM"} | {"A": (0, 4)}

        ld = {n: sem(f"ld_{n}") for n in (
            "consts", "cols", "rows", "x0", "x1", "ctx", "ctxT", "mask", "A_wqkvT", "A_woutT", "X_WqT", "X_WkT",
            "X_WvT", "X_Wo", "F_w_gate", "F_W1m", "F_W2m", "D_Wq", "D_Wkv", "D_Wo", "E_W", "M_w", "M_b2")}
        x_written = [sem(f"x_written{b}") for b in range(B)]
        (ln_bn, ln_stats, ln_eps, ln_r1, ln_rstd, ln_hat, ln_mm, ln_xT) = (
            sem(n) for n in ("ln_bn", "ln_stats", "ln_eps", "ln_r1", "ln_rstd", "ln_hat", "ln_mm", "ln_xT"))
        half_ready, a_mask_half, a_mask_ready = sem("half_ready"), sem("a_mask_half"), sem("a_mask_ready")
        (a_q_mm, a_kv_mm, a_q, a_kv, a_g_mm, a_g, a_gq_mm, a_t1, a_n2_mm, a_n2, a_norm, a_rnorm, a_o_mm, a_o,
         a_oT_mm, a_oT, a_y_mm) = (sem("a_" + n) for n in (
             "q_mm", "kv_mm", "q", "kv", "g_mm", "g", "gq_mm", "t1", "n2_mm", "n2", "norm", "rnorm", "o_mm", "o",
             "oT_mm", "oT", "y_mm"))
        (c_bn_s, c_stats, c_eps, c_rstd_s, c_hat_s, c_mm, c_zT, c_zkT) = (sem("c_" + n) for n in (
            "bn", "stats", "eps", "rstd", "hat", "mm", "zT", "zkT"))
        (w_a_mm, w_a, w_v_mm, w_v, w_b_mm, w_bias, w_vc_mm, w_vc) = (sem("w_" + n) for n in (
            "a_mm", "a", "v_mm", "v", "b_mm", "bias", "vc_mm", "vc"))
        bf_ready = sem("bf_ready")
        keys_ready, d_kv_mm, d_v_ready, d_k1 = (
            sem("keys_ready"), sem("d_kv_mm"), sem("d_v_ready"), sem("d_k1"))
        (w_head_ready, r_mm, r_ready, c_s_mm, s_mm, cmax_ready, max_ready, probs_ready, t_mm, pT_even, pT_odd,
         v_mm, v_ready, o_mm, o_added, denom_ready, rdenom_ready) = (sem(n) for n in (
             "w_head_ready", "r_mm", "r_ready", "c_s_mm", "s_mm", "cmax_ready", "max_ready", "probs_ready", "t_mm",
             "pT_even", "pT_odd", "v_mm", "v_ready", "o_mm", "o_added", "denom_ready", "rdenom_ready"))
        (f_mean, f_lg_mm, f_lg_s, f_max_s, f_idx_s, f_nmax_s, f_exp, f_rs, f_gk, f_a1, f_a_s, f_bias0_s, f_w2m,
         f_w2e, f_b1, f_bias_s, f_h_mm, f_h, f_y_mm) = (sem("f_" + n) for n in (
             "mean", "lg_mm", "lg", "max", "idx", "nmax", "exp", "rs", "gk", "a1", "a", "bias0", "w2m", "w2e", "b1",
             "bias", "h_mm", "h", "y_mm"))
        f_ld = [[sem(f"f_ld{b}{k}") for k in range(2)] for b in range(B)]
        (e_l1, e_lim_s, e_kv_mm, e_k_s, e_v_s, e_q_mm, e_q, e_s_mm, e_ss, e_max, e_exp, e_rs, e_t_mm, e_pT_s,
         e_o_mm, e_o_s, e_bn_s, e_st, e_eps, e_r, e_on_s, e_g_s, e_gb_s) = (sem("e_" + n) for n in (
             "l1", "lim", "kv_mm", "k", "v", "q_mm", "q", "s_mm", "s", "max", "exp", "rs", "t_mm", "pT",
             "o_mm", "o", "bn", "st", "eps", "r", "on", "g", "gb"))
        (m_zero, m_lg_mm, m_chain, m_lexp, m_exp, m_gates, m_gT_mm, m_gT, m_b_mm, m_w_slot0, m_w_slot1, m_h_mm, m_h,
         m_y_mm) = (sem("m_" + n) for n in (
             "zero", "lg_mm", "chain", "lexp", "exp", "gates", "gT_mm", "gT", "b_mm", "w_slot0", "w_slot1", "h_mm",
             "h", "y_mm"))
        m_w_slot = (m_w_slot0, m_w_slot1)
        stored = sem("stored")

        def ln_index(stage, b):
            return B * STAGES.index(stage) + b

        class Head:

            def __init__(self, kind, b, h, par):
                self.kind, self.b, self.h, self.par = kind, b, h, par
                self.g = (0 if kind == "X" else B * H) + b * H + h
                self.chunks = NT + 1 if kind == "X" else NT
                even, odd = (self.chunks + 1) // 2, self.chunks // 2
                self.very_first = kind == "X" and b == 0 and isinstance(h, int) and h == 0
                x_even, x_all = (NT + 2) // 2, NT + 1
                self.c0 = (0 if kind == "X" else B * H * x_all) + (b * H + h) * self.chunks
                self.even0 = (0 if kind == "X" else B * H * x_even) + (b * H + h) * even
                self.odd0 = (self.g) * odd

            def keys(self, i):
                return S if self.kind == "X" else (i + 1) * P

            def chunk_ready(self, eng, c):
                if c % 2 == 0:
                    eng.wait_ge(pT_even, self.even0 + c // 2 + 1)
                else:
                    eng.wait_ge(pT_odd, self.odd0 + c // 2 + 1)

        def run_attention(eng, kind, prologue, step, between):
            prologue(Head(kind, 0, 0, 0), Head(kind, 0, 1, 1))
            for b in range(B):
                with eng.Fori(0, H // 2 - 1) as i:
                    step(Head(kind, b, i * 2 + 1, 1), Head(kind, b, i * 2, 0), Head(kind, b, i * 2 + 2, 0))
                    step(Head(kind, b, i * 2 + 2, 0), Head(kind, b, i * 2 + 1, 1), Head(kind, b, i * 2 + 3, 1))
                nxt = [Head(kind, 1, 0, 0), Head(kind, 1, 1, 1)] if b == 0 else [None, None]
                step(Head(kind, b, H - 1, 1), Head(kind, b, H - 2, 0), nxt[0])
                step(nxt[0], Head(kind, b, H - 1, 1), nxt[1])
                if b == 0:
                    between()

        block = ctx.enter_context(nc.Block())

        @block.sync
        def _(sp):
            def load(dst, src, s):
                sp.dma_start(dst, src).then_inc(s, 16)

            load(x[0][:], t["x"][0].rearrange("(n p) d -> p n d", p=P), ld["x0"])
            load(consts[:], t["consts"], ld["consts"])
            load(x[1][:], t["x"][1].rearrange("(n p) d -> p n d", p=P), ld["x1"])
            load(A_wqkvT[:], t["A_wqkvT"], ld["A_wqkvT"])
            load(cols[:], t["cols"], ld["cols"])
            load(rows[:], t["rows"].to_broadcast((P, N_ROWS)), ld["rows"])
            load(ctx_tok[:], t["ctx"].rearrange("b c d -> c b d"), ld["ctx"])
            load(A_woutT[:], t["A_woutT"], ld["A_woutT"])
            load(X_WqT[:], t["X_WqT"].rearrange("(h k) d -> k h d", k=P), ld["X_WqT"])
            load(X_WkT[:], t["X_WkvT"][0:H * P].rearrange("(h k) d -> k h d", k=P), ld["X_WkT"])
            load(X_WvT[:], t["X_WkvT"][H * P:].rearrange("(h k) d -> k h d", k=P), ld["X_WvT"])
            load(X_Wo[:], t["X_Wo"].rearrange("(h k) d -> k h d", k=P), ld["X_Wo"])
            load(mask[:], t["mask"].rearrange("b (n p) c -> p b n c", p=P), ld["mask"])
            load(ctxT[:], t["ctxT"], ld["ctxT"])
            for w, n in ((E_Wq, "E_Wq"), (E_Wk, "E_Wk"), (E_Wv, "E_Wv")):
                load(w[:], t[n], ld["E_W"])
            load(F_w_gate[:], t["F_w_gate"], ld["F_w_gate"])
            load(F_W1m[:], t["F_W1m"], ld["F_W1m"])
            load(F_W2m[:], t["F_W2m"].rearrange("(m p) d -> p m d", p=P), ld["F_W2m"])
            load(D_Wq[:], t["D_Wq"].rearrange("d (h k) -> d h k", k=P), ld["D_Wq"])
            load(D_Wkv[:], t["D_Wkv"], ld["D_Wkv"])
            load(D_Wo[:], t["D_Wo"].rearrange("(h k) d -> k h d", k=P), ld["D_Wo"])
            load(M_w[:], t["M_w"], ld["M_w"])
            load(M_b2[:], t["M_b2"], ld["M_b2"])

            def expert(e, s):
                load(M_w1[s][:], t["M_w1"][bass.ds(e, 1)].rearrange("e d h -> d (e h)"), m_w_slot[s])
                load(M_b1[s][:], t["M_b1T"][:, bass.ds(e * NM, NM)], m_w_slot[s])
                load(M_w2[s][:], t["M_w2"][bass.ds(e, 1)].rearrange("e (m p) d -> p (e m) d", p=P), m_w_slot[s])

            for e in range(2):
                expert(e, e)

            for b in range(B):
                sp.wait_ge(f_idx_s, b + 1)
                for k in range(2):
                    e = sp.value_load(f_idx[0:1, b, k:k + 1], min_val=0, max_val=NE - 1)
                    load(F_W1e[b][k], t["F_W1e"][bass.ds(e, 1)].rearrange("e d h -> d (e h)"), f_ld[b][k])
                    load(F_W2e[b][k], t["F_W2e"][bass.ds(e, 1)].rearrange("e (m p) d -> p (e m) d", p=P),
                         f_ld[b][k])
                    load(F_b1e[b][k][:], t["F_b1eT"][:, bass.ds(e * NM, NM)], f_ld[b][k])
                    load(F_b2e[b][k][:], t["F_b2e"][bass.ds(e, 1)].to_broadcast((P, P)), f_ld[b][k])

            with sp.Fori(1, NE // 2) as i:
                for s in range(2):
                    sp.wait_ge(m_y_mm, i * (2 * B * NM) + (s - 1) * B * NM)
                    expert(2 * i + s, s)

            for b in range(B):
                sp.wait_ge(x_written[b], W_M)
                sp.dma_start(t["out"][b].rearrange("(n p) d -> p n d", p=P), x[b][:]).then_inc(stored, 16)
            sp.wait_ge(stored, 16 * B)

        @block.gpsimd
        def _(pool):
            g = nc.gpsimd
            g.memset(minus_half[:], -0.5).then_inc(half_ready, 1)
            g.memset(m_lp[:], 0.0).then_inc(m_zero, 1)
            pool.wait_ge(half_ready, 1)

            def ln_rstd_of(stage, b):
                n = ln_index(stage, b)
                var = mv[:, b, :, 1]
                pool.wait_ge(ln_stats, n + 1)
                g.tensor_scalar(var_eps[:, b], var, LN_EPS, 1.0, ALU.add, ALU.mult).then_inc(ln_eps, 1)
                pool.wait_ge(ln_eps, n + 1)
                if stage != "X":
                    g.tensor_tensor(rstd[:, b], var_eps[:, b], minus_half[:], ALU.pow).then_inc(ln_rstd, 1)
                    return
                g.tensor_tensor(rstd1[:, b], var_eps[:, b], minus_half[:], ALU.pow).then_inc(ln_r1, 1)
                pool.wait_ge(ln_r1, 5 * b + 1)
                g.tensor_tensor(rstd[:, b], var, rstd1[:, b], ALU.mult).then_inc(ln_r1, 1)
                pool.wait_ge(ln_r1, 5 * b + 2)
                g.tensor_tensor(var_eps[:, b], rstd[:, b], rstd1[:, b], ALU.mult).then_inc(ln_r1, 1)
                pool.wait_ge(ln_r1, 5 * b + 3)
                g.tensor_scalar(var_eps[:, b], var_eps[:, b], LN_EPS, 1.0, ALU.add, ALU.mult).then_inc(ln_r1, 1)
                pool.wait_ge(ln_r1, 5 * b + 4)
                g.tensor_tensor(rstd[:, b], var_eps[:, b], minus_half[:], ALU.pow).then_inc(ln_r1, 1)
                pool.wait_ge(ln_r1, 5 * b + 5)
                g.tensor_tensor(rstd[:, b], rstd[:, b], rstd1[:, b], ALU.mult).then_inc(ln_rstd, 1)

            def add_row(b, r, stage):
                pool.wait_ge(ln_hat, ln_index(stage, b) + 1)
                g.tensor_tensor(x[b][:], x[b][:], r.unsqueeze(1).to_broadcast((P, NT, P)),
                                ALU.add).then_inc(x_written[b], 1)

            def copy_heads(kind, b, w):
                first = (0 if kind == "X" else B * H) + b * H

                def copy(h, p, wait):
                    if wait is not None:
                        pool.wait_ge(r_mm, wait)
                    g.tensor_copy(w_head[p][:], w[:, bass.ds(h, 1), :].rearrange("p a k -> p (a k)")
                                  ).then_inc(w_head_ready, 1)

                for p in range(2):
                    copy(p, p, first + p - 1 if first else None)
                yield
                with pool.Fori(1, H // 2) as i:
                    for p in range(2):
                        copy(2 * i + p, p, 2 * i + (first + p - 1))
                yield

            pool.wait_ge(ld["x0"], 16)
            ln_rstd_of("A", 0)
            ln_rstd_of("A", 1)
            pool.wait_ge(ld["rows"], 16)
            for b in range(B):
                pool.wait_ge(ld[f"x{b}"], 16)
                add_row(b, row("A_b_out"), "A")
            pool.wait_ge(c_stats, 1)
            g.tensor_scalar(c_var[:], c_mv[:, :, 1], LN_EPS, 1.0, ALU.add, ALU.mult).then_inc(c_eps, 1)
            pool.wait_ge(c_eps, 1)
            g.tensor_tensor(c_rstd[:], c_var[:], minus_half[0:C, 0:B], ALU.pow).then_inc(c_rstd_s, 1)
            pool.wait_ge(ld["consts"], 16)
            g.tensor_copy(ident_bf[:], ident).then_inc(bf_ready, 1)
            g.tensor_copy(causal_bf[:], const("causal", P)).then_inc(bf_ready, 1)
            ln_rstd_of("X", 0)
            ln_rstd_of("X", 1)
            pool.wait_ge(w_bias, 1)
            for b in range(B):
                add_row(b, X_bias[:], "X")
            pool.wait_ge(w_a, 2)
            for _ in copy_heads("X", 0, X_A):
                pass
            heads = copy_heads("X", 1, X_A)
            next(heads)
            ln_rstd_of("F", 0)
            next(heads)
            ln_rstd_of("F", 1)

            for b in range(B):
                pool.wait_ge(ln_xT, ln_index("F", b) + 1)
                g.tensor_scalar(mean_bc[:, b, :], xsum[:, b:b + 1].to_broadcast((P, P)), 1.0 / S, 1.0,
                                ALU.mult, ALU.mult).then_inc(f_mean, 1)
            for b in range(B):
                pool.wait_ge(f_bias_s, b + 1)
                add_row(b, f_bias[:, b, :], "F")
            ln_rstd_of("D", 0)
            ln_rstd_of("D", 1)
            pool.wait_ge(ld["D_Wq"], 16)
            for _ in copy_heads("D", 0, D_Wq):
                pass
            heads = copy_heads("D", 1, D_Wq)
            next(heads)
            ln_rstd_of("E", 0)
            next(heads)
            ln_rstd_of("E", 1)
            for b in range(B):
                pool.wait_ge(e_st, b + 1)
                g.tensor_scalar(var_eps[:, b], mv[:, b, :, 1], LN_EPS, 1.0, ALU.add, ALU.mult).then_inc(e_eps, 1)
                pool.wait_ge(e_eps, b + 1)
                g.tensor_tensor(rstd[:, b], var_eps[:, b], minus_half[:], ALU.pow).then_inc(e_r, 1)
            ln_rstd_of("M", 0)
            ln_rstd_of("M", 1)

        @block.scalar
        def _(act):
            a = nc.scalar

            def xT_of(stage, b):
                act.wait_ge(ln_mm, ln_index(stage, b) + 1)
                src = bank[TR_BANK[stage][b]][:]
                if stage == "X":
                    a.activation(xT[b][:], src, ACT.Identity, scale=col("gamma_lat"),
                                 bias=col("beta_lat")).then_inc(ln_xT, 1)
                elif stage == "F":
                    a.activation(xT[b][:], src, ACT.Copy, accum_out=xsum[:, b:b + 1]).then_inc(ln_xT, 1)
                else:
                    a.copy(xT[b][:], src).then_inc(ln_xT, 1)

            for b in range(B):
                xT_of("A", b)
                act.wait_ge(a_q_mm, b + 1)
                a.copy(qT[b][:], bank[4 * b + 1][:]).then_inc(a_q, 1)
            for b in range(B):
                act.wait_ge(a_n2, b + 1)
                a.activation(norm[:, b], norm2[:, b], ACT.Sqrt).then_inc(a_norm, 1)
            for b in range(B):
                act.wait_ge(a_oT_mm, b + 1)
                act.wait_ge(a_g, B)
                a.activation(t1[b][:], bank[4 * b][:], ACT.Identity, bias=vsum[:, b:b + 1]).then_inc(a_oT, 1)
            act.wait_ge(ld["cols"], 16)
            act.wait_ge(c_mm, 1)
            a.activation(czT[:].rearrange("p b c -> p (b c)"), bank[2][:, 0:B * C], ACT.Identity,
                         scale=col("gamma_media"), bias=col("beta_media")).then_inc(c_zT, 1)
            act.wait_ge(w_a_mm, 1)
            a.copy(X_A[:, 0:4, :].rearrange("p h k -> p (h k)"), bank[0][:]).then_inc(w_a, 1)
            act.wait_ge(w_v_mm, 1)
            a.copy(X_V[:, 0:4, :].rearrange("p h k -> p (h k)"), bank[2][:]).then_inc(w_v, 1)
            for b in range(B):
                xT_of("X", b)

            def e_tile(hd, i):
                g, p = hd.g, hd.par
                act.wait_ge(max_ready, g * NT + i + 1)
                n = hd.keys(i)
                last = a.activation(probs[p][:, i, 0:n], bank[S_BANK[i % 2]][:, 0:n], ACT.Exp,
                                    bias=neg_max[:, p, i:i + 1], accum_out=sum_x[:, p, i:i + 1])
                if hd.kind == "X":
                    last = a.activation(probs[p][:, i, S:S + C], bank[C_BANK][:, i * C:(i + 1) * C], ACT.Exp,
                                        bias=neg_max[:, p, i:i + 1], accum_out=sum_c[:, p, i:i + 1])
                last.then_inc(probs_ready, 1)

            def t_copy(hd, c):
                act.wait_ge(t_mm, hd.c0 + c + 1)
                k = C if c == NT else P
                lo = 0 if hd.kind == "X" else c * P
                a.copy(pT[0:k, c, lo:S], bank[T_BANK[0]][0:k, lo:S]).then_inc(pT_even, 1)

            def prologue(h0, h1):
                for i in range(NT):
                    e_tile(h0, i)

            def step(hs, ht, hn):
                t_copy(ht, 0)
                if hs:
                    e_tile(hs, 0)
                t_copy(ht, 2)
                if hs:
                    e_tile(hs, 1)
                    e_tile(hs, 2)
                if ht.chunks > 4:
                    t_copy(ht, 4)
                if hs:
                    e_tile(hs, 3)

            run_attention(act, "X", prologue, step, lambda: None)

            for b in range(B):
                xT_of("F", b)
            for b in range(B):
                act.wait_ge(f_nmax_s, b + 1)
                a.activation(f_e[:, b, :], f_max[:, b, 0:2], ACT.Exp, bias=f_nmax[:, b:b + 1],
                             accum_out=f_es[:, b:b + 1]).then_inc(f_exp, 1)
            for n, (b, k, m) in enumerate(F_CHUNKS):
                if k is None:
                    bias = col("F_b1m", 1, m)
                else:
                    if m == 0:
                        act.wait_ge(f_ld[b][k], 4 * 16)
                    bias = F_b1e[b][k][:, m:m + 1]
                act.wait_ge(f_h_mm, n + 1)
                if n >= 4:
                    act.wait_ge(f_y_mm, n - 3)
                a.activation(hT[n % 4][:], bank[n % 3][:], ACT.Gelu_apprx_tanh, bias=bias).then_inc(f_h, 1)

            for b in range(B):
                xT_of("D", b)
            for b in range(B):
                act.wait_ge(d_kv_mm, 2 * b + 2)
                a.activation(valuesT[b][:], bank[2 + b][:], ACT.Identity, bias=col("D_bv")).then_inc(d_v_ready, 1)
            run_attention(act, "D", prologue, step, lambda: None)

            for b in range(B):
                xT_of("E", b)
            for b in range(B):
                act.wait_ge(e_q_mm, b + 1)
                a.activation(e_qT[b][:], bank[b][:], ACT.Identity, bias=col("E_bq")).then_inc(e_q, 1)
            for b in range(B):
                act.wait_ge(e_max, b + 1)
                for i in range(NT):
                    last = a.activation(e_p[b][:, i, :], e_s[b][:, i, :], ACT.Exp, bias=e_nmax[:, b, i:i + 1],
                                        accum_out=e_sum[:, b, i:i + 1])
                last.then_inc(e_exp, 1)
            for b in range(B):
                act.wait_ge(e_t_mm, b + 1)
                a.copy(e_pT[b][:], bank[4 + b][0:C, :]).then_inc(e_pT_s, 1)

            for b in range(B):
                xT_of("M", b)
            for b in range(B):
                act.wait_ge(m_chain, M_CHAIN * b + 3)
                a.activation(m_le[:, b], m_ld[:, b], ACT.Exp).then_inc(m_lexp, 1)
                act.wait_ge(m_chain, M_CHAIN * b + M_CHAIN_D)
                a.activation(m_e[:, b], m_d[:, b], ACT.Exp).then_inc(m_exp, 1)
            for b in range(B):
                act.wait_ge(m_gT_mm, b + 1)
                a.copy(gT[b], bank[6 + b][0:NE, :]).then_inc(m_gT, 1)

            def gelu(e, s, n, first):
                m = n % NM
                act.wait_ge(m_h_mm, (B * NM) * e + n + 1)
                if not (first and n < NM):
                    act.wait_ge(m_y_mm, (B * NM) * e + n + 1 - NM)
                a.activation(hT[m][:], bank[m][:], ACT.Gelu, bias=M_b1[s][:, m:m + 1]).then_inc(m_h, 1)

            for e in range(2):
                for n in range(B * NM):
                    gelu(e, e, n, e == 0)
            with act.Fori(1, NE // 2) as i:
                for s in range(2):
                    for n in range(B * NM):
                        gelu(2 * i + s, s, n, False)

        @block.vector
        def _(dve):
            v = nc.vector

            def ln_stats_of(stage, b):
                n = ln_index(stage, b)
                if stage == "A":
                    dve.wait_ge(ld[f"x{b}"], 16)
                elif stage in READ_BY_LN:
                    dve.wait_ge(x_written[b], READ_BY_LN[stage])
                else:
                    dve.wait_ge(o_added, (B * H if stage == "E" else 0) + H * (b + 1))
                for i in range(NT):
                    last = v.bn_stats(bn[:, b, i, :], x[b][:, i, :])
                last.then_inc(ln_bn, 1)
                dve.wait_ge(ln_bn, n + 1)
                for i in range(NT):
                    last = v.bn_aggr(mv[:, b, i, :], bn[:, b, i, :])
                last.then_inc(ln_stats, 1)

            def ln_hat_of(stage, b):
                n = ln_index(stage, b)
                dve.wait_ge(ln_rstd, n + 1)
                for i in range(NT):
                    last = v.tensor_scalar(xhat[b][:, i, :], x[b][:, i, :], mv[:, b, i, 0:1], rstd[:, b, i:i + 1],
                                           ALU.subtract, ALU.mult)
                last.then_inc(ln_hat, 1)

            ln_stats_of("A", 0)
            ln_stats_of("A", 1)
            ln_hat_of("A", 0)
            ln_hat_of("A", 1)
            dve.wait_ge(ld["consts"], 16)
            dve.wait_ge(ld["rows"], 16)
            v.tensor_copy(a_mask[:, 0:P], const("blocks", P)).then_inc(a_mask_half, 1)
            v.tensor_tensor(a_mask[:, P:2 * P], const("blocks", P), row("norm_g"), ALU.mult).then_inc(a_mask_ready, 1)
            dve.wait_ge(a_mask_half, 1)
            dve.wait_ge(a_mask_ready, 1)
            dve.wait_ge(ld["cols"], 16)
            for b in range(B):
                dve.wait_ge(a_kv_mm, b + 1)
                v.tensor_copy(kv[b][:, 0:S], bank[4 * b + 2][:])
                v.tensor_copy(kv[b][:, S:2 * S], bank[4 * b + 3][:]).then_inc(a_kv, 1)
            for b in range(B):
                dve.wait_ge(a_g_mm, b + 1)
                v.tensor_tensor(gm[b][:], bank[4 * b][:, 0:2 * P], a_mask[:], ALU.mult)
                v.tensor_tensor(vsum[:, b:b + 1], bank[4 * b][:, 2 * P:2 * P + 1], col("norm_b"),
                                ALU.mult).then_inc(a_g, 1)
            for b in range(B):
                dve.wait_ge(a_gq_mm, b + 1)
                dve.wait_ge(a_q, b + 1)
                v.tensor_tensor(t1[b][:], bank[4 * b + 1][:], qT[b][:], ALU.mult).then_inc(a_t1, 1)
            for b in range(B):
                dve.wait_ge(a_n2_mm, b + 1)
                v.tensor_scalar(norm2[:, b], bank[4 * b + 2][:, 0:NT * HA], NORM_EPS ** 2, None,
                                ALU.max).then_inc(a_n2, 1)
            dve.wait_ge(ld["ctx"], 16)
            for b in range(B):
                last = v.bn_stats(c_bn[:, b, :], ctx_tok[:, b, :])
            last.then_inc(c_bn_s, 1)
            dve.wait_ge(c_bn_s, 1)
            for b in range(B):
                last = v.bn_aggr(c_mv[:, b, :], c_bn[:, b, :])
            last.then_inc(c_stats, 1)
            for b in range(B):
                dve.wait_ge(a_norm, b + 1)
                v.reciprocal(rnorm[:, b], norm[:, b]).then_inc(a_rnorm, 1)
                dve.wait_ge(a_rnorm, b + 1)
                dve.wait_ge(a_o_mm, b + 1)
                heads = "p (g e) -> p g e"
                v.tensor_tensor(kv[b][:, 0:S].rearrange(heads, e=P // HA), bank[4 * b + 3][:].rearrange(heads, e=P // HA),
                                rnorm[:, b].unsqueeze(2).to_broadcast((P, NT * HA, P // HA)),
                                ALU.mult).then_inc(a_o, 1)
            dve.wait_ge(c_rstd_s, 1)
            for b in range(B):
                last = v.tensor_scalar(c_hat[:, b, :], ctx_tok[:, b, :], c_mv[:, b, 0:1], c_rstd[:, b:b + 1],
                                       ALU.subtract, ALU.mult)
            last.then_inc(c_hat_s, 1)
            for b in range(B):
                dve.wait_ge(a_y_mm, b + 1)
                dve.wait_ge(x_written[b], W_A_BIAS)
                v.tensor_tensor(x[b][:], bank[4 * b + 1][:].rearrange("p (n d) -> p n d", d=P), x[b][:],
                                ALU.add).then_inc(x_written[b], 1)
            for b in range(B):
                ln_stats_of("X", b)
            dve.wait_ge(c_zT, 1)
            v.tensor_scalar(czkT[:], czT[:], SCALE, None, ALU.mult).then_inc(c_zkT, 1)
            dve.wait_ge(w_a_mm, 2)
            v.tensor_copy(X_A[:, 4:8, :].rearrange("p h k -> p (h k)"), bank[1][:]).then_inc(w_a, 1)
            dve.wait_ge(w_v_mm, 2)
            v.tensor_copy(X_V[:, 4:8, :].rearrange("p h k -> p (h k)"), bank[3][:]).then_inc(w_v, 1)
            dve.wait_ge(w_b_mm, 1)
            v.tensor_copy(X_r0[:], bank[5][:, 2 * P:2 * P + H]).then_inc(w_bias, 1)
            v.tensor_tensor(X_bias[:], bank[4][:, 0:P], row("X_bo"), ALU.add).then_inc(w_bias, 1)
            for b in range(B):
                ln_hat_of("X", b)
            for b in range(B):
                dve.wait_ge(ln_xT, ln_index("X", b) + 1)
                v.tensor_scalar(keysT[b][:], xT[b][:], SCALE, None, ALU.mult).then_inc(keys_ready, 1)
            for b in range(B):
                dve.wait_ge(w_vc_mm, b + 1)
                for half in range(2):
                    last = v.tensor_copy(X_vc[:, b, half * S:(half + 1) * S], bank[2 * b + half][0:C, :])
                last.then_inc(w_vc, 1)
            dve.wait_ge(e_kv_mm, 1)
            v.tensor_scalar(e_kT[:].rearrange("p b c -> p (b c)"), bank[4][:, 0:B * C], col("E_bk"), SCALE,
                            ALU.add, ALU.mult).then_inc(e_k_s, 1)
            v.tensor_tensor(e_v[:], bank[4][0:C, 2 * P:4 * P].rearrange("c (b d) -> c b d", b=B),
                            rows[0:C, ROWS["E_bv"]:ROWS["E_bv"] + P].unsqueeze(1).to_broadcast((C, B, P)),
                            ALU.add).then_inc(e_v_s, 1)
            dve.wait_ge(ld["mask"], 16)
            v.tensor_scalar(e_tmp[:], mask[:].rearrange("p b n c -> p (b n c)"), 0.0, -2.0, ALU.is_equal,
                            ALU.mult).then_inc(e_l1, 1)
            dve.wait_ge(e_l1, 1)
            v.tensor_scalar(e_lim[:], e_tmp[:], 1.0, BIG, ALU.add, ALU.mult).then_inc(e_lim_s, 1)

            def r_copy(hd):
                dve.wait_ge(r_mm, hd.g + 1)
                src, dst = bank[R_BANK][:], rT[hd.par][:]
                if hd.kind == "X":
                    v.tensor_scalar(dst, src, X_r0[:, bass.ds(hd.h, 1)], None, ALU.add).then_inc(r_ready, 1)
                else:
                    v.scalar_tensor_tensor(dst, src, cols[:, bass.ds(hd.h + COLS["D_bq"], 1)], const("peT", S),
                                           ALU.add, ALU.add).then_inc(r_ready, 1)

            def v_copy(hd):
                dve.wait_ge(v_mm, hd.g + 1)
                v.tensor_copy(vw[hd.par][:].rearrange("p n d -> p (n d)"), bank[V_BANK][:]).then_inc(v_ready, 1)

            def c_max(hd):
                if hd.kind == "X":
                    dve.wait_ge(c_s_mm, hd.g + 1)
                    v.tensor_reduce(neg_cmax[:, hd.par, :], bank[C_BANK][:, 0:NT * C].rearrange("p (n c) -> p n c", c=C),
                                    AX, ALU.max, negate=True).then_inc(cmax_ready, 1)
                    dve.wait_ge(cmax_ready, hd.g + 1)

            def x_max(hd, i):
                dve.wait_ge(s_mm, hd.g * NT + i + 1)
                n = hd.keys(i)
                v.tensor_scalar(spill[:, i, 0:n], bank[S_BANK[i % 2]][:, 0:n], -1.0,
                                neg_cmax[:, hd.par, i:i + 1] if hd.kind == "X" else None, ALU.mult, ALU.min,
                                accum_out=neg_max[:, hd.par, i:i + 1]).then_inc(max_ready, 1)

            def t_copy(hd, c):
                dve.wait_ge(t_mm, hd.c0 + c + 1)
                lo = 0 if hd.kind == "X" else c * P
                v.tensor_copy(pT[:, c, lo:S], bank[T_BANK[1]][:, lo:S]).then_inc(pT_odd, 1)

            def add_head(hd):
                p = hd.par
                dve.wait_ge(probs_ready, (hd.g + 1) * NT)
                if hd.kind == "X":
                    v.tensor_tensor(denom[:, p], sum_x[:, p], sum_c[:, p], ALU.add).then_inc(denom_ready, 1)
                    dve.wait_ge(denom_ready, hd.g + 1)
                    v.reciprocal(rdenom[:, p], denom[:, p]).then_inc(rdenom_ready, 1)
                else:
                    v.reciprocal(rdenom[:, p], sum_x[:, p]).then_inc(rdenom_ready, 1)
                dve.wait_ge(rdenom_ready, hd.g + 1)
                dve.wait_ge(o_mm, hd.g + 1)
                dve.wait_ge(x_written[hd.b], W_X_BIAS if hd.kind == "X" else W_F)
                if not hd.very_first:
                    dve.wait_ge(o_added, hd.g)
                for i in range(NT):
                    last = v.scalar_tensor_tensor(x[hd.b][:, i, :], bank[O_BANK][:, i * P:(i + 1) * P],
                                                  rdenom[:, p, i:i + 1], x[hd.b][:, i, :], ALU.mult, ALU.add)
                last.then_inc(o_added, 1)

            def prologue(h0, h1):
                r_copy(h0)
                c_max(h0)
                for i in range(NT):
                    x_max(h0, i)
                r_copy(h1)
                v_copy(h0)

            def step(hs, ht, hn):
                if hs:
                    c_max(hs)
                    x_max(hs, 0)
                t_copy(ht, 1)
                if hs:
                    x_max(hs, 1)
                    x_max(hs, 2)
                t_copy(ht, 3)
                if hs:
                    x_max(hs, 3)
                if hn:
                    r_copy(hn)
                if hs:
                    v_copy(hs)
                add_head(ht)

            def norm_next(stage):
                ln_stats_of(stage, 0)
                ln_hat_of(stage, 0)

            run_attention(dve, "X", prologue, step, lambda: norm_next("F"))

            ln_stats_of("F", 1)
            ln_hat_of("F", 1)
            v.tensor_scalar(f_a[:], row("alpha", 1), 0.1, 1.0, ALU.max, ALU.min).then_inc(f_a1, 1)
            dve.wait_ge(f_a1, 1)
            v.tensor_scalar(f_1a[:], f_a[:], -1.0, 1.0, ALU.mult, ALU.add).then_inc(f_a_s, 1)
            dve.wait_ge(ld["F_W2m"], 16)
            v.tensor_scalar(F_W2m[:], F_W2m[:], f_a[:], None, ALU.mult).then_inc(f_w2m, 1)
            v.tensor_scalar(f_bias0[:], row("F_b2m"), f_a[:], None, ALU.mult).then_inc(f_bias0_s, 1)
            dve.wait_ge(f_a_s, 1)
            dve.wait_ge(f_bias0_s, 1)
            for b in range(B):
                dve.wait_ge(f_lg_mm, b + 1)
                v.tensor_tensor(f_lg[:, b], bank[6 + b][:, 0:NE], row("F_b_gate", NE),
                                ALU.add).then_inc(f_lg_s, 1)
                dve.wait_ge(f_lg_s, b + 1)
                v.max(f_max[:, b], f_lg[:, b]).then_inc(f_max_s, 1)
                dve.wait_ge(f_max_s, b + 1)
                v.max_index(f_idx[:, b], f_max[:, b], f_lg[:, b]).then_inc(f_idx_s, 1)
                v.tensor_scalar(f_nmax[:, b:b + 1], f_max[:, b, 0:1], -1.0, None, ALU.mult).then_inc(f_nmax_s, 1)
            for b in range(B):
                dve.wait_ge(f_exp, b + 1)
                v.reciprocal(f_ers[:, b:b + 1], f_es[:, b:b + 1]).then_inc(f_rs, 1)
                dve.wait_ge(f_rs, b + 1)
                v.tensor_scalar(f_g[:, b, :], f_e[:, b, :], f_ers[:, b:b + 1], f_1a[:], ALU.mult,
                                ALU.mult).then_inc(f_gk, 1)
            for b in range(B):
                dve.wait_ge(f_gk, b + 1)
                for k in range(2):
                    dve.wait_ge(f_ld[b][k], 4 * 16)
                    v.tensor_scalar(F_W2e[b][k], F_W2e[b][k], f_g[:, b, k:k + 1], None,
                                    ALU.mult).then_inc(f_w2e, 1)
                v.scalar_tensor_tensor(f_bias1[:, b], F_b2e[b][0][:], f_g[:, b, 0:1], f_bias0[:], ALU.mult,
                                       ALU.add).then_inc(f_b1, 1)
                dve.wait_ge(f_b1, b + 1)
                v.scalar_tensor_tensor(f_bias[:, b], F_b2e[b][1][:], f_g[:, b, 1:2], f_bias1[:, b], ALU.mult,
                                       ALU.add).then_inc(f_bias_s, 1)
            for b in range(B):
                dve.wait_ge(f_y_mm, F_DONE[b])
                dve.wait_ge(x_written[b], W_F_BIAS)
                v.tensor_tensor(x[b][:], bank[3 + b][:].rearrange("p (n d) -> p n d", d=P), x[b][:],
                                ALU.add).then_inc(x_written[b], 1)
                ln_stats_of("D", b)
                ln_hat_of("D", b)
            for b in range(B):
                dve.wait_ge(d_kv_mm, 2 * b + 1)
                v.scalar_tensor_tensor(e_o[b].rearrange("p n d -> p (n d)"), bank[b][:], col("D_bk"),
                                       const("peT", S), ALU.add, ALU.add).then_inc(d_k1, 1)
                dve.wait_ge(d_k1, b + 1)
                v.tensor_scalar(keysT[b][:], e_o[b].rearrange("p n d -> p (n d)"), SCALE, None,
                                ALU.mult).then_inc(keys_ready, 1)
            run_attention(dve, "D", prologue, step, lambda: norm_next("E"))

            ln_stats_of("E", 1)
            ln_hat_of("E", 1)
            for b in range(B):
                dve.wait_ge(e_s_mm, b + 1)
                v.tensor_tensor(e_s[b][:].rearrange("p n c -> p (n c)"), bank[2 + b][:, 0:NT * C],
                                e_lim[:, b * NT * C:(b + 1) * NT * C], ALU.min).then_inc(e_ss, 1)
                dve.wait_ge(e_ss, b + 1)
                v.tensor_reduce(e_nmax[:, b], e_s[b][:], AX, ALU.max, negate=True).then_inc(e_max, 1)
            for b in range(B):
                dve.wait_ge(e_exp, b + 1)
                v.reciprocal(e_rsum[:, b], e_sum[:, b]).then_inc(e_rs, 1)
            for b in range(B):
                dve.wait_ge(e_rs, b + 1)
                dve.wait_ge(e_o_mm, b + 1)
                for i in range(NT):
                    last = v.tensor_scalar(e_o[b][:, i, :], bank[b][:, i * P:(i + 1) * P], e_rsum[:, b, i:i + 1], None,
                                           ALU.mult)
                last.then_inc(e_o_s, 1)
                dve.wait_ge(e_o_s, b + 1)
                for i in range(NT):
                    last = v.bn_stats(bn[:, b, i, :], e_o[b][:, i, :])
                last.then_inc(e_bn_s, 1)
                dve.wait_ge(e_bn_s, b + 1)
                for i in range(NT):
                    last = v.bn_aggr(mv[:, b, i, :], bn[:, b, i, :])
                last.then_inc(e_st, 1)
            for b in range(B):
                dve.wait_ge(e_r, b + 1)
                for i in range(NT):
                    last = v.tensor_scalar(e_on[b][:, i, :], e_o[b][:, i, :], mv[:, b, i, 0:1], rstd[:, b, i:i + 1],
                                           ALU.subtract, ALU.mult)
                last.then_inc(e_on_s, 1)
                dve.wait_ge(e_on_s, b + 1)
                v.tensor_tensor(e_og[b], e_on[b], row("ln_gamma").unsqueeze(1).to_broadcast((P, NT, P)),
                                ALU.mult).then_inc(e_g_s, 1)
                dve.wait_ge(e_g_s, b + 1)
                v.tensor_tensor(e_on[b], e_og[b], row("ln_beta").unsqueeze(1).to_broadcast((P, NT, P)),
                                ALU.add).then_inc(e_gb_s, 1)
                dve.wait_ge(e_gb_s, b + 1)
                v.tensor_tensor(x[b][:], e_on[b], x[b][:], ALU.add).then_inc(x_written[b], 1)
                ln_stats_of("M", b)
                ln_hat_of("M", b)

            dve.wait_ge(m_zero, 1)
            for b in range(B):
                done = [M_CHAIN * b]

                def then(ins):
                    done[0] += 1
                    ins.then_inc(m_chain, 1)
                    dve.wait_ge(m_chain, done[0])

                tiles = (P, NT, NL)
                lang = m_lg[b][:, :, NE:NE + NL]
                dve.wait_ge(m_lg_mm, b + 1)
                then(v.tensor_tensor(m_lg[b][:], bank[4 + b][:, 0:NT * (NE + NL)].rearrange("p (n e) -> p n e", n=NT),
                                     row("M_bias", NE + NL).unsqueeze(1).to_broadcast((P, NT, NE + NL)), ALU.add))
                then(v.tensor_reduce(m_lmax[:, b], lang, AX, ALU.max))
                then(v.tensor_tensor(m_ld[:, b], lang, m_lmax[:, b].unsqueeze(2).to_broadcast(tiles), ALU.subtract))
                dve.wait_ge(m_lexp, b + 1)
                then(v.tensor_reduce(m_ls[:, b], m_le[:, b], AX, ALU.add))
                then(v.reciprocal(m_lr[:, b], m_ls[:, b]))
                then(v.tensor_tensor(m_lp[:, b, :, 0:NL], m_le[:, b], m_lr[:, b].unsqueeze(2).to_broadcast(tiles),
                                     ALU.mult))
                then(v.tensor_tensor(m_ew[:, b], m_lp[:, b, :, 0:NL], m_lp[:, b, :, 1:NL + 1], ALU.add))
                v.scalar_tensor_tensor(m_rl[b][:, :, 0:NL], m_ew[:, b], 0.1, m_lg[b][:, :, 0:NL], ALU.mult, ALU.add)
                then(v.scalar_tensor_tensor(m_rl[b][:, :, NL:NE], m_ew[:, b], 0.1, m_lg[b][:, :, NL:NE], ALU.mult,
                                            ALU.add))
                for i in range(NT):
                    last = v.max(m_max[:, b, i, :], m_rl[b][:, i, :])
                then(last)
                for i in range(NT):
                    last = v.max_index(m_idx[:, b, i, :], m_max[:, b, i, :], m_rl[b][:, i, :])
                then(last)
                then(v.tensor_tensor(m_d[:, b], m_max[:, b, :, 1], m_max[:, b, :, 0], ALU.subtract))
                assert done[0] == M_CHAIN * b + M_CHAIN_D
                then(v.tensor_copy(m_idxf[:, b], m_idx[:, b, :, 0:2]))
                dve.wait_ge(m_exp, b + 1)
                then(v.tensor_scalar(m_s[:, b], m_e[:, b], 1.0, None, ALU.add))
                then(v.reciprocal(m_g0[:, b], m_s[:, b]))
                then(v.tensor_tensor(m_g1[:, b], m_g0[:, b], m_e[:, b], ALU.mult))
                for k, gk in enumerate((m_g0, m_g1)):
                    then(v.tensor_tensor(m_oh[:, b, k], const("iota", NE).unsqueeze(1).to_broadcast((P, NT, NE)),
                                         m_idxf[:, b, :, k:k + 1].to_broadcast((P, NT, NE)), ALU.is_equal))
                    then(v.tensor_tensor(m_og[:, b, k], m_oh[:, b, k],
                                         gk[:, b].unsqueeze(2).to_broadcast((P, NT, NE)), ALU.mult))
                assert done[0] == M_CHAIN * (b + 1)
                v.tensor_tensor(gates[b][:], m_og[:, b, 0], m_og[:, b, 1], ALU.add).then_inc(m_gates, 1)
            for b in range(B):
                dve.wait_ge(m_b_mm, b + 1)
                dve.wait_ge(x_written[b], W_E)
                v.tensor_tensor(x[b][:], bank[4 + b][:].rearrange("p (n d) -> p n d", d=P), x[b][:],
                                ALU.add).then_inc(x_written[b], 1)
            dve.wait_ge(m_gates, B)

            def add_expert(e, b):
                dve.wait_ge(m_y_mm, e * (B * NM) + NM * (b + 1))
                dve.wait_ge(x_written[b], e + W_M_BIAS)
                for i in range(NT):
                    last = v.scalar_tensor_tensor(x[b][:, i, :], bank[4 + b][:, i * P:(i + 1) * P],
                                                  gates[b][:, i, bass.ds(e, 1)], x[b][:, i, :], ALU.mult, ALU.add)
                last.then_inc(x_written[b], 1)

            with dve.Fori(0, NE) as e:
                for b in range(B):
                    add_expert(e, b)

        @block.tensor
        def _(pe):
            def mm(out, lhsT, rhs, start=True, stop=True):
                return nc.tensor.matmul(out, lhsT, rhs, start=start, stop=stop, skip_group_check=True)

            def tile_of(bk, i, n=P):
                return bank[bk][:, i * n:(i + 1) * n]

            def transposes(stage, b):
                pe.wait_ge(ln_hat, ln_index(stage, b) + 1)
                for i in range(NT):
                    last = nc.tensor.transpose(tile_of(TR_BANK[stage][b], i), xhat[b][:, i, :], ident)
                last.then_inc(ln_mm, 1)

            pe.wait_ge(ld["consts"], 16)
            pe.wait_ge(ld["A_wqkvT"], 16)
            for b in range(B):
                transposes("A", b)
            for b in range(B):
                k = 4 * b
                pe.wait_ge(ln_xT, b + 1)
                mm(bank[k + 1][:], A_wqkvT[:, 0:P], xT[b][:]).then_inc(a_q_mm, 1)
                for i in range(NT):
                    last = mm(bank[k + 2 + i // 2][:, (i % 2) * 2 * P:(i % 2 + 1) * 2 * P],
                              xT[b][:, i * P:(i + 1) * P], A_wqkvT[:, P:3 * P])
                last.then_inc(a_kv_mm, 1)
            for b in range(B):
                pe.wait_ge(a_kv, b + 1)
                k4 = kv[b][:].rearrange("p (n w) -> p n w", n=NT)
                for i in range(NT):
                    mm(bank[4 * b][:, 0:2 * P], k4[:, i, 0:P], k4[:, i, :], i == 0, i == NT - 1)
                for i in range(NT):
                    last = mm(bank[4 * b][:, 2 * P:2 * P + 1], k4[:, i, P:2 * P], const("ones", 1), False, i == NT - 1)
                last.then_inc(a_g_mm, 1)
            for b in range(B):
                pe.wait_ge(a_g, b + 1)
                pe.wait_ge(a_q, b + 1)
                mm(bank[4 * b + 1][:], gm[b][:, 0:P], qT[b][:]).then_inc(a_gq_mm, 1)
                for i in range(NT):
                    last = mm(tile_of(4 * b + 3, i), qT[b][:, i * P:(i + 1) * P], gm[b][:, P:2 * P])
                last.then_inc(a_o_mm, 1)
            for b in range(B):
                pe.wait_ge(a_t1, b + 1)
                for i in range(NT):
                    last = mm(tile_of(4 * b + 2, i, HA), t1[b][:, i * P:(i + 1) * P], const("head_sum", HA))
                last.then_inc(a_n2_mm, 1)
            for b in range(B):
                pe.wait_ge(a_o, b + 1)
                for i in range(NT):
                    last = nc.tensor.transpose(tile_of(4 * b, i), kv[b][:, i * P:(i + 1) * P], ident)
                last.then_inc(a_oT_mm, 1)
            pe.wait_ge(ld["A_woutT"], 16)
            for b in range(B):
                pe.wait_ge(a_oT, b + 1)
                for i in range(NT):
                    last = mm(tile_of(4 * b + 1, i), t1[b][:, i * P:(i + 1) * P], A_woutT[:])
                last.then_inc(a_y_mm, 1)
            pe.wait_ge(c_hat_s, 1)
            for b in range(B):
                last = nc.tensor.transpose(bank[2][:, b * C:(b + 1) * C], c_hat[:, b, :], ident[0:C, 0:C])
            last.then_inc(c_mm, 1)
            for n in ("X_WqT", "X_WkT", "X_WvT", "X_Wo"):
                pe.wait_ge(ld[n], 16)
            pe.wait_ge(ld["cols"], 16)
            for b in range(B):
                pe.wait_ge(x_written[b], W_A)
            for h in range(H):
                last = mm(tile_of(h // 4, h % 4), X_WqT[:, h, :], X_WkT[:, h, :])
                if h % 4 == 3:
                    last.then_inc(w_a_mm, 1)
            pe.wait_ge(c_zT, 1)
            for h in range(H):
                last = mm(tile_of(2 + h // 4, h % 4), X_WvT[:, h, :], X_Wo[:, h, :])
                if h % 4 == 3:
                    last.then_inc(w_v_mm, 1)
            for h in range(H):
                mm(bank[5][:, 2 * P + h:2 * P + h + 1], X_WkT[:, h, :], col("X_bq", 1, h))
            for h in range(H):
                last = mm(bank[4][:, 0:P], col("X_bv", 1, h).to_broadcast((P, P)), X_Wo[:, h, :], h == 0, h == H - 1)
            last.then_inc(w_b_mm, 1)
            for b in range(B):
                transposes("X", b)
            pe.wait_ge(c_zkT, 1)
            pe.wait_ge(w_v, 2)
            pe.wait_ge(w_a, 2)
            for b in range(B):
                for half in range(2):
                    last = mm(bank[2 * b + half][0:C, :], czT[:, b, :],
                              X_V[:, 4 * half:4 * half + 4, :].rearrange("p h k -> p (h k)"))
                last.then_inc(w_vc_mm, 1)
            pe.wait_ge(ld["ctxT"], 16)
            pe.wait_ge(ld["E_W"], 3 * 16)
            pe.wait_ge(w_bias, 2)
            mm(bank[4][:, 0:B * C], E_Wk[:], ctxT[:].rearrange("p b c -> p (b c)"))
            for b in range(B):
                last = mm(bank[4][0:C, (2 + b) * P:(3 + b) * P], ctxT[:, b, :], E_Wv[:])
            last.then_inc(e_kv_mm, 1)

            def queries(hd):
                pe.wait_ge(w_head_ready, hd.g + 1)
                if not hd.very_first:
                    pe.wait_ge(r_ready, hd.g)
                mm(bank[R_BANK][:], w_head[hd.par][:], xT[hd.b][:]).then_inc(r_mm, 1)

            def values(hd):
                if not hd.very_first:
                    pe.wait_ge(v_ready, hd.g)
                src = xT[hd.b] if hd.kind == "X" else valuesT[hd.b]
                w = X_V if hd.kind == "X" else D_Wo
                for i in range(NT):
                    last = mm(tile_of(V_BANK, i), src[:, i * P:(i + 1) * P],
                              w[:, bass.ds(hd.h, 1), :].rearrange("p a k -> p (a k)"))
                last.then_inc(v_mm, 1)

            def scores_c(hd):
                pe.wait_ge(r_ready, hd.g + 1)
                if hd.kind == "X":
                    for i in range(NT):
                        last = mm(bank[C_BANK][:, i * C:(i + 1) * C], rT[hd.par][:, i * P:(i + 1) * P],
                                  czkT[:, hd.b, :])
                    last.then_inc(c_s_mm, 1)

            def scores(hd, i, fresh=False):
                n = hd.keys(i)
                if not (fresh and i < 2):
                    pe.wait_ge(probs_ready, hd.g * NT + i - 1)
                dst, q = bank[S_BANK[i % 2]], rT[hd.par][:, i * P:(i + 1) * P]
                if hd.kind == "X":
                    mm(dst[:], q, keysT[hd.b][:]).then_inc(s_mm, 1)
                else:
                    mm(dst[:, 0:n], q, keysT[hd.b][:, 0:n], True, False)
                    mm(dst[:, n - P:n], ident_bf[:], causal_bf[:], False, True).then_inc(s_mm, 1)

            def turn(hd, c):
                if c == 0:
                    pe.wait_ge(probs_ready, (hd.g + 1) * NT)
                if c % 2 == 0:
                    if not (hd.very_first and c == 0):
                        pe.wait_ge(pT_even, hd.even0 + c // 2)
                elif not (hd.very_first and c == 1):
                    pe.wait_ge(pT_odd, hd.odd0 + c // 2)
                k = C if c == NT else P
                first = 0 if hd.kind == "X" else c
                for i in range(first, NT):
                    last = nc.tensor.transpose(bank[T_BANK[c % 2]][0:k, i * P:(i + 1) * P],
                                               probs[hd.par][:, i, c * P:c * P + k], ident)
                last.then_inc(t_mm, 1)

            def weigh(hd, c):
                hd.chunk_ready(pe, c)
                if c == 0:
                    pe.wait_ge(v_ready, hd.g + 1)
                    if not hd.very_first:
                        pe.wait_ge(o_added, hd.g)
                first = 0 if hd.kind == "X" else c
                for i in range(first, NT):
                    if c == NT:
                        l, r = pT[0:C, c, i * P:(i + 1) * P], X_vc[:, hd.b, bass.ds(hd.h * P, P)]
                    else:
                        l, r = pT[:, c, i * P:(i + 1) * P], vw[hd.par][:, c, :]
                    last = mm(tile_of(O_BANK, i), l, r, c == 0 and i == 0, c == hd.chunks - 1)
                if c == hd.chunks - 1:
                    last.then_inc(o_mm, 1)

            def prologue(h0, h1):
                queries(h0)
                scores_c(h0)
                for i in range(NT):
                    scores(h0, i, h0.kind == "X")
                queries(h1)
                values(h0)

            def step(hs, ht, hn):
                turn(ht, 0)
                if hs:
                    scores_c(hs)
                    scores(hs, 0)
                turn(ht, 1)
                weigh(ht, 0)
                if hs:
                    scores(hs, 1)
                turn(ht, 2)
                weigh(ht, 1)
                if hs:
                    scores(hs, 2)
                turn(ht, 3)
                weigh(ht, 2)
                if hs:
                    scores(hs, 3)
                if ht.chunks > NT:
                    turn(ht, NT)
                weigh(ht, 3)
                if hn:
                    queries(hn)
                if hs:
                    values(hs)
                if ht.chunks > NT:
                    weigh(ht, NT)

            pe.wait_ge(keys_ready, B)
            pe.wait_ge(w_vc, B)
            pe.wait_ge(e_v_s, 1)
            run_attention(pe, "X", prologue, step, lambda: None)

            for b in range(B):
                transposes("F", b)
            pe.wait_ge(ld["F_w_gate"], 16)
            for b in range(B):
                pe.wait_ge(f_mean, b + 1)
                mm(bank[6 + b][:, 0:NE], mean_bc[:, b, :], F_w_gate[:]).then_inc(f_lg_mm, 1)
            pe.wait_ge(ld["F_W1m"], 16)
            for n in range(len(F_CHUNKS) + 2):
                if n < len(F_CHUNKS):
                    b, k, m = F_CHUNKS[n]
                    if k is not None and m == 0:
                        pe.wait_ge(f_ld[b][k], 4 * 16)
                    if n >= 3:
                        pe.wait_ge(f_h, n - 2)
                    w = F_W1m if k is None else F_W1e[b][k]
                    mm(bank[n % 3][:], w[:, m * P:(m + 1) * P], xT[b][:]).then_inc(f_h_mm, 1)
                if n >= 2:
                    b, k, m = F_CHUNKS[n - 2]
                    pe.wait_ge(f_h, n - 1)
                    if n == 2:
                        pe.wait_ge(f_w2m, 1)
                    if k is not None and m == 0:
                        pe.wait_ge(f_w2e, 2 * b + k + 1)
                    w = F_W2m if k is None else F_W2e[b][k]
                    for i in range(NT):
                        last = mm(tile_of(3 + b, i), hT[(n - 2) % 4][:, i * P:(i + 1) * P], w[:, m, :],
                                  k is None and m == 0 and i == 0, k == 1 and m == NM - 1)
                    last.then_inc(f_y_mm, 1)

            for b in range(B):
                transposes("D", b)
            pe.wait_ge(ld["D_Wkv"], 16)
            pe.wait_ge(ld["D_Wo"], 16)
            for b in range(B):
                pe.wait_ge(ln_xT, ln_index("D", b) + 1)
                mm(bank[b][:], D_Wkv[:, 0:P], xT[b][:]).then_inc(d_kv_mm, 1)
                mm(bank[2 + b][:], D_Wkv[:, P:2 * P], xT[b][:]).then_inc(d_kv_mm, 1)
            pe.wait_ge(bf_ready, 2)
            pe.wait_ge(keys_ready, 2 * B)
            pe.wait_ge(d_v_ready, B)
            run_attention(pe, "D", prologue, step, lambda: None)

            for b in range(B):
                transposes("E", b)
            for b in range(B):
                pe.wait_ge(ln_xT, ln_index("E", b) + 1)
                mm(bank[b][:], E_Wq[:], xT[b][:]).then_inc(e_q_mm, 1)
            pe.wait_ge(e_k_s, 1)
            for b in range(B):
                pe.wait_ge(e_q, b + 1)
                for i in range(NT):
                    last = mm(bank[2 + b][:, i * C:(i + 1) * C], e_qT[b][:, i * P:(i + 1) * P], e_kT[:, b, :])
                last.then_inc(e_s_mm, 1)
            for b in range(B):
                pe.wait_ge(e_exp, b + 1)
                for i in range(NT):
                    last = nc.tensor.transpose(bank[4 + b][0:C, i * P:(i + 1) * P], e_p[b][:, i, :], ident)
                last.then_inc(e_t_mm, 1)
            for b in range(B):
                pe.wait_ge(e_pT_s, b + 1)
                for i in range(NT):
                    last = mm(tile_of(b, i), e_pT[b][:, i * P:(i + 1) * P], e_v[:, b, :])
                last.then_inc(e_o_mm, 1)

            for b in range(B):
                transposes("M", b)
            pe.wait_ge(ld["M_w"], 16)
            for b in range(B):
                pe.wait_ge(ln_xT, ln_index("M", b) + 1)
                for i in range(NT):
                    last = mm(tile_of(4 + b, i, NE + NL), xT[b][:, i * P:(i + 1) * P], M_w[:])
                last.then_inc(m_lg_mm, 1)

            def hidden(e, n, fresh=False):
                b, m, s = n // NM, n % NM, e[1]
                if n == 0:
                    pe.wait_ge(m_w_slot[s], e[2])
                if not (fresh and n < NM):
                    pe.wait_ge(m_h, B * NM * e[0] + n + 1 - NM)
                mm(bank[m][:], M_w1[s][:, m * P:(m + 1) * P], xT[b][:]).then_inc(m_h_mm, 1)

            def output(e, n):
                b, m, s = n // NM, n % NM, e[1]
                pe.wait_ge(m_h, B * NM * e[0] + n + 1)
                if m == 0:
                    pe.wait_ge(x_written[b], e[0] + W_M_BIAS)
                for i in range(NT):
                    last = mm(tile_of(4 + b, i), hT[m][:, i * P:(i + 1) * P], M_w2[s][:, m, :], m == 0 and i == 0,
                              m == NM - 1)
                last.then_inc(m_y_mm, 1)

            hidden((0, 0, 48), 0, True)
            hidden((0, 0, 48), 1, True)
            for b in range(B):
                pe.wait_ge(m_gates, b + 1)
                for i in range(NT):
                    last = nc.tensor.transpose(bank[6 + b][0:NE, i * P:(i + 1) * P], gates[b][:, i, :], ident)
                last.then_inc(m_gT_mm, 1)
            pe.wait_ge(ld["M_b2"], 16)
            for b in range(B):
                pe.wait_ge(m_gT, b + 1)
                for i in range(NT):
                    last = mm(tile_of(4 + b, i), gT[b][:, i * P:(i + 1) * P], M_b2[:])
                last.then_inc(m_b_mm, 1)

            n_chunks = B * NM

            def pair(e, last_pair=False):
                for s in range(2):
                    for n in range(n_chunks):
                        at = s * n_chunks + n + 2
                        if at < 2 * n_chunks:
                            hidden(e(at // n_chunks), at % n_chunks, False)
                        elif not last_pair:
                            hidden(e(2), at % n_chunks, False)
                        output(e(s), n)

            def of(i):
                return lambda s: (2 * i + s, s % 2, (i + (1 + s // 2)) * 48)

            for s in range(2):
                for n in range(n_chunks):
                    at = s * n_chunks + n + 2
                    hidden(of(0)(at // n_chunks), at % n_chunks, at < NM)
                    output(of(0)(s), n)
            with pe.Fori(1, NE // 2 - 1) as i:
                pair(of(i))
            pair(of(NE // 2 - 1), True)


F_CHUNKS = ([(b, None, m) for b in range(B) for m in range(NM)]
            + [(b, k, m) for b in range(B) for k in range(2) for m in range(NM)])
F_DONE = [B * NM + 2 * NM * (b + 1) for b in range(B)]
M_CHAIN = 19
M_CHAIN_D = 11


def positions():
    pos = np.arange(S, dtype=np.float32)[:, None]
    inv_freq = np.exp(np.float32(-np.log(10000.0)) * np.arange(0, P, 2, dtype=np.float32) / np.float32(P))
    ang = (pos * inv_freq[None, :]).astype(np.float32)
    pe = np.zeros((S, P), np.float32)
    pe[:, 0::2] = np.sin(ang)
    pe[:, 1::2] = np.cos(ang)
    return pe.T


def constants():
    p = np.arange(P)
    blocks = (p[:, None] // (P // HA) == p[None, :] // (P // HA)).astype(np.float32)
    parts = {
        "ident": np.eye(P), "blocks": np.concatenate([blocks, blocks], 1),
        "head_sum": p[:, None] // (P // HA) == np.arange(HA)[None, :],
        "causal": np.where(p[None, :] <= p[:, None], 0.0, NEG),
        "iota": np.broadcast_to(np.arange(NE), (P, NE)), "ones": np.ones((P, 1)), "peT": positions()}
    return np.concatenate([np.asarray(parts[n], np.float32) for n in CONSTS], 1)


def kernel(**inputs):
    import concourse.bacc as bacc
    from concourse.bass_utils import run_bass_kernel_spmd

    w = {n: np.asarray(a) for n, a in inputs.items()}

    def as_cols(v):
        return np.reshape(v, (-1, P)).T

    per_head = P // HA
    bkv = w["L0_xattn_bkv"]
    cols = {
        "norm_b": np.repeat(w["L0_attn_norm_b"].reshape(HA), per_head),
        "gamma_media": w["L0_xattn_gamma_media"], "beta_media": w["L0_xattn_beta_media"],
        "gamma_lat": w["L0_xattn_gamma_lat"], "beta_lat": w["L0_xattn_beta_lat"],
        "X_bq": w["L0_xattn_bq"], "X_bv": bkv[H * P:],
        "F_b1m": w["L0_ffn_b1m"], "D_bq": w["L1_attn_bq"],
        "D_bk": w["L1_attn_bkv"][:P], "D_bv": w["L1_attn_bkv"][P:],
        "E_bq": w["L1_xattn_bq"], "E_bk": w["L1_xattn_bk"]}
    rows = {
        "norm_g": np.repeat(w["L0_attn_norm_g"].reshape(HA), per_head), "A_b_out": w["L0_attn_b_out"],
        "X_bo": w["L0_xattn_bo"], "F_b_gate": w["L0_ffn_b_gate"], "F_b2m": w["L0_ffn_b2m"],
        "alpha": w["L0_ffn_alpha"], "E_bv": w["L1_xattn_bv"], "ln_gamma": w["L1_xattn_ln_gamma"],
        "ln_beta": w["L1_xattn_ln_beta"], "M_bias": np.concatenate([w["L1_ffn_router_b"], w["L1_ffn_lang_b"]])}
    arrays = {
        "x": w["x"], "ctx": w["ctx_1024"], "mask": w["mask_BxSxS2_ik1"],
        "ctxT": w["ctx_1024"].transpose(2, 0, 1),
        "cols": np.concatenate([as_cols(cols[n]) for n in COLS], 1),
        "rows": np.concatenate([rows[n].reshape(1, -1) for n in ROWS], 1),
        "consts": constants(),
        "A_wqkvT": w["L0_attn_w_qkv"].T, "A_woutT": w["L0_attn_w_out"].T,
        "X_WqT": w["L0_xattn_Wq"].T, "X_WkvT": w["L0_xattn_Wkv"].T, "X_Wo": w["L0_xattn_Wo"],
        "F_w_gate": w["L0_ffn_w_gate"], "F_W1m": w["L0_ffn_W1m"], "F_W2m": w["L0_ffn_W2m"],
        "F_W1e": w["L0_ffn_W1e"], "F_W2e": w["L0_ffn_W2e"], "F_b2e": w["L0_ffn_b2e"],
        "F_b1eT": as_cols(w["L0_ffn_b1e"]),
        "D_Wq": w["L1_attn_Wq"], "D_Wkv": w["L1_attn_Wkv"], "D_Wo": w["L1_attn_Wo"],
        "E_Wq": w["L1_xattn_Wq"], "E_Wk": w["L1_xattn_Wk"], "E_Wv": w["L1_xattn_Wv"],
        "M_w": np.concatenate([w["L1_ffn_router_w"], w["L1_ffn_lang_w"]]).T, "M_b2": w["L1_ffn_b2"],
        "M_b1T": as_cols(w["L1_ffn_b1"]), "M_w1": w["L1_ffn_w1"], "M_w2": w["L1_ffn_w2"]}
    arrays = {n: np.ascontiguousarray(a) for n, a in arrays.items()}
    nc = bacc.Bacc("TRN2", target_bir_lowering=False, num_devices=1)
    tensors = {n: nc.dram_tensor(n + "_dram", a.shape, mybir.dt.from_np(a.dtype), kind="ExternalInput").ap()
               for n, a in arrays.items()}
    tensors["out"] = nc.dram_tensor("out_dram", (B, S, P), F32, kind="ExternalOutput").ap()
    build(nc, tensors)
    result = run_bass_kernel_spmd(nc, [{n + "_dram": a for n, a in arrays.items()}], core_ids=[0])
    return result.results[0]["out_dram"]
```

```python
from contextlib import ExitStack

import numpy as np

import concourse.bass as bass
from concourse import mybir

P = 128
B = 2
S = 512
NT = S // P
C = 77
CP = 78
H = 8
HA = 16
HID = 512
NM = HID // P
NE = 8
NL = 4
LN_EPS = 1e-5
NORM_EPS = 1e-12
SCALE = P ** -0.5
BIG = 3e38
NEG = -1e30

F32 = mybir.dt.float32
F32R = mybir.dt.float32r
BF16 = mybir.dt.bfloat16
I32 = mybir.dt.int32
U32 = mybir.dt.uint32
ALU = mybir.AluOpType
ACT = mybir.ActivationFunctionType
AX = mybir.AxisListType.X


def offsets(parts):
    at, out = 0, {}
    for name, n in parts:
        out[name] = at
        at += n
    return out, at


COLS, N_COLS = offsets([
    ("norm_b", 1), ("gamma_media", 1), ("beta_media", 1), ("gamma_lat", 1), ("beta_lat", 1),
    ("X_bq", H), ("X_bv", H), ("F_b1m", NM), ("F_b2m", 1), ("D_bq", H), ("D_bk", 1), ("D_bv", 1),
    ("E_bq", 1), ("E_bk", 1)])
ROWS, N_ROWS = offsets([
    ("norm_g", P), ("A_b_out", P), ("X_bo", P), ("F_b_gate", NE), ("alpha", 1),
    ("E_bv", P), ("ln_gamma", P), ("ln_beta", P), ("M_bias", NE + NL)])
CONSTS, N_CONSTS = offsets([
    ("ident", P), ("blocks", 2 * P), ("head_sum", HA), ("causal", P), ("iota", NE), ("ones", 1), ("peT", S)])

LN_ORDER = ["A0", "A1", "X0", "X1", "F0", "F1", "D0", "D1", "E0", "M0", "E1", "M1"]
W_A_BIAS, W_A, W_X_BIAS = 1, 2, 3
W_F = W_X_BIAS + 1
W_E = W_F + 1
W_M = W_E + 1
READ_BY_LN = {"X": W_A, "D": W_F, "M": W_E}

F_UNITS = [(0, None), (0, 0), (0, 1), (1, None), (1, 0), (1, 1)]
F_CHUNKS = NM * len(F_UNITS)
MAIN = 2

def late_chain(b):
    return [[("stats", "E", b)], [("hat", "E", b)], [("turnx", "E", b)], [("E_q", b)], [("E_s", b)], [("E_exp", b)],
            [("E_t", b)], [("E_o", b)], [("E_ln", b)], [("stats", "M", b)], [("hat", "M", b)], [("turnx", "M", b)],
            [("split", "M", b), ("M_router", b)], [("M_lang", b)], [("M_best", b)], [("M_gates", b)], [("M_b2", b)]]


def new_x(stage, b):
    return [("turnx", stage, b), ("split", stage, b)]


def mix(*lists):
    out = []
    for n in range(max(map(len, lists))):
        for pieces in lists:
            if n < len(pieces):
                out += pieces[n] if isinstance(pieces[n], list) else [pieces[n]]
    return out


def chunks(first, end):
    return [("chunk", n) for n in range(first, end)]


def vall(kind, b):
    return [("vall", kind, b, n) for n in range(NT)]


X_HOOKS = {
    "prologue": [("F_main",)], "late": [*new_x("X", 1), ("keys", "X", 1), *vall("X", 1)],
    "mid": [("stats", "F", 0), ("hat", "F", 0)],
    "late1": [*new_x("F", 0), ("F_gate", 0)], "last": [("F_split", 0, 0), ("F_split", 0, 1)]}
D_HOOKS = {
    "prologue": [("F_out", 1), ("stats", "D", 1), ("hat", "D", 1)],
    "late": [*new_x("D", 1), ("keys", "D", 1), *vall("D", 1)],
    "mid": late_chain(0)[0],
    "steps": [a + b for a, b in zip(late_chain(0)[1:], [[("M_split", r, [part])] for r in range(4) for part in range(4)])]}
F_ITEMS = [
    ("stats", "F", 1), ("chunk", 0), ("hat", "F", 1), ("chunk", 1), *new_x("F", 1), ("chunk", 2), ("F_gate", 1),
    *chunks(3, 9), ("F_split", 1, 0), *chunks(9, 12), ("F_split", 1, 1), ("chunk", 12), ("F_out", 0),
    ("chunk", 13), ("stats", "D", 0), ("chunk", 14), ("hat", "D", 0), ("chunk", 15), *new_x("D", 0), ("chunk", 16),
    ("keys", "D", 0), *chunks(17, 19), *mix(vall("D", 0), chunks(19, 23)), ("chunk", 23)]
late_m, M_ITEMS = late_chain(1), []
for n in range(30):
    if n % 5 in (0, 2, 4) and late_m:
        M_ITEMS += late_m.pop(0)
    M_ITEMS.append(("chunk", n))
    if n % NM == 3 and n < 4 * NM:
        M_ITEMS.append(("M_split", 4 + n // NM))


def follow(do, items):
    for name, *args in items:
        if name in do:
            do[name](*args)


def build(nc, t):
    ctx = ExitStack()
    with ctx:
        def sb(name, shape, dt=F32):
            return ctx.enter_context(nc.sbuf_tensor(name, shape, dt))

        def sem(name):
            return ctx.enter_context(nc.semaphore(name))

        KB2 = 2048
        base = (nc.sbuf_base + 63) // 64 * 64
        V_AT, W_AT, H_AT = (0, 8 * KB2), 16 * KB2, 20 * KB2
        prob_bytes = (NT * (S + C) * 4 + 31) // 32 * 32
        sb("arena", [P, (64 + H_AT + 2 * prob_bytes + 5 * KB2) // 4])

        def at(name, shape, offset, dt=F32):
            return nc.alloc_sbuf_tensor_at(name, shape, dt, offset=base + offset)

        cols, rows, consts = sb("cols", [P, N_COLS]), sb("rows", [P, N_ROWS]), sb("consts", [P, N_CONSTS])
        x = [sb(f"x{b}", [P, NT, P]) for b in range(B)]
        ctx_tok, ctxT = sb("ctx_tok", [C, B, P]), sb("ctxT", [P, B, C])
        mask = sb("mask", [P, B, NT, C], I32)
        A_wqkvT, A_woutT = sb("A_wqkvT", [P, 3 * P]), sb("A_woutT", [P, P])
        X_WqT, X_WkT, X_WvT, X_Wo = (at(f"X_W{n}", [P, H, P], V_AT[1] + i * 2 * KB2)
                                     for i, n in enumerate(("qT", "kT", "vT", "o")))
        F_w_gate, F_W1m, F_W2m = sb("F_w_gate", [P, NE]), sb("F_W1m", [P, HID]), sb("F_W2m", [P, NM, P])
        F_W1e = [[at(f"F_W1e{b}{k}", [P, HID], V_AT[b] + 2 * k * KB2) for k in range(2)] for b in range(B)]
        F_W2e = [[at(f"F_W2e{b}{k}", [P, NM, P], V_AT[b] + (2 * k + 1) * KB2) for k in range(2)] for b in range(B)]
        F_b1e = [[sb(f"F_b1e{b}{k}", [P, NM]) for k in range(2)] for b in range(B)]
        F_b2e = sb("F_b2e", [P, B, 2])
        D_Wq, D_Wkv, D_Wo = sb("D_Wq", [P, H, P]), sb("D_Wkv", [P, 2 * P]), sb("D_Wo", [P, H, P])
        E_Wq, E_Wk, E_Wv = (sb(f"E_W{n}", [P, P]) for n in "qkv")
        M_w, M_b2 = sb("M_w", [P, NE + NL]), sb("M_b2", [NE, P])
        M_b1, M_b1g = sb("M_b1", [P, NE * NM]), [sb(f"M_b1g{k}", [P, NM]) for k in range(4)]
        M_w1 = [sb(f"M_w1{s}", [P, HID]) for s in range(2)]
        M_w2 = [sb(f"M_w2{s}", [P, NM, P]) for s in range(2)]

        def col(name, n=1, at=0):
            return cols[:, COLS[name] + at:COLS[name] + at + n]

        def row(name, n=P):
            return rows[:, ROWS[name]:ROWS[name] + n]

        def const(name, n):
            return consts[:, CONSTS[name]:CONSTS[name] + n]

        def flat(ap):
            return ap.rearrange("p a b -> p (a b)")

        def tiled(ap):
            return ap.rearrange("p (n d) -> p n d", d=P)

        ident = const("ident", P)

        bn, mv = sb("bn", [P, B, NT, 6]), sb("mv", [P, B, NT, 2])
        var_eps, rstd, rstd1 = (sb(n, [P, B, NT]) for n in ("var_eps", "rstd", "rstd1"))
        minus_half = sb("minus_half", [P, NT])
        xhat = [sb(f"xhat{b}", [P, NT, P]) for b in range(B)]
        xT = [sb(f"xT{b}", [P, S]) for b in range(B)]
        z_hi, z_lo = ([sb(f"z_{n}{b}", [P, S], F32R) for b in range(B)] for n in ("hi", "lo"))
        a_mask = sb("a_mask", [P, 2 * P])
        kv = [at(f"kv{b}", [P, NT * 2 * P], V_AT[0] + 2 * b * KB2) for b in range(B)]
        qT = [at(f"qT{b}", [P, S], V_AT[0] + (4 + b) * KB2) for b in range(B)]
        t1 = [at(f"t1{b}", [P, S], V_AT[0] + (6 + b) * KB2) for b in range(B)]
        gm = [sb(f"gm{b}", [P, 2 * P]) for b in range(B)]
        vsum = sb("vsum", [P, B])
        norm2, norm1, rnorm = (sb(n, [P, B, NT * HA]) for n in ("norm2", "norm1", "rnorm"))
        c_bn, c_mv, c_var = sb("c_bn", [C, B, 6]), sb("c_mv", [C, B, 2]), sb("c_var", [C, B])
        c_rstd, c_hat = sb("c_rstd", [C, B]), sb("c_hat", [C, B, P])
        czT = sb("czT", [P, B, C])
        cz_hi, cz_lo = (sb(f"cz_{n}", [P, B, CP], F32R) for n in ("hi", "lo"))
        X_A, X_V = (at(n, [P, H, P], W_AT + i * 2 * KB2) for i, n in enumerate(("X_A", "X_V")))
        X_r0, X_bias = sb("X_r0", [P, H]), sb("X_bias", [P, P])
        X_vc = sb("X_vc", [C, B, H * P])
        k_hi, k_lo = ([sb(f"k_{n}{b}", [P, S], F32R) for b in range(B)] for n in ("hi", "lo"))
        valuesT = [sb(f"valuesT{b}", [P, S]) for b in range(B)]
        vall = [at(f"vall{b}", [P, NT, H * P], V_AT[b]) for b in range(B)]
        w_hi, w_lo = ([sb(f"w_{n}{p}", [P, P], F32R) for p in range(2)] for n in ("hi", "lo"))
        w_full = [sb(f"w_full{p}", [P, P]) for p in range(2)]
        q_hi, q_lo = ([sb(f"q_{n}{p}", [P, S], F32R) for p in range(2)] for n in ("hi", "lo"))
        q_full = [sb(f"q_full{p}", [P, S]) for p in range(2)]
        probs = [at(f"probs{p}", [P, NT, S + C], H_AT + p * prob_bytes) for p in range(2)]
        pT = at("pT", [P, NT + 1, S], H_AT + 2 * prob_bytes)
        neg_cmax, neg_max = sb("neg_cmax", [P, 2, NT]), sb("neg_max", [P, 2, NT])
        sum_x, sum_c = sb("sum_x", [P, 2, NT]), sb("sum_c", [P, 2, NT])
        denom, rdenom = sb("denom", [P, 2, NT]), sb("rdenom", [P, 2, NT])
        ident_bf, causal_bf = sb("ident_bf", [P, P], BF16), sb("causal_bf", [P, P], BF16)
        w1_hi, w1_lo, w2_hi, w2_lo = (
            [sb(f"{n}{s}", [P, HID], F32R) for s in range(3)] + [at(f"{n}3", [P, HID], W_AT + k * KB2, F32R)]
            for k, n in enumerate(("w1_hi", "w1_lo", "w2_hi", "w2_lo")))
        h_full = [at(f"h_full{i}", [P, S], H_AT + i * KB2) for i in range(4)]
        h_hi = [at(f"h_hi{i}", [P, S], H_AT + (4 + i) * KB2, F32R) for i in range(4)]
        h_lo = [at(f"h_lo{i}", [P, S], H_AT + (8 + i) * KB2, F32R) for i in range(4)]
        yT = [sb(f"yT{b}", [P, S]) for b in range(B)]
        y_gated = [sb(f"y_gated{i}", [P, S]) for i in range(2)]
        xsum, mean_bc = sb("xsum", [P, B]), sb("mean_bc", [P, B, P])
        f_lg, f_max, f_idx = sb("f_lg", [P, B, NE]), sb("f_max", [P, B, 8]), sb("f_idx", [P, B, 8], U32)
        f_nmax, f_e, f_es = sb("f_nmax", [P, B]), sb("f_e", [P, B, 2]), sb("f_es", [P, B])
        f_ers, f_g = sb("f_ers", [P, B]), sb("f_g", [P, B, 2])
        f_a, f_1a = sb("f_a", [P, 1]), sb("f_1a", [P, 1])
        f_bias0, f_bias1, f_bias = sb("f_bias0", [P, 1]), sb("f_bias1", [P, B]), sb("f_bias", [P, B])
        e_lim = sb("e_lim", [P, B * NT * C])
        e_tmp = at("e_tmp", [P, B * NT * C], V_AT[1])
        e_kT, e_v = sb("e_kT", [P, B, C]), sb("e_v", [C, B, P])
        e_qT, e_o, e_on, e_og = ([at(f"{n}{b}", [P, NT, P], V_AT[b] + i * KB2) for b in range(B)]
                                 for i, n in enumerate(("e_qT", "e_o", "e_on", "e_og")))
        e_s, e_p = ([at(f"{n}{b}", [P, NT, C], V_AT[b] + (4 + i) * KB2) for b in range(B)]
                    for i, n in enumerate(("e_s", "e_p")))
        e_pT = [at(f"e_pT{b}", [C, S], V_AT[b] + 6 * KB2) for b in range(B)]
        e_nmax, e_sum, e_rsum = (sb(n, [P, B, NT]) for n in ("e_nmax", "e_sum", "e_rsum"))
        m_lg = [sb(f"m_lg{b}", [P, NT, NE + NL]) for b in range(B)]
        m_lmax = sb("m_lmax", [P, B, NT])
        m_ld, m_le = sb("m_ld", [P, B, NT, NL]), sb("m_le", [P, B, NT, NL])
        m_ls, m_lr = sb("m_ls", [P, B, NT]), sb("m_lr", [P, B, NT])
        m_lp, m_ew = sb("m_lp", [P, B, NT, NL + 1]), sb("m_ew", [P, B, NT, NL])
        m_rl = [sb(f"m_rl{b}", [P, NT, NE]) for b in range(B)]
        m_max, m_idx = sb("m_max", [P, B, NT, 8]), sb("m_idx", [P, B, NT, 8], U32)
        m_idxf = sb("m_idxf", [P, B, NT, 2])
        m_d, m_e = sb("m_d", [P, B, NT]), sb("m_e", [P, B, NT])
        m_s, m_g0, m_g1 = (sb(n, [P, B, NT]) for n in ("m_s", "m_g0", "m_g1"))
        m_oh, m_og = sb("m_oh", [P, B, 2, NT, NE]), sb("m_og", [P, B, 2, NT, NE])
        gates = [sb(f"gates{b}", [P, NT, NE]) for b in range(B)]
        gT = [sb(f"gT{b}", [NE, S]) for b in range(B)]
        gates_bc = at("gates_bc", [P, B * NE, S], V_AT[0])

        bank = [ctx.enter_context(nc.psum_tensor(f"bank{i}", [P, S], F32)) for i in range(8)]
        S_BANK, C_BANK, T_BANK, R_BANK, O_BANK = (0, 1), 2, (3, 4), 5, 7
        V_BANK = {"X": (5, 6), "D": (2, 6)}
        TR_BANK = {"A0": 0, "A1": 4, "X0": 6, "X1": 6, "F0": 6, "F1": 7, "D0": 6, "D1": 6, "E0": 6, "M0": 2,
                   "E1": 7, "M1": 5}
        EA, EB = (2, 5), (6, 7)
        Y_BANK = (3, 4)

        ld = {n: sem(f"ld_{n}") for n in (
            "consts", "cols", "rows", "x0", "x1", "ctx", "ctxT", "mask", "A_wqkvT", "A_woutT", "X_Wqk", "X_Wvo",
            "F_W", "D_W", "E_W", "M_W", "M_b1")}
        x_written = [sem(f"x_written{b}") for b in range(B)]
        (ln_bn, ln_stats, ln_eps, ln_r1, ln_rstd, ln_hat, ln_mm, ln_xT, z_hi_s, z_split) = (
            sem(n) for n in ("ln_bn", "ln_stats", "ln_eps", "ln_r1", "ln_rstd", "ln_hat", "ln_mm", "ln_xT", "z_hi",
                             "z_split"))
        fills, a_mask_ready, f_alpha = sem("fills"), sem("a_mask_ready"), sem("f_alpha")
        (a_q_mm, a_kv_mm, a_q, a_kv, a_g_mm, a_g, a_gq_mm, a_t1, a_n2_mm, a_n2, a_norm, a_rnorm, a_o_mm, a_o,
         a_oT_mm, a_oT, a_y_mm) = (sem("a_" + n) for n in (
             "q_mm", "kv_mm", "q", "kv", "g_mm", "g", "gq_mm", "t1", "n2_mm", "n2", "norm", "rnorm", "o_mm", "o",
             "oT_mm", "oT", "y_mm"))
        (c_bn_s, c_stats, c_eps, c_rstd_s, c_hat_s, c_mm, c_zT, c_hi_s, c_split) = (sem("c_" + n) for n in (
            "bn", "stats", "eps", "rstd", "hat", "mm", "zT", "hi", "split"))
        (w_a_mm, w_a, w_v_mm, w_v, w_b_mm, w_bias, w_vc_mm, w_vc) = (sem("w_" + n) for n in (
            "a_mm", "a", "v_mm", "v", "b_mm", "bias", "vc_mm", "vc"))
        bf_ready = sem("bf_ready")
        k_hi_s, keys_ready, d_k_mm, d_v_mm, d_v_ready, d_k_full = (sem(n) for n in (
            "k_hi", "keys_ready", "d_k_mm", "d_v_mm", "d_v_ready", "d_k_full"))
        vall_mm, vall_even, vall_odd = sem("vall_mm"), sem("vall_even"), sem("vall_odd")
        (w_hi_s, w_ready, r_mm, q_first, q_hi_s, q_ready, c_s_mm, s_mm, cmax_ready, max_ready, probs_ready, t_mm,
         pT_even, pT_odd, o_mm, o_added, denom_ready, rdenom_ready) = (sem(n) for n in (
             "w_hi", "w_ready", "r_mm", "q_first", "q_hi", "q_ready", "c_s_mm", "s_mm", "cmax_ready", "max_ready",
             "probs_ready", "t_mm", "pT_even", "pT_odd", "o_mm", "o_added", "denom_ready", "rdenom_ready"))
        h_mm, h_gelu, h_hi_even, h_hi_odd, h_split, y_mm = (sem(n) for n in (
            "h_mm", "h_gelu", "h_hi_even", "h_hi_odd", "h_split", "y_mm"))
        ws_hi, ws_ready = sem("ws_hi"), sem("ws_ready")
        y_gated_s, y_start, y_added = sem("y_gated"), sem("y_start"), sem("y_added")
        (f_mean, f_lg_mm, f_pick, f_idx_s, f_nmax_s, f_exp, f_w2,
         f_bias_s, f_yT, f_out_mm) = (sem("f_" + n) for n in (
             "mean", "lg_mm", "pick", "idx", "nmax", "exp", "w2",
             "bias", "yT", "out_mm"))
        f_ld = [[sem(f"f_ld{b}{k}") for k in range(2)] for b in range(B)]
        (e_lim_s, e_kv_mm, e_k_s, e_v_s, e_q_mm, e_q, e_s_mm, e_max, e_exp, e_t_mm, e_pT_s,
         e_o_mm, e_norm, e_st, e_eps, e_r) = (sem("e_" + n) for n in (
             "lim", "kv_mm", "k", "v", "q_mm", "q", "s_mm", "max", "exp", "t_mm", "pT",
             "o_mm", "norm", "st", "eps", "r"))
        (m_lg_mm, m_chain, m_lexp, m_exp, m_gates, m_gT_mm, m_gT, m_b_mm, m_out_mm) = (
            sem("m_" + n) for n in ("lg_mm", "chain", "lexp", "exp", "gates", "gT_mm", "gT", "b_mm",
                                    "out_mm"))
        m_raw, m_gates_bc = ([sem(f"m_{n}{i}") for i in range(2)] for n in ("raw", "gates_bc"))
        m_bias = [sem(f"m_bias{k}") for k in range(4)]
        m_gates_out = sem("m_gates_out")
        stored = sem("stored")

        def ln_index(stage, b):
            return LN_ORDER.index(f"{stage}{b}")

        def z_index(stage, b):
            return len([n for n in LN_ORDER[:ln_index(stage, b)] if n[0] not in "AE"])

        def v_index(kind, b):
            return (0 if kind == "X" else B) + b

        class Head:

            def __init__(self, kind, b, h, par):
                self.kind, self.b, self.h, self.par = kind, b, h, par
                self.g = (0 if kind == "X" else B * H) + b * H + h
                self.chunks = NT + 1 if kind == "X" else NT
                even, odd = (self.chunks + 1) // 2, self.chunks // 2
                self.very_first = kind == "X" and b == 0 and isinstance(h, int) and h == 0
                x_even, x_all = (NT + 2) // 2, NT + 1
                self.c0 = (0 if kind == "X" else B * H * x_all) + (b * H + h) * self.chunks
                self.even0 = (0 if kind == "X" else B * H * x_even) + (b * H + h) * even
                self.odd0 = self.g * odd

            def keys(self, i):
                return S if self.kind == "X" else (i + 1) * P

        ORDER = list(reversed(range(NT)))

        def run_attention(eng, do, kind, hooks, prologue, step):
            def head(b, h):
                if isinstance(h, int) and h >= H:
                    b, h = b + 1, h - H
                if b >= B:
                    return None
                return Head(kind, b, h, h % 2 if isinstance(h, int) else None)

            def heads(b, k):
                return head(b, k + 1), head(b, k), head(b, k + 2), head(b, k + 3)

            def run_step(*hs, between=()):
                middle, end = [*between, [], []][:2]
                step(*hs, lambda: follow(do, middle))
                follow(do, end)

            prologue(head(0, 0), head(0, 1), head(0, 2))
            follow(do, hooks["prologue"])
            for b in range(B):
                if b and "steps" in hooks:
                    for k in range(H):
                        run_step(*heads(b, k), between=hooks["steps"][2 * k:2 * k + 2])
                    continue
                with eng.Fori(0, H // 2 - 2) as i:
                    for s in range(2):
                        run_step(*(Head(kind, b, i * 2 + (s + d), (s + d) % 2) for d in (1, 0, 2, 3)))
                for k in range(H - 4, H):
                    if k == H - 2:
                        follow(do, hooks["late1" if b else "late"])
                    if k == H - 1 and b:
                        follow(do, hooks["last"])
                    run_step(*heads(b, k))
                if not b:
                    follow(do, hooks["mid"])

        GROUP, GROUP_CHUNKS = 4, 4 * NM
        GROUPS = B * NE // GROUP

        def m_at(i, n):
            return i * GROUP_CHUNKS + (F_CHUNKS + n)

        block = ctx.enter_context(nc.Block())

        @block.sync
        def _(sp):
            def load(dst, src, s):
                sp.dma_start(dst, src).then_inc(s, 16)

            load(x[0][:], t["x"][0].rearrange("(n p) d -> p n d", p=P), ld["x0"])
            load(x[1][:], t["x"][1].rearrange("(n p) d -> p n d", p=P), ld["x1"])
            load(consts[:], t["consts"], ld["consts"])
            load(A_wqkvT[:], t["A_wqkvT"], ld["A_wqkvT"])
            load(cols[:], t["cols"], ld["cols"])
            load(ctx_tok[:], t["ctx"].rearrange("b c d -> c b d"), ld["ctx"])
            load(rows[:], t["rows"].to_broadcast((P, N_ROWS)), ld["rows"])
            load(A_woutT[:], t["A_woutT"], ld["A_woutT"])
            load(X_WqT[:], t["X_WqT"].rearrange("(h k) d -> k h d", k=P), ld["X_Wqk"])
            load(X_WkT[:], t["X_WkvT"][0:H * P].rearrange("(h k) d -> k h d", k=P), ld["X_Wqk"])
            load(X_WvT[:], t["X_WkvT"][H * P:].rearrange("(h k) d -> k h d", k=P), ld["X_Wvo"])
            load(X_Wo[:], t["X_Wo"].rearrange("(h k) d -> k h d", k=P), ld["X_Wvo"])
            load(ctxT[:], t["ctxT"], ld["ctxT"])
            for w, n in ((E_Wq, "E_Wq"), (E_Wk, "E_Wk"), (E_Wv, "E_Wv")):
                load(w[:], t[n], ld["E_W"])
            load(mask[:], t["mask"].rearrange("b (n p) c -> p b n c", p=P), ld["mask"])
            load(F_w_gate[:], t["F_w_gate"], ld["F_W"])
            load(F_W1m[:], t["F_W1m"], ld["F_W"])
            load(F_W2m[:], t["F_W2m"].rearrange("(m p) d -> p m d", p=P), ld["F_W"])
            load(D_Wq[:], t["D_Wq"].rearrange("d (h k) -> d h k", k=P), ld["D_W"])
            load(D_Wkv[:], t["D_Wkv"], ld["D_W"])
            load(D_Wo[:], t["D_Wo"].rearrange("(h k) d -> k h d", k=P), ld["D_W"])
            load(M_w[:], t["M_w"], ld["M_W"])
            load(M_b2[:], t["M_b2"], ld["M_W"])

            def expert(e, s):
                load(M_w1[s][:], t["M_w1"][bass.ds(e, 1)].rearrange("e d h -> d (e h)"), m_raw[s])
                load(M_w2[s][:], t["M_w2"][bass.ds(e, 1)].rearrange("e (m p) d -> p (e m) d", p=P), m_raw[s])

            load(M_b1[:], t["M_b1T"], ld["M_b1"])
            for k in range(GROUP):
                load(M_b1g[k][:], t["M_b1T"][:, (GROUP + k) * NM:(GROUP + k + 1) * NM], m_bias[k])
            for e in range(2):
                expert(e, e)

            for b in range(B):
                sp.wait_ge(f_idx_s, b + 1)
                sp.wait_ge(o_added, H * (b + 1))
                for k in range(2):
                    e = sp.value_load(f_idx[0:1, b, k:k + 1], min_val=0, max_val=NE - 1)
                    load(F_W1e[b][k][:], t["F_W1e"][bass.ds(e, 1)].rearrange("e d h -> d (e h)"), f_ld[b][k])
                    load(F_W2e[b][k][:], t["F_W2e"][bass.ds(e, 1)].rearrange("e (m p) d -> p (e m) d", p=P),
                         f_ld[b][k])
                    load(F_b1e[b][k][:], t["F_b1eT"][:, bass.ds(e * NM, NM)], f_ld[b][k])
                    load(F_b2e[:, b, k:k + 1], t["F_b2e"][bass.ds(e, 1)].rearrange("e d -> d e"), f_ld[b][k])

            def spread_gates(b):
                sp.wait_ge(m_gT, b + 1)
                sp.dma_start(t["gates"][b], gT[b][:]).then_inc(m_gates_out, 16)
                sp.wait_ge(m_gates_out, 16 * (b + 1))
                for e in range(NE):
                    load(gates_bc[:, b * NE + e, :], t["gates"][b, e:e + 1, :].to_broadcast((P, S)), m_gates_bc[b])

            def next_expert(r, e):
                sp.wait_ge(ws_ready, r + (len(F_UNITS) - 2))
                expert(e, r % 2)

            for e in range(2, 4):
                next_expert(e, e)
            spread_gates(0)
            for e in range(4, NE):
                next_expert(e, e)
            spread_gates(1)
            for e in range(GROUP):
                next_expert(NE + e, e)
            for k in range(GROUP):
                sp.wait_ge(h_gelu, m_at(2, NM * (k + 1)))
                load(M_b1g[k][:], t["M_b1T"][:, k * NM:(k + 1) * NM], m_bias[k])

            for b in range(B):
                sp.wait_ge(x_written[b], W_M)
                sp.dma_start(t["out"][b].rearrange("(n p) d -> p n d", p=P), x[b][:]).then_inc(stored, 16)
            sp.wait_ge(stored, 16 * B)

        @block.gpsimd
        def _(pool):
            g = nc.gpsimd
            g.memset(minus_half[:], -0.5).then_inc(fills, 1)
            g.memset(m_lp[:], 0.0).then_inc(fills, 1)
            pool.wait_ge(fills, 1)

            def norm(stage, b):
                n = ln_index(stage, b)
                var = mv[:, b, :, 1]
                pool.wait_ge(ln_stats, n + 1)
                g.tensor_scalar(var_eps[:, b], var, LN_EPS, 1.0, ALU.add, ALU.mult).then_inc(ln_eps, 1)
                pool.wait_ge(ln_eps, n + 1)
                if stage != "X":
                    g.tensor_tensor(rstd[:, b], var_eps[:, b], minus_half[:], ALU.pow).then_inc(ln_rstd, 1)
                    return
                g.tensor_tensor(rstd1[:, b], var_eps[:, b], minus_half[:], ALU.pow).then_inc(ln_r1, 1)
                pool.wait_ge(ln_r1, 5 * b + 1)
                g.tensor_tensor(rstd[:, b], var, rstd1[:, b], ALU.mult).then_inc(ln_r1, 1)
                pool.wait_ge(ln_r1, 5 * b + 2)
                g.tensor_tensor(var_eps[:, b], rstd[:, b], rstd1[:, b], ALU.mult).then_inc(ln_r1, 1)
                pool.wait_ge(ln_r1, 5 * b + 3)
                g.tensor_scalar(var_eps[:, b], var_eps[:, b], LN_EPS, 1.0, ALU.add, ALU.mult).then_inc(ln_r1, 1)
                pool.wait_ge(ln_r1, 5 * b + 4)
                g.tensor_tensor(rstd[:, b], var_eps[:, b], minus_half[:], ALU.pow).then_inc(ln_r1, 1)
                pool.wait_ge(ln_r1, 5 * b + 5)
                g.tensor_tensor(rstd[:, b], rstd[:, b], rstd1[:, b], ALU.mult).then_inc(ln_rstd, 1)

            def add_row(b, r, stage):
                pool.wait_ge(ln_hat, ln_index(stage, b) + 1)
                g.tensor_tensor(x[b][:], x[b][:], r.unsqueeze(1).to_broadcast((P, NT, P)),
                                ALU.add).then_inc(x_written[b], 1)

            def split_w(hd):
                w = (X_A if hd.kind == "X" else D_Wq)[:, bass.ds(hd.h, 1), :].rearrange("p a k -> p (a k)")
                p = hd.par
                if not (hd.kind == "X" and hd.b == 0 and isinstance(hd.h, int) and hd.h < 2):
                    pool.wait_ge(w_ready, hd.g - 1)
                g.tensor_copy(w_full[p][:], w).then_inc(w_hi_s, 1)
                pool.wait_ge(w_hi_s, hd.g * 2 + 1)
                if not (hd.kind == "X" and hd.b == 0 and isinstance(hd.h, int) and hd.h < 2):
                    pool.wait_ge(r_mm, hd.g - 1)
                g.tensor_tensor(w_hi[p][:], w_full[p][:], const("ones", 1).to_broadcast((P, P)),
                                ALU.mult).then_inc(w_hi_s, 1)
                pool.wait_ge(w_hi_s, hd.g * 2 + 2)
                g.tensor_tensor(w_lo[p][:], w_full[p][:], w_hi[p][:], ALU.subtract).then_inc(w_ready, 1)

            def split_q(hd):
                if hd.kind == "D":
                    p = hd.par
                    pool.wait_ge(q_hi_s, hd.g + 1)
                    g.tensor_tensor(q_lo[p][:], q_full[p][:], q_hi[p][:], ALU.subtract).then_inc(q_ready, 1)

            def prologue(h0, h1, h2):
                split_w(h0)
                split_w(h1)
                split_q(h0)
                split_w(h2)
                split_q(h1)

            def step(hs, ht, hn, hw, middle):
                if hw:
                    split_w(hw)
                middle()
                if hn:
                    split_q(hn)

            ws_done = [0, 0]

            def split_mlp(w1, w2, slot):
                g.tensor_tensor(w1_hi[slot][:], w1, const("ones", 1).to_broadcast((P, HID)), ALU.mult).then_inc(ws_hi, 1)
                g.tensor_scalar(w2_hi[slot][:], w2, 1.0, 1.0, ALU.mult, ALU.mult).then_inc(ws_hi, 1)
                return [(w1, w1_hi, w1_lo), (w2, w2_hi, w2_lo)]

            def split_mlp_lo(parts, slot, his, ready=None):
                for n, (w, hi, lo) in enumerate(parts):
                    pool.wait_ge(ws_hi, his + n + 1)
                    last = g.tensor_tensor(lo[slot][:], w, hi[slot][:], ALU.subtract)
                last.then_inc(ws_ready, 1)

            def f_split(b, k):
                pool.wait_ge(f_w2, 2 + 2 * b + k)
                if b:
                    pool.wait_ge(y_mm, NM * (2 + k))
                n = 1 + 2 * b + k
                split_mlp_lo(split_mlp(F_W1e[b][k][:], flat(F_W2e[b][k][:]), k), k, 2 * n)

            def m_split(r, parts=range(4)):
                slot = r % 4
                w1, w2 = M_w1[r % 2][:], flat(M_w2[r % 2][:])
                for part in parts:
                    m_split_part(r, slot, w1, w2, part)

            def m_split_part(r, slot, w1, w2, part):
                if part == 1:
                    g.tensor_scalar(w2_hi[slot][:], w2, 1.0, 1.0, ALU.mult, ALU.mult).then_inc(ws_hi, 1)
                elif part == 2:
                    pool.wait_ge(ws_hi, 2 * (5 + r) + 1)
                    g.tensor_tensor(w1_lo[slot][:], w1, w1_hi[slot][:], ALU.subtract)
                elif part == 3:
                    pool.wait_ge(ws_hi, 2 * (5 + r) + 2)
                    g.tensor_tensor(w2_lo[slot][:], w2, w2_hi[slot][:], ALU.subtract).then_inc(ws_ready, 1)
                if part:
                    return
                pool.wait_ge(y_mm, NM * ((5, 6, 4, 4)[r] if r < 4 else m_at(0, 0) // NM + (r - 3 if r < NE else r + 1)))
                pool.wait_ge(m_raw[r % 2], 32 * (r // 2 + 1))
                g.tensor_tensor(w1_hi[slot][:], w1, const("ones", 1).to_broadcast((P, HID)),
                                ALU.mult).then_inc(ws_hi, 1)

            def add_gated(u):
                b = u // NE
                pool.wait_ge(y_gated_s, u + 1)
                pool.wait_ge(y_start, b + 1)
                if u:
                    pool.wait_ge(y_added, u)
                g.tensor_tensor(yT[b][:], yT[b][:], y_gated[u % 2][:], ALU.add).then_inc(y_added, 1)

            def f_gate(b):
                pool.wait_ge(ln_xT, ln_index("F", b) + 1)
                g.tensor_scalar(mean_bc[:, b, :], xsum[:, b:b + 1].to_broadcast((P, P)), 1.0 / S, 1.0,
                                ALU.mult, ALU.mult).then_inc(f_mean, 1)

            def e_o_piece(b):
                pool.wait_ge(e_st, b + 1)
                g.tensor_scalar(var_eps[:, b], mv[:, b, :, 1], LN_EPS, 1.0, ALU.add, ALU.mult).then_inc(e_eps, 1)
                pool.wait_ge(e_eps, b + 1)
                g.tensor_tensor(rstd[:, b], var_eps[:, b], minus_half[:], ALU.pow).then_inc(e_r, 1)

            do = {"stats": norm, "F_gate": f_gate, "F_split": f_split, "M_split": m_split, "E_o": e_o_piece}

            norm("A", 0)
            norm("A", 1)
            pool.wait_ge(ld["rows"], 16)
            for b in range(B):
                add_row(b, row("A_b_out"), "A")
            pool.wait_ge(c_stats, 1)
            g.tensor_scalar(c_var[:], c_mv[:, :, 1], LN_EPS, 1.0, ALU.add, ALU.mult).then_inc(c_eps, 1)
            pool.wait_ge(c_eps, 1)
            g.tensor_tensor(c_rstd[:], c_var[:], minus_half[0:C, 0:B], ALU.pow).then_inc(c_rstd_s, 1)
            pool.wait_ge(ld["consts"], 16)
            g.tensor_copy(ident_bf[:], ident).then_inc(bf_ready, 1)
            g.tensor_copy(causal_bf[:], const("causal", P)).then_inc(bf_ready, 1)
            norm("X", 0)
            norm("X", 1)
            pool.wait_ge(w_bias, 2)
            for b in range(B):
                add_row(b, X_bias[:], "X")
            pool.wait_ge(w_a, 2)
            def f_main():
                pool.wait_ge(ld["F_W"], 3 * 16)
                pool.wait_ge(f_w2, 1)
                split_mlp_lo(split_mlp(F_W1m[:], flat(F_W2m[:]), MAIN), MAIN, 0)

            do["F_main"] = f_main
            run_attention(pool, do, "X", X_HOOKS, prologue, step)
            follow(do, F_ITEMS)
            pool.wait_ge(ld["D_W"], 3 * 16)
            run_attention(pool, do, "D", D_HOOKS, prologue, step)

            def m_chunk(n):
                if n >= NM and n % NM == 2:
                    add_gated(n // NM - 1)

            do["chunk"] = m_chunk
            follow(do, M_ITEMS)
            add_gated(NE - 2)
            for u in range(NE, B * NE):
                add_gated(u - 1)
                if u < NE + GROUP:
                    m_split(u)
            add_gated(B * NE - 1)

        @block.scalar
        def _(act):
            a = nc.scalar

            def turnx(stage, b):
                act.wait_ge(ln_mm, ln_index(stage, b) + 1)
                src = bank[TR_BANK[f"{stage}{b}"]][:]
                if stage == "X":
                    a.activation(xT[b][:], src, ACT.Identity, scale=col("gamma_lat"),
                                 bias=col("beta_lat")).then_inc(ln_xT, 1)
                elif stage == "F":
                    a.activation(xT[b][:], src, ACT.Copy, accum_out=xsum[:, b:b + 1]).then_inc(ln_xT, 1)
                else:
                    a.copy(xT[b][:], src).then_inc(ln_xT, 1)

            def keys(kind, b):
                if kind == "D":
                    act.wait_ge(d_v_mm, b + 1)
                    a.activation(valuesT[b][:], bank[6][:], ACT.Identity, bias=col("D_bv")).then_inc(d_v_ready, 1)

            def vall_piece(kind, b, i):
                act.wait_ge(vall_mm, 2 * NT * v_index(kind, b) + 2 * i + 1)
                a.copy(vall[b][:, i, 0:S], bank[V_BANK[kind][0]][:]).then_inc(vall_even, 1)

            def f_gate(b):
                act.wait_ge(f_nmax_s, b + 1)
                a.activation(f_e[:, b, :], f_max[:, b, 0:2], ACT.Exp, bias=f_nmax[:, b:b + 1],
                             accum_out=f_es[:, b:b + 1]).then_inc(f_exp, 1)

            def gelu(n, func, bias):
                k, g = n
                act.wait_ge(h_mm, g + 1)
                if not (isinstance(g, int) and g < 4):
                    act.wait_ge(h_split, g - 3)
                a.activation(h_full[k % 4][:], bank[k % 2][:], func, bias=bias).then_inc(h_gelu, 1)

            def gelu_hi(n):
                k, g = n
                act.wait_ge(h_gelu, g + 1)
                if not (isinstance(g, int) and g < 4):
                    act.wait_ge(y_mm, g - 3)
                a.copy(h_hi[k % 4][:], h_full[k % 4][:]).then_inc(h_hi_even, 1)

            def f_gelu(n):
                if n >= F_CHUNKS:
                    return
                b, k = F_UNITS[n // NM]
                m = n % NM
                if k is None:
                    bias = col("F_b1m", 1, m)
                else:
                    if m == 0:
                        act.wait_ge(f_ld[b][k], 4 * 16)
                    bias = F_b1e[b][k][:, m:m + 1]
                gelu((n, n), ACT.Gelu_apprx_tanh, bias)
                if n % 2 == 0:
                    gelu_hi((n, n))

            def f_out(b):
                act.wait_ge(y_mm, NM * 3 * (b + 1))
                act.wait_ge(f_bias_s, 2 * b + 2)
                a.activation(yT[b][:], bank[Y_BANK[b]][:], ACT.Identity, bias=f_bias[:, b:b + 1]).then_inc(f_yT, 1)

            def e_q_piece(b):
                act.wait_ge(e_q_mm, b + 1)
                a.activation(flat(e_qT[b][:]), bank[EA[b]][:], ACT.Identity, bias=col("E_bq")).then_inc(e_q, 1)

            def e_exp_piece(b):
                act.wait_ge(e_max, b + 1)
                for i in range(NT):
                    last = a.activation(e_p[b][:, i, :], e_s[b][:, i, :], ACT.Exp, bias=e_nmax[:, b, i:i + 1],
                                        accum_out=e_sum[:, b, i:i + 1])
                last.then_inc(e_exp, 1)

            def e_t_piece(b):
                act.wait_ge(e_t_mm, b + 1)
                a.copy(e_pT[b][:], bank[EA[b]][0:C, :]).then_inc(e_pT_s, 1)

            def m_lang(b):
                act.wait_ge(m_chain, M_CHAIN * b + 3)
                a.activation(m_le[:, b], m_ld[:, b], ACT.Exp).then_inc(m_lexp, 1)

            def m_best(b):
                act.wait_ge(m_chain, M_CHAIN * b + M_CHAIN_D)
                a.activation(m_e[:, b], m_d[:, b], ACT.Exp).then_inc(m_exp, 1)

            def m_gates_piece(b):
                act.wait_ge(m_gT_mm, b + 1)
                a.copy(gT[b][:], bank[EA[b]][0:NE, :]).then_inc(m_gT, 1)

            def m_b2(b):
                act.wait_ge(m_b_mm, b + 1)
                a.copy(yT[b][:], bank[EB[b]][:]).then_inc(y_start, 1)

            do = {"turnx": turnx, "keys": keys, "vall": vall_piece, "F_gate": f_gate, "F_out": f_out,
                  "chunk": lambda n: f_gelu(n + 2), "E_q": e_q_piece, "E_exp": e_exp_piece, "E_t": e_t_piece, "M_lang": m_lang, "M_best": m_best,
                  "M_gates": m_gates_piece, "M_b2": m_b2}

            for b in range(B):
                turnx("A", b)
                act.wait_ge(a_q_mm, b + 1)
                a.copy(qT[b][:], bank[4 * b + 1][:]).then_inc(a_q, 1)
            for b in range(B):
                act.wait_ge(a_n2, b + 1)
                a.activation(norm1[:, b], norm2[:, b], ACT.Sqrt).then_inc(a_norm, 1)
            for b in range(B):
                act.wait_ge(a_oT_mm, b + 1)
                act.wait_ge(a_g, B)
                a.activation(t1[b][:], bank[4 * b][:], ACT.Identity, bias=vsum[:, b:b + 1]).then_inc(a_oT, 1)
            act.wait_ge(ld["cols"], 16)
            act.wait_ge(c_mm, 1)
            a.activation(flat(czT[:]), bank[2][:, 0:B * C], ACT.Identity,
                         scale=col("gamma_media"), bias=col("beta_media")).then_inc(c_zT, 1)
            act.wait_ge(w_a_mm, 1)
            a.copy(flat(X_A[:, 0:4, :]), bank[0][:]).then_inc(w_a, 1)
            act.wait_ge(w_v_mm, 1)
            a.copy(flat(X_V[:, 0:4, :]), bank[2][:]).then_inc(w_v, 1)
            turnx("X", 0)
            for i in range(NT):
                vall_piece("X", 0, i)

            def e_tile(hd, j):
                i, p, n = ORDER[j], hd.par, hd.keys(ORDER[j])
                act.wait_ge(max_ready, hd.g * NT + j + 1)
                last = a.activation(probs[p][:, i, 0:n], bank[S_BANK[i % 2]][:, 0:n], ACT.Exp,
                                    bias=neg_max[:, p, i:i + 1], scale=-1.0, accum_out=sum_x[:, p, i:i + 1])
                if hd.kind == "X":
                    last = a.activation(probs[p][:, i, S:S + C], bank[C_BANK][:, i * CP:i * CP + C], ACT.Exp,
                                        bias=neg_max[:, p, i:i + 1], accum_out=sum_c[:, p, i:i + 1])
                last.then_inc(probs_ready, 1)

            def t_copy(hd, c):
                act.wait_ge(t_mm, hd.c0 + c + 1)
                k = C if c == NT else P
                lo = 0 if hd.kind == "X" else c * P
                a.copy(pT[0:k, c, lo:S], bank[T_BANK[0]][0:k, lo:S]).then_inc(pT_even, 1)

            def prologue(h0, h1, h2):
                for j in range(NT):
                    e_tile(h0, j)

            def step(hs, ht, hn, hw, middle):
                t_copy(ht, 0)
                if hs:
                    e_tile(hs, 0)
                t_copy(ht, 2)
                if hs:
                    e_tile(hs, 1)
                middle()
                if hs:
                    e_tile(hs, 2)
                if ht.chunks > 4:
                    t_copy(ht, 4)
                if hs:
                    e_tile(hs, 3)

            run_attention(act, do, "X", X_HOOKS, prologue, step)
            f_gelu(0)
            f_gelu(1)
            follow(do, F_ITEMS)
            run_attention(act, do, "D", D_HOOKS, prologue, step)

            def m_gelu(i, n):
                g, m = m_at(i, n), n % NM
                if isinstance(i, int):
                    bias = M_b1[:, n:n + 1]
                else:
                    k = n // NM
                    bias = M_b1g[k][:, m:m + 1]
                    if m == 0:
                        act.wait_ge(m_bias[k], i * 16 - 16)
                gelu((n, g), ACT.Gelu, bias)
                if n % 2 == 0:
                    gelu_hi((n, g))

            act.wait_ge(ld["M_b1"], 16)
            do["chunk"] = lambda n: m_gelu(0, n + 2)
            m_gelu(0, 0)
            m_gelu(0, 1)
            follow(do, M_ITEMS)
            with act.Fori(2, GROUPS) as i:
                for n in range(GROUP_CHUNKS):
                    m_gelu(i, n)

        @block.vector
        def _(dve):
            v = nc.vector

            def ln_stats_of(stage, b):
                n = ln_index(stage, b)
                if stage == "A":
                    dve.wait_ge(ld[f"x{b}"], 16)
                elif stage in READ_BY_LN:
                    dve.wait_ge(x_written[b], READ_BY_LN[stage])
                else:
                    dve.wait_ge(o_added, (B * H if stage == "E" else 0) + H * (b + 1))
                for i in range(NT):
                    last = v.bn_stats(bn[:, b, i, :], x[b][:, i, :])
                last.then_inc(ln_bn, 1)
                dve.wait_ge(ln_bn, n + 1)
                for i in range(NT):
                    last = v.bn_aggr(mv[:, b, i, :], bn[:, b, i, :])
                last.then_inc(ln_stats, 1)

            def ln_hat_of(stage, b):
                dve.wait_ge(ln_rstd, ln_index(stage, b) + 1)
                for i in range(NT):
                    last = v.tensor_scalar(xhat[b][:, i, :], x[b][:, i, :], mv[:, b, i, 0:1], rstd[:, b, i:i + 1],
                                           ALU.subtract, ALU.mult)
                last.then_inc(ln_hat, 1)

            def split_z(stage, b):
                n = z_index(stage, b)
                dve.wait_ge(ln_xT, ln_index(stage, b) + 1)
                v.tensor_copy(z_hi[b][:], xT[b][:]).then_inc(z_hi_s, 1)
                dve.wait_ge(z_hi_s, n + 1)
                v.tensor_tensor(z_lo[b][:], xT[b][:], z_hi[b][:], ALU.subtract).then_inc(z_split, 1)

            def keys(kind, b):
                n = v_index(kind, b)
                full = xT[b][:]
                if kind == "D":
                    full = flat(xhat[b][:])
                    dve.wait_ge(d_k_mm, b + 1)
                    v.scalar_tensor_tensor(full, bank[2][:], col("D_bk"), const("peT", S), ALU.add,
                                           ALU.add).then_inc(d_k_full, 1)
                    dve.wait_ge(d_k_full, b + 1)
                v.tensor_scalar(k_hi[b][:], full, SCALE, None, ALU.mult).then_inc(k_hi_s, 1)
                dve.wait_ge(k_hi_s, n + 1)
                v.scalar_tensor_tensor(k_lo[b][:], full, SCALE, k_hi[b][:], ALU.mult,
                                       ALU.subtract).then_inc(keys_ready, 1)

            def vall_piece(kind, b, i):
                dve.wait_ge(vall_mm, 2 * NT * v_index(kind, b) + 2 * i + 2)
                v.tensor_copy(vall[b][:, i, S:2 * S], bank[V_BANK[kind][1]][:]).then_inc(vall_odd, 1)

            def f_gate(b):
                dve.wait_ge(f_lg_mm, b + 1)
                v.tensor_tensor(f_lg[:, b], bank[TR_BANK[f"F{b}"]][:, 0:NE], row("F_b_gate", NE),
                                ALU.add).then_inc(f_pick, 1)
                dve.wait_ge(f_pick, 4 * b + 1)
                v.max(f_max[:, b], f_lg[:, b]).then_inc(f_pick, 1)
                dve.wait_ge(f_pick, 4 * b + 2)
                v.max_index(f_idx[:, b], f_max[:, b], f_lg[:, b]).then_inc(f_idx_s, 1)
                v.tensor_scalar(f_nmax[:, b:b + 1], f_max[:, b, 0:1], -1.0, None, ALU.mult).then_inc(f_nmax_s, 1)

            def f_split(b, k):
                if k == 0:
                    dve.wait_ge(f_exp, b + 1)
                    v.reciprocal(f_ers[:, b:b + 1], f_es[:, b:b + 1]).then_inc(f_pick, 1)
                    dve.wait_ge(f_pick, 4 * b + 3)
                    v.tensor_scalar(f_g[:, b, :], f_e[:, b, :], f_ers[:, b:b + 1], f_1a[:], ALU.mult,
                                    ALU.mult).then_inc(f_pick, 1)
                    dve.wait_ge(f_pick, 4 * b + 4)
                dve.wait_ge(f_ld[b][k], 4 * 16)
                v.tensor_scalar(F_W2e[b][k][:], F_W2e[b][k][:], f_g[:, b, k:k + 1], None, ALU.mult).then_inc(f_w2, 1)
                if k == 0:
                    v.scalar_tensor_tensor(f_bias1[:, b:b + 1], F_b2e[:, b, 0:1], f_g[:, b, 0:1], f_bias0[:],
                                           ALU.mult, ALU.add).then_inc(f_bias_s, 1)
                else:
                    dve.wait_ge(f_bias_s, 2 * b + 1)
                    v.scalar_tensor_tensor(f_bias[:, b:b + 1], F_b2e[:, b, 1:2], f_g[:, b, 1:2],
                                           f_bias1[:, b:b + 1], ALU.mult, ALU.add).then_inc(f_bias_s, 1)

            def split_h(k, g, pairs):
                slot = k % 4
                if k % 2:
                    dve.wait_ge(h_gelu, g + 1)
                    if not (isinstance(g, int) and g < 4):
                        dve.wait_ge(y_mm, g - 3)
                    v.tensor_copy(h_hi[slot][:], h_full[slot][:]).then_inc(h_hi_odd, 1)
                elif not (isinstance(g, int) and g < 4):
                    dve.wait_ge(y_mm, g - 3)
                dve.wait_ge(h_hi_odd if k % 2 else h_hi_even, pairs + 1)
                v.tensor_tensor(h_lo[slot][:], h_full[slot][:], h_hi[slot][:], ALU.subtract).then_inc(h_split, 1)

            def f_split_h(n):
                if n < F_CHUNKS:
                    split_h(n, n, n // 2)

            def f_out(b):
                dve.wait_ge(f_out_mm, b + 1)
                v.tensor_tensor(x[b][:], tiled(bank[5 + b][:]), x[b][:], ALU.add).then_inc(x_written[b], 1)

            def e_s_piece(b):
                dve.wait_ge(e_s_mm, b + 1)
                v.tensor_tensor(flat(e_s[b][:]), bank[EB[b]][:, 0:NT * C],
                                e_lim[:, b * NT * C:(b + 1) * NT * C], ALU.min).then_inc(e_norm, 1)
                dve.wait_ge(e_norm, 7 * b + 1)
                v.tensor_reduce(e_nmax[:, b], e_s[b][:], AX, ALU.max, negate=True).then_inc(e_max, 1)

            def e_o_piece(b):
                dve.wait_ge(e_exp, b + 1)
                v.reciprocal(e_rsum[:, b], e_sum[:, b]).then_inc(e_norm, 1)
                dve.wait_ge(e_norm, 7 * b + 2)
                dve.wait_ge(e_o_mm, b + 1)
                for i in range(NT):
                    last = v.tensor_scalar(e_o[b][:, i, :], bank[EB[b]][:, i * P:(i + 1) * P],
                                           e_rsum[:, b, i:i + 1], None, ALU.mult)
                last.then_inc(e_norm, 1)
                dve.wait_ge(e_norm, 7 * b + 3)
                for i in range(NT):
                    last = v.bn_stats(bn[:, b, i, :], e_o[b][:, i, :])
                last.then_inc(e_norm, 1)
                dve.wait_ge(e_norm, 7 * b + 4)
                for i in range(NT):
                    last = v.bn_aggr(mv[:, b, i, :], bn[:, b, i, :])
                last.then_inc(e_st, 1)

            def e_ln_piece(b):
                dve.wait_ge(e_r, b + 1)
                for i in range(NT):
                    last = v.tensor_scalar(e_on[b][:, i, :], e_o[b][:, i, :], mv[:, b, i, 0:1], rstd[:, b, i:i + 1],
                                           ALU.subtract, ALU.mult)
                last.then_inc(e_norm, 1)
                dve.wait_ge(e_norm, 7 * b + 5)
                v.tensor_tensor(e_og[b][:], e_on[b][:], row("ln_gamma").unsqueeze(1).to_broadcast((P, NT, P)),
                                ALU.mult).then_inc(e_norm, 1)
                dve.wait_ge(e_norm, 7 * b + 6)
                v.tensor_tensor(e_on[b][:], e_og[b][:], row("ln_beta").unsqueeze(1).to_broadcast((P, NT, P)),
                                ALU.add).then_inc(e_norm, 1)
                dve.wait_ge(e_norm, 7 * b + 7)
                v.tensor_tensor(x[b][:], e_on[b][:], x[b][:], ALU.add).then_inc(x_written[b], 1)

            done = [0]

            def then(ins):
                done[0] += 1
                ins.then_inc(m_chain, 1)
                dve.wait_ge(m_chain, done[0])

            def m_router(b):
                tiles = (P, NT, NL)
                lang = m_lg[b][:, :, NE:NE + NL]
                dve.wait_ge(m_lg_mm, b + 1)
                then(v.tensor_tensor(m_lg[b][:],
                                     bank[EB[b]][:, 0:NT * (NE + NL)].rearrange("p (n e) -> p n e", n=NT),
                                     row("M_bias", NE + NL).unsqueeze(1).to_broadcast((P, NT, NE + NL)), ALU.add))
                then(v.tensor_reduce(m_lmax[:, b], lang, AX, ALU.max))
                then(v.tensor_tensor(m_ld[:, b], lang, m_lmax[:, b].unsqueeze(2).to_broadcast(tiles), ALU.subtract))

            def m_lang(b):
                tiles = (P, NT, NL)
                dve.wait_ge(m_lexp, b + 1)
                then(v.tensor_reduce(m_ls[:, b], m_le[:, b], AX, ALU.add))
                then(v.reciprocal(m_lr[:, b], m_ls[:, b]))
                then(v.tensor_tensor(m_lp[:, b, :, 0:NL], m_le[:, b], m_lr[:, b].unsqueeze(2).to_broadcast(tiles),
                                     ALU.mult))
                then(v.tensor_tensor(m_ew[:, b], m_lp[:, b, :, 0:NL], m_lp[:, b, :, 1:NL + 1], ALU.add))
                v.scalar_tensor_tensor(m_rl[b][:, :, 0:NL], m_ew[:, b], 0.1, m_lg[b][:, :, 0:NL], ALU.mult, ALU.add)
                then(v.scalar_tensor_tensor(m_rl[b][:, :, NL:NE], m_ew[:, b], 0.1, m_lg[b][:, :, NL:NE], ALU.mult,
                                            ALU.add))
                for i in range(NT):
                    last = v.max(m_max[:, b, i, :], m_rl[b][:, i, :])
                then(last)
                for i in range(NT):
                    last = v.max_index(m_idx[:, b, i, :], m_max[:, b, i, :], m_rl[b][:, i, :])
                then(last)
                then(v.tensor_tensor(m_d[:, b], m_max[:, b, :, 1], m_max[:, b, :, 0], ALU.subtract))
                assert done[0] == M_CHAIN * b + M_CHAIN_D

            def m_best(b):
                then(v.tensor_copy(m_idxf[:, b], m_idx[:, b, :, 0:2]))
                dve.wait_ge(m_exp, b + 1)
                then(v.tensor_scalar(m_s[:, b], m_e[:, b], 1.0, None, ALU.add))
                then(v.reciprocal(m_g0[:, b], m_s[:, b]))
                then(v.tensor_tensor(m_g1[:, b], m_g0[:, b], m_e[:, b], ALU.mult))
                for k, gk in enumerate((m_g0, m_g1)):
                    then(v.tensor_tensor(m_oh[:, b, k], const("iota", NE).unsqueeze(1).to_broadcast((P, NT, NE)),
                                         m_idxf[:, b, :, k:k + 1].to_broadcast((P, NT, NE)), ALU.is_equal))
                    then(v.tensor_tensor(m_og[:, b, k], m_oh[:, b, k],
                                         gk[:, b].unsqueeze(2).to_broadcast((P, NT, NE)), ALU.mult))
                assert done[0] == M_CHAIN * (b + 1)
                v.tensor_tensor(gates[b][:], m_og[:, b, 0], m_og[:, b, 1], ALU.add).then_inc(m_gates, 1)

            do = {"stats": ln_stats_of, "hat": ln_hat_of, "split": split_z, "keys": keys, "vall": vall_piece, "F_gate": f_gate,
                  "F_split": f_split, "chunk": lambda n: f_split_h(n + 1), "F_out": f_out, "E_s": e_s_piece,
                  "E_o": e_o_piece, "E_ln": e_ln_piece, "M_router": m_router, "M_lang": m_lang, "M_best": m_best}

            ln_stats_of("A", 0)
            ln_stats_of("A", 1)
            ln_hat_of("A", 0)
            ln_hat_of("A", 1)
            dve.wait_ge(ld["consts"], 16)
            dve.wait_ge(ld["rows"], 16)
            v.tensor_copy(a_mask[:, 0:P], const("blocks", P)).then_inc(a_mask_ready, 1)
            v.tensor_tensor(a_mask[:, P:2 * P], const("blocks", P), row("norm_g"), ALU.mult).then_inc(a_mask_ready, 1)
            dve.wait_ge(a_mask_ready, 2)
            dve.wait_ge(ld["cols"], 16)
            for b in range(B):
                dve.wait_ge(a_kv_mm, b + 1)
                v.tensor_copy(kv[b][:, 0:S], bank[4 * b + 2][:])
                v.tensor_copy(kv[b][:, S:2 * S], bank[4 * b + 3][:]).then_inc(a_kv, 1)
            for b in range(B):
                dve.wait_ge(a_g_mm, b + 1)
                v.tensor_tensor(gm[b][:], bank[4 * b][:, 0:2 * P], a_mask[:], ALU.mult)
                v.tensor_tensor(vsum[:, b:b + 1], bank[4 * b][:, 2 * P:2 * P + 1], col("norm_b"),
                                ALU.mult).then_inc(a_g, 1)
            for b in range(B):
                dve.wait_ge(a_gq_mm, b + 1)
                dve.wait_ge(a_q, b + 1)
                v.tensor_tensor(t1[b][:], bank[4 * b + 1][:], qT[b][:], ALU.mult).then_inc(a_t1, 1)
            for b in range(B):
                dve.wait_ge(a_n2_mm, b + 1)
                v.tensor_scalar(norm2[:, b], bank[4 * b + 2][:, 0:NT * HA], NORM_EPS ** 2, None,
                                ALU.max).then_inc(a_n2, 1)
            dve.wait_ge(ld["ctx"], 16)
            for b in range(B):
                last = v.bn_stats(c_bn[:, b, :], ctx_tok[:, b, :])
            last.then_inc(c_bn_s, 1)
            dve.wait_ge(c_bn_s, 1)
            for b in range(B):
                last = v.bn_aggr(c_mv[:, b, :], c_bn[:, b, :])
            last.then_inc(c_stats, 1)
            for b in range(B):
                dve.wait_ge(a_norm, b + 1)
                v.reciprocal(rnorm[:, b], norm1[:, b]).then_inc(a_rnorm, 1)
                dve.wait_ge(a_rnorm, b + 1)
                dve.wait_ge(a_o_mm, b + 1)
                heads = "p (g e) -> p g e"
                v.tensor_tensor(kv[b][:, 0:S].rearrange(heads, e=P // HA),
                                bank[4 * b + 3][:].rearrange(heads, e=P // HA),
                                rnorm[:, b].unsqueeze(2).to_broadcast((P, NT * HA, P // HA)),
                                ALU.mult).then_inc(a_o, 1)
            dve.wait_ge(c_rstd_s, 1)
            for b in range(B):
                last = v.tensor_scalar(c_hat[:, b, :], ctx_tok[:, b, :], c_mv[:, b, 0:1], c_rstd[:, b:b + 1],
                                       ALU.subtract, ALU.mult)
            last.then_inc(c_hat_s, 1)
            for b in range(B):
                dve.wait_ge(a_y_mm, b + 1)
                dve.wait_ge(x_written[b], W_A_BIAS)
                v.tensor_tensor(x[b][:], tiled(bank[4 * b + 1][:]), x[b][:], ALU.add).then_inc(x_written[b], 1)
            for b in range(B):
                ln_stats_of("X", b)
            dve.wait_ge(c_zT, 1)
            for parts in (cz_hi, cz_lo):
                v.tensor_copy(parts[:, :, C:CP], czT[:, :, 0:CP - C])
            dve.wait_ge(fills, 2)
            v.tensor_scalar(cz_hi[:, :, 0:C], czT[:], SCALE, None, ALU.mult).then_inc(c_hi_s, 1)
            dve.wait_ge(c_hi_s, 1)
            v.scalar_tensor_tensor(cz_lo[:, :, 0:C], czT[:], SCALE, cz_hi[:, :, 0:C], ALU.mult,
                                   ALU.subtract).then_inc(c_split, 1)
            dve.wait_ge(w_a_mm, 2)
            v.tensor_copy(flat(X_A[:, 4:8, :]), bank[1][:]).then_inc(w_a, 1)
            dve.wait_ge(w_v_mm, 2)
            v.tensor_copy(flat(X_V[:, 4:8, :]), bank[3][:]).then_inc(w_v, 1)
            dve.wait_ge(w_b_mm, 1)
            v.tensor_copy(X_r0[:], bank[5][:, 2 * P:2 * P + H]).then_inc(w_bias, 1)
            v.tensor_tensor(X_bias[:], bank[4][:, 0:P], row("X_bo"), ALU.add).then_inc(w_bias, 1)
            for b in range(B):
                ln_hat_of("X", b)
            split_z("X", 0)
            keys("X", 0)
            for b in range(B):
                dve.wait_ge(w_vc_mm, b + 1)
                for half in range(2):
                    last = v.tensor_copy(X_vc[:, b, half * S:(half + 1) * S], bank[2 * b + half][0:C, :])
                last.then_inc(w_vc, 1)
            for i in range(NT):
                vall_piece("X", 0, i)
            dve.wait_ge(e_kv_mm, 1)
            v.tensor_scalar(flat(e_kT[:]), bank[4][:, 0:B * C], col("E_bk"), SCALE, ALU.add, ALU.mult).then_inc(e_k_s, 1)
            v.tensor_tensor(e_v[:], bank[4][0:C, 2 * P:4 * P].rearrange("c (b d) -> c b d", b=B),
                            rows[0:C, ROWS["E_bv"]:ROWS["E_bv"] + P].unsqueeze(1).to_broadcast((C, B, P)),
                            ALU.add).then_inc(e_v_s, 1)

            def limits_and_alpha():
                dve.wait_ge(ld["mask"], 16)
                v.tensor_scalar(e_tmp[:], mask[:].rearrange("p b n c -> p (b n c)"), 0.0, -2.0, ALU.is_equal,
                                ALU.mult).then_inc(e_lim_s, 1)
                dve.wait_ge(e_lim_s, 1)
                v.tensor_scalar(e_lim[:], e_tmp[:], 1.0, BIG, ALU.add, ALU.mult).then_inc(e_lim_s, 1)
                v.tensor_scalar(f_a[:], row("alpha", 1), 0.1, 1.0, ALU.max, ALU.min).then_inc(f_alpha, 1)
                dve.wait_ge(f_alpha, 1)
                v.tensor_scalar(f_1a[:], f_a[:], -1.0, 1.0, ALU.mult, ALU.add).then_inc(f_alpha, 1)
                dve.wait_ge(ld["F_W"], 3 * 16)
                v.tensor_scalar(F_W2m[:], F_W2m[:], f_a[:], None, ALU.mult).then_inc(f_w2, 1)
                v.tensor_tensor(f_bias0[:], col("F_b2m"), f_a[:], ALU.mult).then_inc(f_alpha, 1)
                dve.wait_ge(f_alpha, 3)

            def q_copy(hd):
                p = hd.par
                dve.wait_ge(r_mm, hd.g + 1)
                src = bank[R_BANK][:]
                if hd.kind == "X":
                    r0 = X_r0[:, bass.ds(hd.h, 1)]
                    v.tensor_scalar(q_hi[p][:], src, r0, None, ALU.add).then_inc(q_hi_s, 1)
                    dve.wait_ge(q_hi_s, hd.g + 1)
                    v.scalar_tensor_tensor(q_lo[p][:], src, r0, q_hi[p][:], ALU.add, ALU.subtract).then_inc(q_ready, 1)
                else:
                    if not (isinstance(hd.h, int) and hd.b == 0 and hd.h < 2):
                        dve.wait_ge(q_ready, hd.g - 1)
                    v.scalar_tensor_tensor(q_full[p][:], src, cols[:, bass.ds(hd.h + COLS["D_bq"], 1)],
                                           const("peT", S), ALU.add, ALU.add).then_inc(q_first, 1)
                    dve.wait_ge(q_first, hd.g - B * H + 1)
                    dve.wait_ge(s_mm, (hd.g - 1) * NT)
                    v.tensor_copy(q_hi[p][:], q_full[p][:]).then_inc(q_hi_s, 1)

            def c_max(hd):
                if hd.kind == "X":
                    dve.wait_ge(c_s_mm, hd.g + 1)
                    v.tensor_reduce(neg_cmax[:, hd.par, :],
                                    bank[C_BANK][:, 0:NT * CP].rearrange("p (n c) -> p n c", c=CP)[:, :, 0:C],
                                    AX, ALU.max, negate=True).then_inc(cmax_ready, 1)
                    dve.wait_ge(cmax_ready, hd.g + 1)

            def x_max(hd, j):
                i, n = ORDER[j], hd.keys(ORDER[j])
                dve.wait_ge(s_mm, hd.g * NT + j + 1)
                scores = bank[S_BANK[i % 2]][:, 0:n]
                v.tensor_scalar(scores, scores, -1.0, neg_cmax[:, hd.par, i:i + 1] if hd.kind == "X" else None,
                                ALU.mult, ALU.min, accum_out=neg_max[:, hd.par, i:i + 1]).then_inc(max_ready, 1)

            def t_copy(hd, c):
                dve.wait_ge(t_mm, hd.c0 + c + 1)
                lo = 0 if hd.kind == "X" else c * P
                v.tensor_copy(pT[:, c, lo:S], bank[T_BANK[1]][:, lo:S]).then_inc(pT_odd, 1)

            def add_head(hd):
                p = hd.par
                dve.wait_ge(probs_ready, (hd.g + 1) * NT)
                if hd.kind == "X":
                    v.tensor_tensor(denom[:, p], sum_x[:, p], sum_c[:, p], ALU.add).then_inc(denom_ready, 1)
                    dve.wait_ge(denom_ready, hd.g + 1)
                    v.reciprocal(rdenom[:, p], denom[:, p]).then_inc(rdenom_ready, 1)
                else:
                    v.reciprocal(rdenom[:, p], sum_x[:, p]).then_inc(rdenom_ready, 1)
                dve.wait_ge(rdenom_ready, hd.g + 1)
                dve.wait_ge(o_mm, hd.g + 1)
                dve.wait_ge(x_written[hd.b], W_X_BIAS if hd.kind == "X" else W_F)
                if not hd.very_first:
                    dve.wait_ge(o_added, hd.g)
                for i in range(NT):
                    last = v.scalar_tensor_tensor(x[hd.b][:, i, :], bank[O_BANK][:, i * P:(i + 1) * P],
                                                  rdenom[:, p, i:i + 1], x[hd.b][:, i, :], ALU.mult, ALU.add)
                last.then_inc(o_added, 1)

            def prologue(h0, h1, h2):
                q_copy(h0)
                c_max(h0)
                for j in range(NT):
                    x_max(h0, j)
                q_copy(h1)
                if h0.kind == "X":
                    limits_and_alpha()

            def step(hs, ht, hn, hw, middle):
                if hs:
                    c_max(hs)
                    x_max(hs, 0)
                t_copy(ht, 1)
                if hs:
                    x_max(hs, 1)
                if hn:
                    q_copy(hn)
                middle()
                if hs:
                    x_max(hs, 2)
                t_copy(ht, 3)
                if hs:
                    x_max(hs, 3)
                add_head(ht)

            run_attention(dve, do, "X", X_HOOKS, prologue, step)
            f_split_h(0)
            follow(do, F_ITEMS)
            run_attention(dve, do, "D", D_HOOKS, prologue, step)

            def gate_unit(i, u):
                if isinstance(i, int):
                    b, gate = u // NE, gates_bc[:, u, :]
                else:
                    b, row_ = 1, i * 8 - 9 if u < 0 else i * -4 + (20 + u)
                    gate = gates_bc[:, bass.ds(row_, 1), :].rearrange("p e s -> p (e s)")
                dve.wait_ge(m_gates_bc[b], 16 * NE)
                dve.wait_ge(y_mm, m_at(i, NM * (u + 1)))
                if not (isinstance(i, int) and u < 2):
                    dve.wait_ge(y_added, i * 4 + (u - 1))
                v.tensor_tensor(y_gated[u % 2][:], bank[Y_BANK[u % 2]][:], gate, ALU.mult).then_inc(y_gated_s, 1)

            def m_split_h(i, n):
                split_h(n, m_at(i, n), i * (GROUP_CHUNKS // 2) + (F_CHUNKS + n) // 2)
                if n % NM == 1 and not (isinstance(i, int) and n < NM):
                    gate_unit(i, n // NM - 1)

            def store_batch(b):
                dve.wait_ge(m_out_mm, b + 1)
                v.tensor_tensor(x[b][:], tiled(bank[5 + b][:]), x[b][:], ALU.add).then_inc(x_written[b], 1)

            do["chunk"] = lambda n: m_split_h(0, n + 1)
            m_split_h(0, 0)
            follow(do, M_ITEMS)
            m_split_h(0, 31)
            with dve.Fori(2, GROUPS) as i:
                for n in range(GROUP_CHUNKS):
                    m_split_h(i, n)
            dve.wait_ge(y_mm, m_at(GROUPS, 0))
            dve.wait_ge(y_added, B * NE - 2)
            v.tensor_tensor(y_gated[1][:], bank[Y_BANK[1]][:], gates_bc[:, NE + GROUP - 1, :],
                            ALU.mult).then_inc(y_gated_s, 1)
            for b in range(B):
                store_batch(b)

        @block.tensor
        def _(pe):
            def mm(out, lhsT, rhs, start=True, stop=True):
                return nc.tensor.matmul(out, lhsT, rhs, start=start, stop=stop, skip_group_check=True)

            def mm3(out, l_hi, l_lo, r_hi, r_lo, start=True, stop=True):
                mm(out, l_hi, r_hi, start, False)
                mm(out, l_hi, r_lo, False, False)
                return mm(out, l_lo, r_hi, False, stop)

            def tile_of(bk, i, n=P):
                return bank[bk][:, i * n:(i + 1) * n]

            def turnx(stage, b):
                pe.wait_ge(ln_hat, ln_index(stage, b) + 1)
                for i in range(NT):
                    last = nc.tensor.transpose(tile_of(TR_BANK[f"{stage}{b}"], i), xhat[b][:, i, :], ident)
                last.then_inc(ln_mm, 1)

            def keys(kind, b):
                if kind == "D":
                    pe.wait_ge(ln_xT, ln_index("D", b) + 1)
                    mm(bank[2][:], D_Wkv[:, 0:P], xT[b][:]).then_inc(d_k_mm, 1)
                    mm(bank[6][:], D_Wkv[:, P:2 * P], xT[b][:]).then_inc(d_v_mm, 1)

            def vall_piece(kind, b, i):
                n0 = v_index(kind, b)
                w = X_V if kind == "X" else D_Wo
                if i == 0 and kind == "X":
                    pe.wait_ge(ln_xT, ln_index("X", b) + 1)
                    if b:
                        pe.wait_ge(q_ready, H)
                elif i == 0:
                    pe.wait_ge(d_v_ready, b + 1)
                    pe.wait_ge(d_k_full, b + 1)
                src = xT[b] if kind == "X" else valuesT[b]
                for half in range(2):
                    if i:
                        pe.wait_ge((vall_even, vall_odd)[half], NT * n0 + i)
                    mm(bank[V_BANK[kind][half]][:], src[:, i * P:(i + 1) * P],
                       flat(w[:, 4 * half:4 * half + 4, :])).then_inc(vall_mm, 1)
                if i == NT - 1:
                    pe.wait_ge(vall_even, NT * (n0 + 1))
                    pe.wait_ge(vall_odd, NT * (n0 + 1))

            def f_gate(b):
                pe.wait_ge(f_mean, b + 1)
                mm(bank[TR_BANK[f"F{b}"]][:, 0:NE], mean_bc[:, b, :], F_w_gate[:]).then_inc(f_lg_mm, 1)

            def hidden(k, g, slot, b, m):
                if not (isinstance(g, int) and g < 2):
                    pe.wait_ge(h_gelu, g - 1)
                w = slice(m * P, (m + 1) * P)
                mm3(bank[k % 2][:], w1_hi[slot][:, w], w1_lo[slot][:, w], z_hi[b][:], z_lo[b][:]).then_inc(h_mm, 1)

            def output(k, g, slot, bk, m, start, stop):
                pe.wait_ge(h_split, g + 1)
                w = slice(m * P, (m + 1) * P)
                mm3(bank[bk][:], w2_hi[slot][:, w], w2_lo[slot][:, w], h_hi[k % 4][:], h_lo[k % 4][:], start,
                    stop).then_inc(y_mm, 1)

            def f_hidden(n):
                u = n // NM
                b, k = F_UNITS[u]
                if n % NM == 0:
                    if k is None:
                        pe.wait_ge(z_split, z_index("F", b) + 1)
                    pe.wait_ge(ws_ready, {None: 1}.get(k, 2 + 2 * b + (k or 0)))
                hidden(n, n, MAIN if k is None else k, b, n % NM)

            def f_chunk(n):
                if n + 2 < F_CHUNKS:
                    f_hidden(n + 2)
                b, k = F_UNITS[n // NM]
                output(n, n, MAIN if k is None else k, Y_BANK[b], n % NM, k is None and n % NM == 0,
                       k == 1 and n % NM == NM - 1)

            def turn_y(b, bk, s):
                for i in range(NT):
                    last = nc.tensor.transpose(tile_of(bk, i), yT[b][:, i * P:(i + 1) * P], ident)
                last.then_inc(s, 1)

            def f_out(b):
                pe.wait_ge(f_yT, b + 1)
                turn_y(b, 5 + b, f_out_mm)

            def e_q_piece(b):
                pe.wait_ge(ln_xT, ln_index("E", b) + 1)
                mm(bank[EA[b]][:], E_Wq[:], xT[b][:]).then_inc(e_q_mm, 1)

            def e_s_piece(b):
                pe.wait_ge(e_q, b + 1)
                for i in range(NT):
                    last = mm(bank[EB[b]][:, i * C:(i + 1) * C], e_qT[b][:, i, :], e_kT[:, b, :])
                last.then_inc(e_s_mm, 1)

            def e_t_piece(b):
                pe.wait_ge(e_exp, b + 1)
                for i in range(NT):
                    last = nc.tensor.transpose(bank[EA[b]][0:C, i * P:(i + 1) * P], e_p[b][:, i, :], ident)
                last.then_inc(e_t_mm, 1)

            def e_o_piece(b):
                pe.wait_ge(e_pT_s, b + 1)
                for i in range(NT):
                    last = mm(tile_of(EB[b], i), e_pT[b][:, i * P:(i + 1) * P], e_v[:, b, :])
                last.then_inc(e_o_mm, 1)

            def m_router(b):
                pe.wait_ge(ln_xT, ln_index("M", b) + 1)
                for i in range(NT):
                    last = mm(tile_of(EB[b], i, NE + NL), xT[b][:, i * P:(i + 1) * P], M_w[:])
                last.then_inc(m_lg_mm, 1)

            def m_gates_piece(b):
                pe.wait_ge(m_gates, b + 1)
                for i in range(NT):
                    last = nc.tensor.transpose(bank[EA[b]][0:NE, i * P:(i + 1) * P], gates[b][:, i, :], ident)
                last.then_inc(m_gT_mm, 1)

            def m_b2(b):
                pe.wait_ge(m_gT, b + 1)
                mm(bank[EB[b]][:], M_b2[:], gT[b][:]).then_inc(m_b_mm, 1)

            do = {"turnx": turnx, "keys": keys, "vall": vall_piece, "F_gate": f_gate, "chunk": f_chunk, "F_out": f_out,
                  "E_q": e_q_piece, "E_s": e_s_piece, "E_t": e_t_piece, "E_o": e_o_piece, "M_router": m_router,
                  "M_gates": m_gates_piece, "M_b2": m_b2}

            pe.wait_ge(ld["consts"], 16)
            pe.wait_ge(ld["A_wqkvT"], 16)
            for b in range(B):
                turnx("A", b)
            for b in range(B):
                k = 4 * b
                pe.wait_ge(ln_xT, b + 1)
                mm(bank[k + 1][:], A_wqkvT[:, 0:P], xT[b][:]).then_inc(a_q_mm, 1)
                for i in range(NT):
                    last = mm(bank[k + 2 + i // 2][:, (i % 2) * 2 * P:(i % 2 + 1) * 2 * P],
                              xT[b][:, i * P:(i + 1) * P], A_wqkvT[:, P:3 * P])
                last.then_inc(a_kv_mm, 1)
            for b in range(B):
                pe.wait_ge(a_kv, b + 1)
                k4 = kv[b][:].rearrange("p (n w) -> p n w", n=NT)
                for i in range(NT):
                    mm(bank[4 * b][:, 0:2 * P], k4[:, i, 0:P], k4[:, i, :], i == 0, i == NT - 1)
                for i in range(NT):
                    last = mm(bank[4 * b][:, 2 * P:2 * P + 1], k4[:, i, P:2 * P], const("ones", 1), False, i == NT - 1)
                last.then_inc(a_g_mm, 1)
            for b in range(B):
                pe.wait_ge(a_g, b + 1)
                pe.wait_ge(a_q, b + 1)
                mm(bank[4 * b + 1][:], gm[b][:, 0:P], qT[b][:]).then_inc(a_gq_mm, 1)
                for i in range(NT):
                    last = mm(tile_of(4 * b + 3, i), qT[b][:, i * P:(i + 1) * P], gm[b][:, P:2 * P])
                last.then_inc(a_o_mm, 1)
            for b in range(B):
                pe.wait_ge(a_t1, b + 1)
                for i in range(NT):
                    last = mm(tile_of(4 * b + 2, i, HA), t1[b][:, i * P:(i + 1) * P], const("head_sum", HA))
                last.then_inc(a_n2_mm, 1)
            for b in range(B):
                pe.wait_ge(a_o, b + 1)
                for i in range(NT):
                    last = nc.tensor.transpose(tile_of(4 * b, i), kv[b][:, i * P:(i + 1) * P], ident)
                last.then_inc(a_oT_mm, 1)
            pe.wait_ge(ld["A_woutT"], 16)
            for b in range(B):
                pe.wait_ge(a_oT, b + 1)
                for i in range(NT):
                    last = mm(tile_of(4 * b + 1, i), t1[b][:, i * P:(i + 1) * P], A_woutT[:])
                last.then_inc(a_y_mm, 1)
            pe.wait_ge(c_hat_s, 1)
            for b in range(B):
                last = nc.tensor.transpose(bank[2][:, b * C:(b + 1) * C], c_hat[:, b, :], ident[0:C, 0:C])
            last.then_inc(c_mm, 1)
            pe.wait_ge(ld["cols"], 16)
            pe.wait_ge(ld["X_Wqk"], 2 * 16)
            pe.wait_ge(ld["X_Wvo"], 2 * 16)
            for b in range(B):
                pe.wait_ge(x_written[b], W_A)
            for h in range(H):
                last = mm(tile_of(h // 4, h % 4), X_WqT[:, h, :], X_WkT[:, h, :])
                if h % 4 == 3:
                    last.then_inc(w_a_mm, 1)
            pe.wait_ge(c_zT, 1)
            for h in range(H):
                last = mm(tile_of(2 + h // 4, h % 4), X_WvT[:, h, :], X_Wo[:, h, :])
                if h % 4 == 3:
                    last.then_inc(w_v_mm, 1)
            for h in range(H):
                mm(bank[5][:, 2 * P + h:2 * P + h + 1], X_WkT[:, h, :], col("X_bq", 1, h))
            for h in range(H):
                last = mm(bank[4][:, 0:P], col("X_bv", 1, h).to_broadcast((P, P)), X_Wo[:, h, :], h == 0, h == H - 1)
            last.then_inc(w_b_mm, 1)
            turnx("X", 0)
            pe.wait_ge(c_split, 1)
            pe.wait_ge(w_v, 2)
            pe.wait_ge(w_a, 2)
            for b in range(B):
                for half in range(2):
                    last = mm(bank[2 * b + half][0:C, :], czT[:, b, :], flat(X_V[:, 4 * half:4 * half + 4, :]))
                last.then_inc(w_vc_mm, 1)
            pe.wait_ge(w_bias, 2)
            for i in range(NT):
                vall_piece("X", 0, i)
            pe.wait_ge(ld["ctxT"], 16)
            pe.wait_ge(ld["E_W"], 3 * 16)
            mm(bank[4][:, 0:B * C], E_Wk[:], flat(ctxT[:]))
            for b in range(B):
                last = mm(bank[4][0:C, (2 + b) * P:(3 + b) * P], ctxT[:, b, :], E_Wv[:])
            last.then_inc(e_kv_mm, 1)

            def queries(hd):
                pe.wait_ge(w_ready, hd.g + 1)
                if hd.kind == "X":
                    if not hd.very_first:
                        pe.wait_ge(q_ready, hd.g)
                elif not (isinstance(hd.h, int) and hd.h == 0 and hd.b == 0):
                    pe.wait_ge(q_first, hd.g - B * H)
                mm3(bank[R_BANK][:], w_hi[hd.par][:], w_lo[hd.par][:], z_hi[hd.b][:], z_lo[hd.b][:]).then_inc(r_mm, 1)

            def scores_c(hd):
                pe.wait_ge(q_ready, hd.g + 1)
                if hd.kind == "X":
                    if not hd.very_first:
                        pe.wait_ge(probs_ready, hd.g * NT)
                    for i in range(NT):
                        w = slice(i * P, (i + 1) * P)
                        last = mm3(bank[C_BANK][:, i * CP:(i + 1) * CP], q_hi[hd.par][:, w], q_lo[hd.par][:, w],
                                   cz_hi[:, hd.b, :], cz_lo[:, hd.b, :])
                    last.then_inc(c_s_mm, 1)

            def scores(hd, j):
                i, n = ORDER[j], hd.keys(ORDER[j])
                if not (hd.very_first and j < 2):
                    pe.wait_ge(probs_ready, hd.g * NT + j - 1)
                dst, w, b = bank[S_BANK[i % 2]], slice(i * P, (i + 1) * P), hd.b
                last = mm3(dst[:, 0:n], q_hi[hd.par][:, w], q_lo[hd.par][:, w], k_hi[b][:, 0:n], k_lo[b][:, 0:n],
                           True, hd.kind == "X")
                if hd.kind == "D":
                    last = mm(dst[:, n - P:n], ident_bf[:], causal_bf[:], False, True)
                last.then_inc(s_mm, 1)

            def turn(hd, c):
                if c == 0:
                    pe.wait_ge(probs_ready, (hd.g + 1) * NT)
                if c % 2 == 0:
                    if not (hd.very_first and c == 0):
                        pe.wait_ge(pT_even, hd.even0 + c // 2)
                elif not (hd.very_first and c == 1):
                    pe.wait_ge(pT_odd, hd.odd0 + c // 2)
                k = C if c == NT else P
                for i in range(0 if hd.kind == "X" else c, NT):
                    last = nc.tensor.transpose(bank[T_BANK[c % 2]][0:k, i * P:(i + 1) * P],
                                               probs[hd.par][:, i, c * P:c * P + k], ident)
                last.then_inc(t_mm, 1)

            def weigh(hd, c):
                if c % 2 == 0:
                    pe.wait_ge(pT_even, hd.even0 + c // 2 + 1)
                else:
                    pe.wait_ge(pT_odd, hd.odd0 + c // 2 + 1)
                if c == 0 and not hd.very_first:
                    pe.wait_ge(o_added, hd.g)
                for i in range(0 if hd.kind == "X" else c, NT):
                    if c == NT:
                        l, r = pT[0:C, c, i * P:(i + 1) * P], X_vc[:, hd.b, bass.ds(hd.h * P, P)]
                    else:
                        l, r = pT[:, c, i * P:(i + 1) * P], vall[hd.b][:, c, bass.ds(hd.h * P, P)]
                    last = mm(tile_of(O_BANK, i), l, r, c == 0 and i == 0, c == hd.chunks - 1)
                if c == hd.chunks - 1:
                    last.then_inc(o_mm, 1)

            def prologue(h0, h1, h2):
                pe.wait_ge(z_split, z_index(h0.kind, 0) + 1)
                pe.wait_ge(keys_ready, v_index(h0.kind, 0) + 1)
                queries(h0)
                scores_c(h0)
                for j in range(NT):
                    scores(h0, j)
                queries(h1)

            def step(hs, ht, hn, hw, middle):
                turn(ht, 0)
                if hs:
                    scores_c(hs)
                    scores(hs, 0)
                turn(ht, 1)
                weigh(ht, 0)
                if hs:
                    scores(hs, 1)
                if hn:
                    if isinstance(hn.h, int) and hn.h == 0:
                        pe.wait_ge(z_split, z_index(hn.kind, hn.b) + 1)
                        pe.wait_ge(keys_ready, v_index(hn.kind, hn.b) + 1)
                    queries(hn)
                middle()
                turn(ht, 2)
                weigh(ht, 1)
                if hs:
                    scores(hs, 2)
                turn(ht, 3)
                weigh(ht, 2)
                if hs:
                    scores(hs, 3)
                if ht.chunks > NT:
                    turn(ht, NT)
                weigh(ht, 3)
                if ht.chunks > NT:
                    weigh(ht, NT)

            pe.wait_ge(w_vc, B)
            pe.wait_ge(e_v_s, 1)
            run_attention(pe, do, "X", X_HOOKS, prologue, step)
            pe.wait_ge(ld["F_W"], 3 * 16)
            pe.wait_ge(ld["D_W"], 3 * 16)
            pe.wait_ge(ld["M_W"], 2 * 16)
            f_hidden(0)
            f_hidden(1)
            follow(do, F_ITEMS)
            pe.wait_ge(bf_ready, 2)
            run_attention(pe, do, "D", D_HOOKS, prologue, step)

            def m_hidden(i, n):
                k = n // NM
                b = 0 if isinstance(i, int) else 1
                if n % NM == 0:
                    pe.wait_ge(ws_ready, i * 4 + (len(F_UNITS) + k) if b == 0 else i * 4 + (len(F_UNITS) - 4 + k))
                    if n == 0:
                        pe.wait_ge(z_split, z_index("M", b) + 1)
                hidden(n, m_at(i, n), k % 4, b, n % NM)

            def m_output(i, n):
                u = n // NM
                if n % NM == 0 and not (isinstance(i, int) and u < 2):
                    pe.wait_ge(y_gated_s, i * 4 + (u - 1))
                output(n, m_at(i, n), u % 4, Y_BANK[u % 2], n % NM, n % NM == 0, n % NM == NM - 1)

            def store_batch(b):
                pe.wait_ge(y_added, NE * (b + 1))
                turn_y(b, 5 + b, m_out_mm)

            do["chunk"] = lambda n: (m_hidden(0, n + 2), m_output(0, n))
            m_hidden(0, 0)
            m_hidden(0, 1)
            follow(do, M_ITEMS)
            with pe.Fori(2, GROUPS) as i:
                for n in range(GROUP_CHUNKS):
                    m_hidden(i, n)
                    m_output(i, n - 2)
            for n in (-2, -1):
                m_output(GROUPS, n)
            for b in range(B):
                store_batch(b)


M_CHAIN = 19
M_CHAIN_D = 11


def positions():
    pos = np.arange(S, dtype=np.float32)[:, None]
    inv_freq = np.exp(np.float32(-np.log(10000.0)) * np.arange(0, P, 2, dtype=np.float32) / np.float32(P))
    ang = (pos * inv_freq[None, :]).astype(np.float32)
    pe = np.zeros((S, P), np.float32)
    pe[:, 0::2] = np.sin(ang)
    pe[:, 1::2] = np.cos(ang)
    return pe.T


def constants():
    p = np.arange(P)
    blocks = (p[:, None] // (P // HA) == p[None, :] // (P // HA)).astype(np.float32)
    parts = {
        "ident": np.eye(P), "blocks": np.concatenate([blocks, blocks], 1),
        "head_sum": p[:, None] // (P // HA) == np.arange(HA)[None, :],
        "causal": np.where(p[None, :] <= p[:, None], 0.0, NEG),
        "iota": np.broadcast_to(np.arange(NE), (P, NE)), "ones": np.ones((P, 1)), "peT": positions()}
    return np.concatenate([np.asarray(parts[n], np.float32) for n in CONSTS], 1)


def kernel(**inputs):
    import concourse.bacc as bacc
    from concourse.bass_utils import run_bass_kernel_spmd

    w = {n: np.asarray(a) for n, a in inputs.items()}

    def as_cols(v):
        return np.reshape(v, (-1, P)).T

    per_head = P // HA
    bkv = w["L0_xattn_bkv"]
    cols = {
        "norm_b": np.repeat(w["L0_attn_norm_b"].reshape(HA), per_head),
        "gamma_media": w["L0_xattn_gamma_media"], "beta_media": w["L0_xattn_beta_media"],
        "gamma_lat": w["L0_xattn_gamma_lat"], "beta_lat": w["L0_xattn_beta_lat"],
        "X_bq": w["L0_xattn_bq"], "X_bv": bkv[H * P:],
        "F_b1m": w["L0_ffn_b1m"], "F_b2m": w["L0_ffn_b2m"], "D_bq": w["L1_attn_bq"],
        "D_bk": w["L1_attn_bkv"][:P], "D_bv": w["L1_attn_bkv"][P:],
        "E_bq": w["L1_xattn_bq"], "E_bk": w["L1_xattn_bk"]}
    rows = {
        "norm_g": np.repeat(w["L0_attn_norm_g"].reshape(HA), per_head), "A_b_out": w["L0_attn_b_out"],
        "X_bo": w["L0_xattn_bo"], "F_b_gate": w["L0_ffn_b_gate"], "alpha": w["L0_ffn_alpha"], "E_bv": w["L1_xattn_bv"], "ln_gamma": w["L1_xattn_ln_gamma"],
        "ln_beta": w["L1_xattn_ln_beta"], "M_bias": np.concatenate([w["L1_ffn_router_b"], w["L1_ffn_lang_b"]])}
    arrays = {
        "x": w["x"], "ctx": w["ctx_1024"], "mask": w["mask_BxSxS2_ik1"],
        "ctxT": w["ctx_1024"].transpose(2, 0, 1),
        "cols": np.concatenate([as_cols(cols[n]) for n in COLS], 1),
        "rows": np.concatenate([rows[n].reshape(1, -1) for n in ROWS], 1),
        "consts": constants(),
        "A_wqkvT": w["L0_attn_w_qkv"].T, "A_woutT": w["L0_attn_w_out"].T,
        "X_WqT": w["L0_xattn_Wq"].T, "X_WkvT": w["L0_xattn_Wkv"].T, "X_Wo": w["L0_xattn_Wo"],
        "F_w_gate": w["L0_ffn_w_gate"], "F_W1m": w["L0_ffn_W1m"], "F_W2m": w["L0_ffn_W2m"],
        "F_W1e": w["L0_ffn_W1e"], "F_W2e": w["L0_ffn_W2e"], "F_b2e": w["L0_ffn_b2e"],
        "F_b1eT": as_cols(w["L0_ffn_b1e"]),
        "D_Wq": w["L1_attn_Wq"], "D_Wkv": w["L1_attn_Wkv"], "D_Wo": w["L1_attn_Wo"],
        "E_Wq": w["L1_xattn_Wq"], "E_Wk": w["L1_xattn_Wk"], "E_Wv": w["L1_xattn_Wv"],
        "M_w": np.concatenate([w["L1_ffn_router_w"], w["L1_ffn_lang_w"]]).T, "M_b2": w["L1_ffn_b2"],
        "M_b1T": as_cols(w["L1_ffn_b1"]), "M_w1": w["L1_ffn_w1"], "M_w2": w["L1_ffn_w2"]}
    arrays = {n: np.ascontiguousarray(a) for n, a in arrays.items()}
    nc = bacc.Bacc("TRN2", target_bir_lowering=False, num_devices=1, dynamic_dma_scratch_size=1024)
    tensors = {n: nc.dram_tensor(n + "_dram", a.shape, mybir.dt.from_np(a.dtype), kind="ExternalInput").ap()
               for n, a in arrays.items()}
    tensors["out"] = nc.dram_tensor("out_dram", (B, S, P), F32, kind="ExternalOutput").ap()
    tensors["gates"] = nc.dram_tensor("gates_dram", (B, NE, S), F32, kind="Internal").ap()
    build(nc, tensors)
    result = run_bass_kernel_spmd(nc, [{n + "_dram": a for n, a in arrays.items()}], core_ids=[0])
    return result.results[0]["out_dram"]
```

```python
from contextlib import ExitStack

import numpy as np

import concourse.bass as bass
from concourse import mybir

P = 128
B = 2
S = 512
NT = S // P
C = 77
H = 8
HA = 16
HID = 512
NM = HID // P
NE = 8
NL = 4
LN_EPS = 1e-5
NORM_EPS = 1e-12
SCALE = P ** -0.5
BIG = 3e38
NEG = -1e30

F32 = mybir.dt.float32
F32R = mybir.dt.float32r
BF16 = mybir.dt.bfloat16
I32 = mybir.dt.int32
U32 = mybir.dt.uint32
ALU = mybir.AluOpType
ACT = mybir.ActivationFunctionType
AX = mybir.AxisListType.X


def offsets(parts):
    at, out = 0, {}
    for name, n in parts:
        out[name] = at
        at += n
    return out, at


COLS, N_COLS = offsets([
    ("norm_b", 1), ("gamma_media", 1), ("beta_media", 1), ("gamma_lat", 1), ("beta_lat", 1),
    ("X_bq", H), ("X_bv", H), ("F_b1m", NM), ("F_b2m", 1), ("D_bq", H), ("D_bk", 1), ("D_bv", 1),
    ("E_bq", 1), ("E_bk", 1)])
ROWS, N_ROWS = offsets([
    ("norm_g", P), ("A_b_out", P), ("X_bo", P), ("F_b_gate", NE), ("alpha", 1),
    ("E_bv", P), ("ln_gamma", P), ("ln_beta", P), ("M_bias", NE + NL)])
CONSTS, N_CONSTS = offsets([
    ("ident", P), ("blocks", 2 * P), ("head_sum", HA), ("causal", P), ("iota", NE), ("ones", 1), ("peT", S)])

LN_ORDER = ["A0", "A1", "X0", "X1", "F0", "F1", "D0", "D1", "E0", "M0", "E1", "M1"]
W_A_BIAS, W_A, W_X_BIAS = 1, 2, 3
W_F = W_X_BIAS + 1
W_E_BETA = W_F + 1
W_E = W_E_BETA + 1
W_M = W_E + 1
READ_BY_LN = {"X": W_A, "D": W_F, "M": W_E}

F_UNITS = [(0, None), (0, 0), (0, 1), (1, None), (1, 0), (1, 1)]
F_CHUNKS = NM * len(F_UNITS)
MAIN = 2


def late_chain(b):
    return [[("stats", "E", b)], [("hat", "E", b)], [("turnx", "E", b)], [("E_q", b)], [("E_s", b)], [("E_exp", b)],
            [("E_t", b)], [("E_o", b)], [("E_ln", b)], [("stats", "M", b)], [("hat", "M", b)], [("turnx", "M", b)],
            [("split", "M", b), ("M_router", b)], [("M_lang", b)], [("M_best", b)], [("M_gates", b)], [("M_b2", b)]]


def new_x(stage, b):
    return [("turnx", stage, b), ("split", stage, b)]


def mix(*lists):
    out = []
    for n in range(max(map(len, lists))):
        for pieces in lists:
            if n < len(pieces):
                out += pieces[n] if isinstance(pieces[n], list) else [pieces[n]]
    return out


def mix_steps(*lists):
    return [sum(pieces, []) for pieces in zip(*lists)]


def chunks(first, end):
    return [("chunk", n) for n in range(first, end)]


def vall(kind, b):
    return [("vall", kind, b, n) for n in range(NT)]


X_HOOKS = {
    "prologue": [("F_main",)], "late": [*new_x("X", 1), ("keys", "X", 1), *vall("X", 1)],
    "mid": [("stats", "F", 0), ("hat", "F", 0)],
    "late1": [*new_x("F", 0), ("F_gate", 0)], "last": [("F_split", 0, 0), ("F_split", 0, 1)]}
D_HOOKS = {
    "prologue": [("F_out", 1), ("stats", "D", 1), ("hat", "D", 1)],
    "late": [*new_x("D", 1), ("keys", "D", 1), *vall("D", 1)],
    "mid": late_chain(0)[0],
    "steps": mix_steps(late_chain(0)[1:7] + [[]] + late_chain(0)[7:-1],
                       [[("M_split", r, [part])] for r in range(4) for part in range(4)])}
F_ITEMS = [
    ("stats", "F", 1), ("chunk", 0), ("hat", "F", 1), ("chunk", 1), *new_x("F", 1), ("chunk", 2), ("F_gate", 1),
    *chunks(3, 9), ("F_split", 1, 0), *chunks(9, 12), ("F_split", 1, 1), ("chunk", 12), ("F_out", 0),
    ("chunk", 13), ("stats", "D", 0), ("chunk", 14), ("hat", "D", 0), ("chunk", 15), *new_x("D", 0), ("chunk", 16),
    ("keys", "D", 0), ("chunk", 17), ("first_q", "D"), ("chunk", 18), *mix(vall("D", 0), chunks(19, 23)), ("chunk", 23)]
late_m, M_ITEMS = late_chain(1), [("M_b2", 0)]
for n in range(30):
    if n % 3 != 2 and late_m:
        M_ITEMS += late_m.pop(0)
    M_ITEMS.append(("chunk", n))
    if n % NM == 3 and n < 4 * NM:
        M_ITEMS.append(("M_split", 4 + n // NM))


def follow(do, items):
    for name, *args in items:
        if name in do:
            do[name](*args)


def build(nc, t):
    ctx = ExitStack()
    with ctx:
        def sb(name, shape, dt=F32):
            return ctx.enter_context(nc.sbuf_tensor(name, shape, dt))

        def sem(name):
            return ctx.enter_context(nc.semaphore(name))

        KB2 = 2048
        base = (nc.sbuf_base + 63) // 64 * 64
        V_AT, W_AT, H_AT = (0, 8 * KB2), 16 * KB2, 20 * KB2
        prob_bytes = (NT * (S + C) * 4 + 31) // 32 * 32
        sb("arena", [P, (64 + H_AT + 2 * prob_bytes + 5 * KB2) // 4])

        def at(name, shape, offset, dt=F32):
            return nc.alloc_sbuf_tensor_at(name, shape, dt, offset=base + offset)

        cols, rows, consts = sb("cols", [P, N_COLS]), sb("rows", [P, N_ROWS]), sb("consts", [P, N_CONSTS])
        x = [sb(f"x{b}", [P, NT, P]) for b in range(B)]
        ctx_tok, ctxT = sb("ctx_tok", [C, B, P]), sb("ctxT", [P, B, C])
        mask = sb("mask", [P, B, NT, C], I32)
        A_wqkvT, A_woutT = sb("A_wqkvT", [P, 3 * P]), sb("A_woutT", [P, P])
        X_WqT, X_WkT, X_WvT, X_Wo = (at(f"X_W{n}", [P, H, P], V_AT[1] + i * 2 * KB2)
                                     for i, n in enumerate(("qT", "kT", "vT", "o")))
        F_w_gate, F_W1m, F_W2m = sb("F_w_gate", [P, NE]), sb("F_W1m", [P, HID]), sb("F_W2m", [P, NM, P])
        F_W1e = [[at(f"F_W1e{b}{k}", [P, HID], V_AT[b] + 2 * k * KB2) for k in range(2)] for b in range(B)]
        F_W2e = [[at(f"F_W2e{b}{k}", [P, NM, P], V_AT[b] + (2 * k + 1) * KB2) for k in range(2)] for b in range(B)]
        F_b1e = [[sb(f"F_b1e{b}{k}", [P, NM]) for k in range(2)] for b in range(B)]
        F_b2e = sb("F_b2e", [P, B, 2])
        D_Wq, D_Wkv, D_Wo = sb("D_Wq", [P, H, P]), sb("D_Wkv", [P, 2 * P]), sb("D_Wo", [P, H, P])
        E_Wq, E_Wk, E_Wv = (sb(f"E_W{n}", [P, P]) for n in "qkv")
        M_w, M_b2 = sb("M_w", [P, NE + NL]), sb("M_b2", [NE, P])
        M_b1, M_b1g = sb("M_b1", [P, NE * NM]), [sb(f"M_b1g{k}", [P, NM]) for k in range(4)]
        M_w1 = [sb(f"M_w1{s}", [P, HID]) for s in range(2)]
        M_w2 = [sb(f"M_w2{s}", [P, NM, P]) for s in range(2)]

        def col(name, n=1, at=0):
            return cols[:, COLS[name] + at:COLS[name] + at + n]

        def row(name, n=P):
            return rows[:, ROWS[name]:ROWS[name] + n]

        def const(name, n):
            return consts[:, CONSTS[name]:CONSTS[name] + n]

        def flat(ap):
            return ap.rearrange("p a b -> p (a b)")

        def tiled(ap):
            return ap.rearrange("p (n d) -> p n d", d=P)

        ident = const("ident", P)

        bn, mv = sb("bn", [P, B, NT, 6]), sb("mv", [P, B, NT, 2])
        var_eps, rstd = (sb(n, [P, B, NT]) for n in ("var_eps", "rstd"))
        minus_half = sb("minus_half", [P, NT])
        xhat = [sb(f"xhat{b}", [P, NT, P]) for b in range(B)]
        xT = [sb(f"xT{b}", [P, S]) for b in range(B)]
        z_hi, z_lo = ([sb(f"z_{n}{b}", [P, S], F32R) for b in range(B)] for n in ("hi", "lo"))
        a_mask = sb("a_mask", [P, 2 * P])
        kv = [at(f"kv{b}", [P, NT * 2 * P], V_AT[0] + 2 * b * KB2) for b in range(B)]
        qT = [at(f"qT{b}", [P, S], V_AT[0] + (4 + b) * KB2) for b in range(B)]
        t1 = [at(f"t1{b}", [P, S], V_AT[0] + (6 + b) * KB2) for b in range(B)]
        gm = [sb(f"gm{b}", [P, 2 * P]) for b in range(B)]
        vsum = sb("vsum", [P, B])
        norm2, norm1, rnorm = (sb(n, [P, B, NT * HA]) for n in ("norm2", "norm1", "rnorm"))
        c_bn, c_mv, c_var = sb("c_bn", [C, B, 6]), sb("c_mv", [C, B, 2]), sb("c_var", [C, B])
        c_rstd, c_hat = sb("c_rstd", [C, B]), sb("c_hat", [C, B, P])
        czT = sb("czT", [P, B, C])
        cz_scaled = sb("cz_scaled", [P, B, C])
        X_A, X_V = (at(n, [P, H, P], W_AT + i * 2 * KB2) for i, n in enumerate(("X_A", "X_V")))
        X_r0, X_bias = sb("X_r0", [P, H]), sb("X_bias", [P, P])
        X_vc = sb("X_vc", [C, B, H * P])
        k_hi, k_lo = ([sb(f"k_{n}{b}", [P, S], F32R) for b in range(B)] for n in ("hi", "lo"))
        valuesT = [sb(f"valuesT{b}", [P, S]) for b in range(B)]
        vall = [at(f"vall{b}", [P, NT, H * P], V_AT[b]) for b in range(B)]
        w_hi, w_lo = ([sb(f"w_{n}{p}", [P, P], F32R) for p in range(2)] for n in ("hi", "lo"))
        w_full = [sb(f"w_full{p}", [P, P]) for p in range(2)]
        q_hi, q_lo = ([sb(f"q_{n}{p}", [P, S], F32R) for p in range(2)] for n in ("hi", "lo"))
        q_full = [sb(f"q_full{p}", [P, S]) for p in range(2)]
        probs = [at(f"probs{p}", [P, NT, S + C], H_AT + p * prob_bytes) for p in range(2)]
        pT = at("pT", [P, NT + 1, S], H_AT + 2 * prob_bytes)
        neg_cmax, neg_max = sb("neg_cmax", [P, 2, NT]), sb("neg_max", [P, 2, NT])
        sum_x, sum_c = sb("sum_x", [P, 2, NT]), sb("sum_c", [P, 2, NT])
        o_start = sb("o_start", [P, 1])
        denom, rdenom = sb("denom", [P, 2, NT]), sb("rdenom", [P, 2, NT])
        ident_bf, causal_bf = sb("ident_bf", [P, P], BF16), sb("causal_bf", [P, P], BF16)
        w1_hi, w1_lo, w2_hi, w2_lo = (
            [sb(f"{n}{s}", [P, HID], F32R) for s in range(3)] + [at(f"{n}3", [P, HID], W_AT + k * KB2, F32R)]
            for k, n in enumerate(("w1_hi", "w1_lo", "w2_hi", "w2_lo")))
        h_full = [at(f"h_full{i}", [P, S], H_AT + i * KB2) for i in range(4)]
        h_hi = [at(f"h_hi{i}", [P, S], H_AT + (4 + i) * KB2, F32R) for i in range(4)]
        h_lo = [at(f"h_lo{i}", [P, S], H_AT + (8 + i) * KB2, F32R) for i in range(4)]
        yT = [sb(f"yT{b}", [P, S]) for b in range(B)]
        y_gated = [sb(f"y_gated{i}", [P, S]) for i in range(2)]
        xsum, mean_bc = sb("xsum", [P, B]), sb("mean_bc", [P, B, P])
        f_lg, f_max, f_idx = sb("f_lg", [P, B, NE]), sb("f_max", [P, B, 8]), sb("f_idx", [P, B, 8], U32)
        f_nmax, f_e, f_es = sb("f_nmax", [P, B]), sb("f_e", [P, B, 2]), sb("f_es", [P, B])
        f_ers, f_g = sb("f_ers", [P, B]), sb("f_g", [P, B, 2])
        f_a, f_1a = sb("f_a", [P, 1]), sb("f_1a", [P, 1])
        f_bias0, f_bias1, f_bias = sb("f_bias0", [P, 1]), sb("f_bias1", [P, B]), sb("f_bias", [P, B])
        e_lim = sb("e_lim", [P, B * NT * C])
        e_tmp = at("e_tmp", [P, B * NT * C], V_AT[1])
        e_kT, e_v = sb("e_kT", [P, B, C]), sb("e_v", [C, B, P])
        e_qT, e_on, e_og = ([at(f"{n}{b}", [P, NT, P], V_AT[b] + i * KB2) for b in range(B)]
                            for i, n in enumerate(("e_qT", "e_on", "e_og")))
        e_s, e_p = ([at(f"{n}{b}", [P, NT, C], V_AT[b] + (3 + i) * KB2) for b in range(B)]
                    for i, n in enumerate(("e_s", "e_p")))
        e_pT = [at(f"e_pT{b}", [C, S], V_AT[b] + 5 * KB2) for b in range(B)]
        e_nmax, e_sum, e_rsum, e_rsum2 = (sb(n, [P, B, NT]) for n in ("e_nmax", "e_sum", "e_rsum", "e_rsum2"))
        m_lg = [sb(f"m_lg{b}", [P, NT, NE + NL]) for b in range(B)]
        m_lmax = sb("m_lmax", [P, B, NT])
        m_ld, m_le = sb("m_ld", [P, B, NT, NL]), sb("m_le", [P, B, NT, NL])
        m_ls, m_lr = sb("m_ls", [P, B, NT]), sb("m_lr", [P, B, NT])
        m_lp, m_ew = sb("m_lp", [P, B, NT, NL + 1]), sb("m_ew", [P, B, NT, NL])
        m_rl = [sb(f"m_rl{b}", [P, NT, NE]) for b in range(B)]
        m_max, m_idx = sb("m_max", [P, B, NT, 8]), sb("m_idx", [P, B, NT, 8], U32)
        m_idxf = sb("m_idxf", [P, B, NT, 2])
        m_d, m_e = sb("m_d", [P, B, NT]), sb("m_e", [P, B, NT])
        m_s, m_g0, m_g1 = (sb(n, [P, B, NT]) for n in ("m_s", "m_g0", "m_g1"))
        m_oh, m_og = sb("m_oh", [P, B, 2, NT, NE]), sb("m_og", [P, B, 2, NT, NE])
        gates = [sb(f"gates{b}", [P, NT, NE]) for b in range(B)]
        gT = [sb(f"gT{b}", [NE, S]) for b in range(B)]
        gates_bc = at("gates_bc", [P, B * NE, S], V_AT[0])

        bank = [ctx.enter_context(nc.psum_tensor(f"bank{i}", [P, S], F32)) for i in range(8)]
        S_BANK, C_BANK, T_BANK, R_BANK, O_BANK = (0, 1), 2, (3, 4), 5, 7
        V_BANK = {"X0": (3, 4), "X1": (5, 6), "D0": (2, 6), "D1": (2, 6)}
        TR_BANK = {"A0": 0, "A1": 4, "X0": 1, "X1": 6, "F0": 6, "F1": 7, "D0": 6, "D1": 6, "E0": 6, "M0": 2,
                   "E1": 7, "M1": 5}
        EA, EB = (2, 5), (6, 7)
        VC_BANK = ((0, 4), (2, 6))
        Y_BANK = (3, 4)

        ld = {n: sem(f"ld_{n}") for n in (
            "consts", "cols", "rows", "x0", "x1", "ctx", "ctxT", "mask", "A_wqkvT", "A_woutT", "X_Wqk", "X_Wvo",
            "F_W", "D_W", "E_W", "M_W", "M_b1")}
        x_written = [sem(f"x_written{b}") for b in range(B)]
        (ln_bn, ln_stats, ln_eps, ln_rstd, ln_hat, ln_mm, ln_xT, z_hi_s, z_split) = (
            sem(n) for n in ("ln_bn", "ln_stats", "ln_eps", "ln_rstd", "ln_hat", "ln_mm", "ln_xT", "z_hi",
                             "z_split"))
        fills, a_mask_ready, f_alpha = sem("fills"), sem("a_mask_ready"), sem("f_alpha")
        (a_q_mm, a_kv_mm, a_q, a_kv, a_g_mm, a_g, a_gq_mm, a_t1, a_n2_mm, a_n2, a_norm, a_rnorm, a_o_mm, a_o,
         a_oT_mm, a_oT, a_y_mm) = (sem("a_" + n) for n in (
             "q_mm", "kv_mm", "q", "kv", "g_mm", "g", "gq_mm", "t1", "n2_mm", "n2", "norm", "rnorm", "o_mm", "o",
             "oT_mm", "oT", "y_mm"))
        (c_bn_s, c_stats, c_eps, c_rstd_s, c_hat_s, c_mm, c_zT, c_scaled) = (sem("c_" + n) for n in (
            "bn", "stats", "eps", "rstd", "hat", "mm", "zT", "scaled"))
        (w_a_mm, w_a, w_v_mm, w_v, w_b_mm, w_bias, w_vc_mm, w_vc) = (sem("w_" + n) for n in (
            "a_mm", "a", "v_mm", "v", "b_mm", "bias", "vc_mm", "vc"))
        bf_ready = sem("bf_ready")
        k_hi_s, keys_ready, d_k_mm, d_v_mm, d_v_ready, d_k_full = (sem(n) for n in (
            "k_hi", "keys_ready", "d_k_mm", "d_v_mm", "d_v_ready", "d_k_full"))
        vall_mm, vall_even, vall_odd = sem("vall_mm"), sem("vall_even"), sem("vall_odd")
        (w_hi_s, w_ready, r_mm, q_first, q_hi_s, q_ready, c_s_mm, s_mm, cmax_ready, max_ready, probs_ready, t_mm,
         pT_even, pT_odd, o_mm, o_added, denom_ready, rdenom_ready) = (sem(n) for n in (
             "w_hi", "w_ready", "r_mm", "q_first", "q_hi", "q_ready", "c_s_mm", "s_mm", "cmax_ready", "max_ready",
             "probs_ready", "t_mm", "pT_even", "pT_odd", "o_mm", "o_added", "denom_ready", "rdenom_ready"))
        h_mm, h_gelu, h_hi_even, h_hi_odd, h_split, y_mm = (sem(n) for n in (
            "h_mm", "h_gelu", "h_hi_even", "h_hi_odd", "h_split", "y_mm"))
        ws_hi, ws_ready = sem("ws_hi"), sem("ws_ready")
        y_gated_s, y_start, y_added = sem("y_gated"), sem("y_start"), sem("y_added")
        (f_mean, f_lg_mm, f_pick, f_idx_s, f_nmax_s, f_exp, f_w2,
         f_bias_s, f_yT, f_out_mm) = (sem("f_" + n) for n in (
             "mean", "lg_mm", "pick", "idx", "nmax", "exp", "w2",
             "bias", "yT", "out_mm"))
        f_ld = [[sem(f"f_ld{b}{k}") for k in range(2)] for b in range(B)]
        (e_lim_s, e_kv_mm, e_k_s, e_v_s, e_q_mm, e_q, e_s_mm, e_max, e_exp, e_t_mm, e_pT_s,
         e_o_mm, e_norm, e_st, e_eps, e_r) = (sem("e_" + n) for n in (
             "lim", "kv_mm", "k", "v", "q_mm", "q", "s_mm", "max", "exp", "t_mm", "pT",
             "o_mm", "norm", "st", "eps", "r"))
        (m_lg_mm, m_chain, m_lexp, m_exp, m_gates, m_gT_mm, m_gT, m_b_mm, m_out_mm) = (
            sem("m_" + n) for n in ("lg_mm", "chain", "lexp", "exp", "gates", "gT_mm", "gT", "b_mm",
                                    "out_mm"))
        m_raw, m_gates_bc = ([sem(f"m_{n}{i}") for i in range(2)] for n in ("raw", "gates_bc"))
        m_bias = [sem(f"m_bias{k}") for k in range(4)]
        m_gates_out = sem("m_gates_out")
        stored = sem("stored")

        def ln_index(stage, b):
            return LN_ORDER.index(f"{stage}{b}")

        def z_index(stage, b):
            return len([n for n in LN_ORDER[:ln_index(stage, b)] if n[0] not in "AE"])

        def v_index(kind, b):
            return (0 if kind == "X" else B) + b

        class Head:

            def __init__(self, kind, b, h, par):
                self.kind, self.b, self.h, self.par = kind, b, h, par
                self.g = (0 if kind == "X" else B * H) + b * H + h
                self.chunks = NT + 1 if kind == "X" else NT
                even, odd = (self.chunks + 1) // 2, self.chunks // 2
                self.very_first = kind == "X" and b == 0 and isinstance(h, int) and h == 0
                x_even, x_all = (NT + 2) // 2, NT + 1
                self.c0 = (0 if kind == "X" else B * H * x_all) + (b * H + h) * self.chunks
                self.even0 = (0 if kind == "X" else B * H * x_even) + (b * H + h) * even
                self.odd0 = self.g * odd

            def keys(self, i):
                return S if self.kind == "X" else (i + 1) * P

        ORDER = list(reversed(range(NT)))

        def run_attention(eng, do, kind, hooks, prologue, step):
            def head(b, h):
                if isinstance(h, int) and h >= H:
                    b, h = b + 1, h - H
                if b >= B:
                    return None
                return Head(kind, b, h, h % 2 if isinstance(h, int) else None)

            def heads(b, k):
                return head(b, k + 1), head(b, k), head(b, k + 2), head(b, k + 3)

            def run_step(*hs, between=()):
                middle, end = [*between, [], []][:2]
                step(*hs, lambda: follow(do, middle))
                follow(do, end)

            prologue(head(0, 0), head(0, 1), head(0, 2))
            follow(do, hooks["prologue"])
            for b in range(B):
                if b and "steps" in hooks:
                    for k in range(H):
                        run_step(*heads(b, k), between=hooks["steps"][2 * k:2 * k + 2])
                    continue
                with eng.Fori(0, H // 2 - 2) as i:
                    for s in range(2):
                        run_step(*(Head(kind, b, i * 2 + (s + d), (s + d) % 2) for d in (1, 0, 2, 3)))
                for k in range(H - 4, H):
                    if k == H - 2:
                        follow(do, hooks["late1" if b else "late"])
                    if k == H - 1 and b:
                        follow(do, hooks["last"])
                    run_step(*heads(b, k))
                if not b:
                    follow(do, hooks["mid"])

        GROUP, GROUP_CHUNKS = 4, 4 * NM
        GROUPS = B * NE // GROUP

        def m_at(i, n):
            return i * GROUP_CHUNKS + (F_CHUNKS + n)

        block = ctx.enter_context(nc.Block())

        @block.sync
        def _(sp):
            def load(dst, src, s):
                sp.dma_start(dst, src).then_inc(s, 16)

            load(x[0][:], t["x"][0].rearrange("(n p) d -> p n d", p=P), ld["x0"])
            load(x[1][:], t["x"][1].rearrange("(n p) d -> p n d", p=P), ld["x1"])
            load(consts[:], t["consts"], ld["consts"])
            load(A_wqkvT[:], t["A_wqkvT"], ld["A_wqkvT"])
            load(cols[:], t["cols"], ld["cols"])
            load(ctx_tok[:], t["ctx"].rearrange("b c d -> c b d"), ld["ctx"])
            load(rows[:], t["rows"].to_broadcast((P, N_ROWS)), ld["rows"])
            load(A_woutT[:], t["A_woutT"], ld["A_woutT"])
            load(X_WqT[:], t["X_WqT"].rearrange("(h k) d -> k h d", k=P), ld["X_Wqk"])
            load(X_WkT[:], t["X_WkvT"][0:H * P].rearrange("(h k) d -> k h d", k=P), ld["X_Wqk"])
            load(X_WvT[:], t["X_WkvT"][H * P:].rearrange("(h k) d -> k h d", k=P), ld["X_Wvo"])
            load(X_Wo[:], t["X_Wo"].rearrange("(h k) d -> k h d", k=P), ld["X_Wvo"])
            load(ctxT[:], t["ctxT"], ld["ctxT"])
            for w, n in ((E_Wq, "E_Wq"), (E_Wk, "E_Wk"), (E_Wv, "E_Wv")):
                load(w[:], t[n], ld["E_W"])
            load(mask[:], t["mask"].rearrange("b (n p) c -> p b n c", p=P), ld["mask"])
            load(F_w_gate[:], t["F_w_gate"], ld["F_W"])
            load(F_W1m[:], t["F_W1m"], ld["F_W"])
            load(F_W2m[:], t["F_W2m"].rearrange("(m p) d -> p m d", p=P), ld["F_W"])
            load(D_Wq[:], t["D_Wq"].rearrange("d (h k) -> d h k", k=P), ld["D_W"])
            load(D_Wkv[:], t["D_Wkv"], ld["D_W"])
            load(D_Wo[:], t["D_Wo"].rearrange("(h k) d -> k h d", k=P), ld["D_W"])
            load(M_w[:], t["M_w"], ld["M_W"])
            load(M_b2[:], t["M_b2"], ld["M_W"])

            def expert(e, s):
                load(M_w1[s][:], t["M_w1"][bass.ds(e, 1)].rearrange("e d h -> d (e h)"), m_raw[s])
                load(M_w2[s][:], t["M_w2"][bass.ds(e, 1)].rearrange("e (m p) d -> p (e m) d", p=P), m_raw[s])

            load(M_b1[:], t["M_b1T"], ld["M_b1"])
            for k in range(GROUP):
                load(M_b1g[k][:], t["M_b1T"][:, (GROUP + k) * NM:(GROUP + k + 1) * NM], m_bias[k])
            for e in range(2):
                expert(e, e)

            for b in range(B):
                sp.wait_ge(f_idx_s, b + 1)
                sp.wait_ge(o_added, H * (b + 1) + 1)
                for k in range(2):
                    e = sp.value_load(f_idx[0:1, b, k:k + 1], min_val=0, max_val=NE - 1)
                    load(F_W1e[b][k][:], t["F_W1e"][bass.ds(e, 1)].rearrange("e d h -> d (e h)"), f_ld[b][k])
                    load(F_W2e[b][k][:], t["F_W2e"][bass.ds(e, 1)].rearrange("e (m p) d -> p (e m) d", p=P),
                         f_ld[b][k])
                    load(F_b1e[b][k][:], t["F_b1eT"][:, bass.ds(e * NM, NM)], f_ld[b][k])
                    load(F_b2e[:, b, k:k + 1], t["F_b2e"][bass.ds(e, 1)].rearrange("e d -> d e"), f_ld[b][k])

            def spread_gates(b):
                sp.wait_ge(m_gT, b + 1)
                sp.dma_start(t["gates"][b], gT[b][:]).then_inc(m_gates_out, 16)
                sp.wait_ge(m_gates_out, 16 * (b + 1))
                for n in range(NE):
                    e = (n + GROUP * b) % NE
                    load(gates_bc[:, b * NE + n, :], t["gates"][b, e:e + 1, :].to_broadcast((P, S)), m_gates_bc[b])

            def next_expert(r, e):
                sp.wait_ge(ws_ready, r + (len(F_UNITS) - 2))
                expert(e, r % 2)

            for e in range(2, 4):
                next_expert(e, e)
            spread_gates(0)
            for e in range(4, NE):
                next_expert(e, e)
            spread_gates(1)
            for e in range(GROUP):
                next_expert(NE + e, e)
            for k in range(GROUP):
                sp.wait_ge(h_gelu, m_at(2, NM * (k + 1)))
                load(M_b1g[k][:], t["M_b1T"][:, k * NM:(k + 1) * NM], m_bias[k])

            for b in range(B):
                sp.wait_ge(x_written[b], W_M)
                sp.dma_start(t["out"][b].rearrange("(n p) d -> p n d", p=P), x[b][:]).then_inc(stored, 16)
            sp.wait_ge(stored, 16 * B)

        @block.gpsimd
        def _(pool):
            g = nc.gpsimd
            g.memset(minus_half[:], -0.5).then_inc(fills, 1)
            g.memset(m_lp[:], 0.0).then_inc(fills, 1)
            pool.wait_ge(fills, 1)

            def norm(stage, b):
                n = ln_index(stage, b)
                scale, eps = (1.0 + LN_EPS, LN_EPS ** 2) if stage == "X" else (1.0, LN_EPS)
                pool.wait_ge(ln_stats, n + 1)
                g.tensor_scalar(var_eps[:, b], mv[:, b, :, 1], scale, eps, ALU.mult, ALU.add).then_inc(ln_eps, 1)
                pool.wait_ge(ln_eps, n + 1)
                g.tensor_tensor(rstd[:, b], var_eps[:, b], minus_half[:], ALU.pow).then_inc(ln_rstd, 1)

            def add_row(b, r, stage):
                pool.wait_ge(ln_hat, ln_index(stage, b) + 1)
                g.tensor_tensor(x[b][:], x[b][:], r.unsqueeze(1).to_broadcast((P, NT, P)),
                                ALU.add).then_inc(x_written[b], 1)

            def split_w(hd):
                w = (X_A if hd.kind == "X" else D_Wq)[:, bass.ds(hd.h, 1), :].rearrange("p a k -> p (a k)")
                p = hd.par
                if not (hd.kind == "X" and hd.b == 0 and isinstance(hd.h, int) and hd.h < 2):
                    pool.wait_ge(w_ready, hd.g - 1)
                g.tensor_copy(w_full[p][:], w).then_inc(w_hi_s, 1)
                pool.wait_ge(w_hi_s, hd.g * 2 + 1)
                if not (hd.kind == "X" and hd.b == 0 and isinstance(hd.h, int) and hd.h < 2):
                    pool.wait_ge(r_mm, hd.g - 1)
                g.tensor_tensor(w_hi[p][:], w_full[p][:], const("ones", 1).to_broadcast((P, P)),
                                ALU.mult).then_inc(w_hi_s, 1)
                pool.wait_ge(w_hi_s, hd.g * 2 + 2)
                g.tensor_tensor(w_lo[p][:], w_full[p][:], w_hi[p][:], ALU.subtract).then_inc(w_ready, 1)

            def split_q(hd):
                p = hd.par
                pool.wait_ge(q_hi_s, hd.g + 1)
                if not (hd.kind == "X" and hd.b == 0 and isinstance(hd.h, int) and hd.h < 2):
                    pool.wait_ge(s_mm, (hd.g - 1) * NT)
                g.tensor_tensor(q_lo[p][:], q_full[p][:], q_hi[p][:], ALU.subtract).then_inc(q_ready, 1)

            def prologue(h0, h1, h2):
                split_w(h1)
                split_w(h2)
                split_q(h1)

            def step(hs, ht, hn, hw, middle):
                if hw:
                    split_w(hw)
                if hn:
                    split_q(hn)
                middle()

            def split_mlp(w1, w2, slot, his):
                g.tensor_tensor(w1_hi[slot][:], w1, const("ones", 1).to_broadcast((P, HID)),
                                ALU.mult).then_inc(ws_hi, 1)
                g.tensor_scalar(w2_hi[slot][:], w2, 1.0, 1.0, ALU.mult, ALU.mult).then_inc(ws_hi, 1)
                pool.wait_ge(ws_hi, his + 1)
                g.tensor_tensor(w1_lo[slot][:], w1, w1_hi[slot][:], ALU.subtract)
                pool.wait_ge(ws_hi, his + 2)
                g.tensor_tensor(w2_lo[slot][:], w2, w2_hi[slot][:], ALU.subtract).then_inc(ws_ready, 1)

            def f_split(b, k):
                pool.wait_ge(f_w2, 2 + 2 * b + k)
                if b:
                    pool.wait_ge(y_mm, NM * (2 + k))
                n = 1 + 2 * b + k
                split_mlp(F_W1e[b][k][:], flat(F_W2e[b][k][:]), k, 2 * n)

            def m_split(r, parts=range(4)):
                slot = r % 4
                w1, w2 = M_w1[r % 2][:], flat(M_w2[r % 2][:])
                his = 2 * (1 + B * 2 + r)
                if 0 in parts:
                    last_use = (5, 6, 4, 4)[r] if r < 4 else m_at(0, 0) // NM + (r - 3 if r < NE else r + 1)
                    pool.wait_ge(y_mm, NM * last_use)
                    pool.wait_ge(m_raw[r % 2], 32 * (r // 2 + 1))
                    g.tensor_tensor(w1_hi[slot][:], w1, const("ones", 1).to_broadcast((P, HID)),
                                    ALU.mult).then_inc(ws_hi, 1)
                if 1 in parts:
                    g.tensor_scalar(w2_hi[slot][:], w2, 1.0, 1.0, ALU.mult, ALU.mult).then_inc(ws_hi, 1)
                if 2 in parts:
                    pool.wait_ge(ws_hi, his + 1)
                    g.tensor_tensor(w1_lo[slot][:], w1, w1_hi[slot][:], ALU.subtract)
                if 3 in parts:
                    pool.wait_ge(ws_hi, his + 2)
                    g.tensor_tensor(w2_lo[slot][:], w2, w2_hi[slot][:], ALU.subtract).then_inc(ws_ready, 1)

            def add_gated(u):
                b = u // NE
                pool.wait_ge(y_gated_s, u + 1)
                pool.wait_ge(y_start, b + 1)
                if u:
                    pool.wait_ge(y_added, u)
                g.tensor_tensor(yT[b][:], yT[b][:], y_gated[u % 2][:], ALU.add).then_inc(y_added, 1)

            def f_gate(b):
                pool.wait_ge(ln_xT, ln_index("F", b) + 1)
                g.tensor_scalar(mean_bc[:, b, :], xsum[:, b:b + 1].to_broadcast((P, P)), 1.0 / S, 1.0,
                                ALU.mult, ALU.mult).then_inc(f_mean, 1)

            def e_o_piece(b):
                pool.wait_ge(e_st, b + 1)
                g.tensor_tensor(var_eps[:, b], mv[:, b, :, 1], e_rsum2[:, b], ALU.mult).then_inc(e_eps, 1)
                pool.wait_ge(e_eps, 3 * b + 1)
                g.tensor_scalar(var_eps[:, b], var_eps[:, b], LN_EPS, 1.0, ALU.add, ALU.mult).then_inc(e_eps, 1)
                pool.wait_ge(e_eps, 3 * b + 2)
                g.tensor_tensor(rstd[:, b], var_eps[:, b], minus_half[:], ALU.pow).then_inc(e_eps, 1)
                pool.wait_ge(e_eps, 3 * b + 3)
                g.tensor_tensor(rstd[:, b], rstd[:, b], e_rsum[:, b], ALU.mult).then_inc(e_r, 1)

            def e_beta(b):
                add_row(b, row("ln_beta"), "E")

            do = {"stats": norm, "F_gate": f_gate, "F_split": f_split, "M_split": m_split, "E_o": e_o_piece,
                  "E_s": e_beta}

            norm("A", 0)
            norm("A", 1)
            pool.wait_ge(c_stats, 1)
            g.tensor_scalar(c_var[:], c_mv[:, :, 1], LN_EPS, 1.0, ALU.add, ALU.mult).then_inc(c_eps, 1)
            pool.wait_ge(c_eps, 1)
            g.tensor_tensor(c_rstd[:], c_var[:], minus_half[0:C, 0:B], ALU.pow).then_inc(c_rstd_s, 1)
            pool.wait_ge(ld["rows"], 16)
            for b in range(B):
                add_row(b, row("A_b_out"), "A")
            pool.wait_ge(ld["consts"], 16)
            g.tensor_copy(ident_bf[:], ident).then_inc(bf_ready, 1)
            g.tensor_copy(causal_bf[:], const("causal", P)).then_inc(bf_ready, 1)
            pool.wait_ge(w_a, 2)
            split_w(Head("X", 0, 0, 0))
            norm("X", 0)
            norm("X", 1)
            pool.wait_ge(w_bias, 2)
            for b in range(B):
                add_row(b, X_bias[:], "X")
            split_q(Head("X", 0, 0, 0))
            def f_main():
                pool.wait_ge(ld["F_W"], 3 * 16)
                pool.wait_ge(f_w2, 1)
                split_mlp(F_W1m[:], flat(F_W2m[:]), MAIN, 0)

            do["F_main"] = f_main
            do["first_q"] = lambda kind: (split_w(Head(kind, 0, 0, 0)), split_q(Head(kind, 0, 0, 0)))
            run_attention(pool, do, "X", X_HOOKS, prologue, step)
            pool.wait_ge(ld["D_W"], 3 * 16)
            follow(do, F_ITEMS)
            run_attention(pool, do, "D", D_HOOKS, prologue, step)

            def m_chunk(n):
                if n >= NM and n % NM == 2:
                    add_gated(n // NM - 1)

            do["chunk"] = m_chunk
            follow(do, M_ITEMS)
            add_gated(NE - 2)
            for u in range(NE, B * NE):
                add_gated(u - 1)
                if u < NE + GROUP:
                    m_split(u)
            add_gated(B * NE - 1)

        @block.scalar
        def _(act):
            a = nc.scalar

            def turnx(stage, b):
                act.wait_ge(ln_mm, ln_index(stage, b) + 1)
                src = bank[TR_BANK[f"{stage}{b}"]][:]
                if stage == "X":
                    a.activation(xT[b][:], src, ACT.Identity, scale=col("gamma_lat"),
                                 bias=col("beta_lat")).then_inc(ln_xT, 1)
                elif stage == "F":
                    a.activation(xT[b][:], src, ACT.Copy, accum_out=xsum[:, b:b + 1]).then_inc(ln_xT, 1)
                else:
                    a.copy(xT[b][:], src).then_inc(ln_xT, 1)

            def keys(kind, b):
                if kind == "D":
                    act.wait_ge(d_v_mm, b + 1)
                    a.activation(valuesT[b][:], bank[6][:], ACT.Identity, bias=col("D_bv")).then_inc(d_v_ready, 1)

            def vall_piece(kind, b, i):
                act.wait_ge(vall_mm, 2 * NT * v_index(kind, b) + 2 * i + 1)
                a.copy(vall[b][:, i, 0:S], bank[V_BANK[f"{kind}{b}"][0]][:]).then_inc(vall_even, 1)

            def f_gate(b):
                act.wait_ge(f_nmax_s, b + 1)
                a.activation(f_e[:, b, :], f_max[:, b, 0:2], ACT.Exp, bias=f_nmax[:, b:b + 1],
                             accum_out=f_es[:, b:b + 1]).then_inc(f_exp, 1)

            def gelu(n, func, bias):
                k, g = n
                act.wait_ge(h_mm, g + 1)
                if not (isinstance(g, int) and g < 4):
                    act.wait_ge(h_split, g - 3)
                a.activation(h_full[k % 4][:], bank[k % 2][:], func, bias=bias).then_inc(h_gelu, 1)

            def gelu_hi(n):
                k, g = n
                act.wait_ge(h_gelu, g + 1)
                if not (isinstance(g, int) and g < 4):
                    act.wait_ge(y_mm, g - 3)
                a.copy(h_hi[k % 4][:], h_full[k % 4][:]).then_inc(h_hi_even, 1)

            def f_gelu(n):
                if n >= F_CHUNKS:
                    return
                b, k = F_UNITS[n // NM]
                m = n % NM
                if k is None:
                    bias = col("F_b1m", 1, m)
                else:
                    if m == 0:
                        act.wait_ge(f_ld[b][k], 4 * 16)
                    bias = F_b1e[b][k][:, m:m + 1]
                gelu((n, n), ACT.Gelu_apprx_tanh, bias)
                if n % 2 == 0:
                    gelu_hi((n, n))

            def f_out(b):
                act.wait_ge(y_mm, NM * 3 * (b + 1))
                act.wait_ge(f_bias_s, 2 * b + 2)
                a.activation(yT[b][:], bank[Y_BANK[b]][:], ACT.Identity, bias=f_bias[:, b:b + 1]).then_inc(f_yT, 1)

            def e_q_piece(b):
                act.wait_ge(e_q_mm, b + 1)
                a.activation(flat(e_qT[b][:]), bank[EA[b]][:], ACT.Identity, bias=col("E_bq")).then_inc(e_q, 1)

            def e_exp_piece(b):
                act.wait_ge(e_max, b + 1)
                for i in range(NT):
                    last = a.activation(e_p[b][:, i, :], e_s[b][:, i, :], ACT.Exp, bias=e_nmax[:, b, i:i + 1],
                                        accum_out=e_sum[:, b, i:i + 1])
                last.then_inc(e_exp, 1)

            def e_t_piece(b):
                act.wait_ge(e_t_mm, b + 1)
                a.copy(e_pT[b][:], bank[EA[b]][0:C, :]).then_inc(e_pT_s, 1)

            def m_lang(b):
                act.wait_ge(m_chain, M_CHAIN * b + 3)
                a.activation(m_le[:, b], m_ld[:, b], ACT.Exp).then_inc(m_lexp, 1)

            def m_best(b):
                act.wait_ge(m_chain, M_CHAIN * b + M_CHAIN_D)
                a.activation(m_e[:, b], m_d[:, b], ACT.Exp).then_inc(m_exp, 1)

            def m_gates_piece(b):
                act.wait_ge(m_gT_mm, b + 1)
                a.copy(gT[b][:], bank[EA[b]][0:NE, :]).then_inc(m_gT, 1)

            def m_b2(b):
                act.wait_ge(m_b_mm, b + 1)
                a.copy(yT[b][:], bank[EB[b]][:]).then_inc(y_start, 1)

            do = {"turnx": turnx, "keys": keys, "vall": vall_piece, "F_gate": f_gate, "F_out": f_out,
                  "chunk": lambda n: f_gelu(n + 2), "E_q": e_q_piece, "E_exp": e_exp_piece, "E_t": e_t_piece,
                  "M_lang": m_lang, "M_best": m_best, "M_gates": m_gates_piece, "M_b2": m_b2}

            for b in range(B):
                turnx("A", b)
                act.wait_ge(a_q_mm, b + 1)
                a.copy(qT[b][:], bank[4 * b + 1][:]).then_inc(a_q, 1)
            for b in range(B):
                act.wait_ge(a_n2, b + 1)
                a.activation(norm1[:, b], norm2[:, b], ACT.Sqrt).then_inc(a_norm, 1)
            act.wait_ge(ld["cols"], 16)
            act.wait_ge(c_mm, 1)
            a.activation(flat(czT[:]), bank[0][:, 0:B * C], ACT.Identity,
                         scale=col("gamma_media"), bias=col("beta_media")).then_inc(c_zT, 1)
            act.wait_ge(w_a_mm, 1)
            a.copy(flat(X_A[:, 0:4, :]), bank[1][:]).then_inc(w_a, 1)
            for b in range(B):
                act.wait_ge(a_oT_mm, b + 1)
                act.wait_ge(a_g, B)
                a.activation(t1[b][:], bank[4 * b][:], ACT.Identity, bias=vsum[:, b:b + 1]).then_inc(a_oT, 1)
            act.wait_ge(w_v_mm, 1)
            a.copy(flat(X_V[:, 0:4, :]), bank[2][:]).then_inc(w_v, 1)
            turnx("X", 0)
            for i in range(NT):
                vall_piece("X", 0, i)

            def e_tile(hd, j):
                i, p, n = ORDER[j], hd.par, hd.keys(ORDER[j])
                act.wait_ge(max_ready, hd.g * NT + j + 1)
                last = a.activation(probs[p][:, i, 0:n], bank[S_BANK[i % 2]][:, 0:n], ACT.Exp,
                                    bias=neg_max[:, p, i:i + 1], scale=-1.0, accum_out=sum_x[:, p, i:i + 1])
                if hd.kind == "X":
                    last = a.activation(probs[p][:, i, S:S + C], bank[C_BANK][:, i * C:(i + 1) * C], ACT.Exp,
                                        bias=neg_max[:, p, i:i + 1], accum_out=sum_c[:, p, i:i + 1])
                last.then_inc(probs_ready, 1)

            def t_copy(hd, c):
                act.wait_ge(t_mm, hd.c0 + c + 1)
                k = C if c == NT else P
                lo = 0 if hd.kind == "X" else c * P
                a.copy(pT[0:k, c, lo:S], bank[T_BANK[0]][0:k, lo:S]).then_inc(pT_even, 1)

            def prologue(h0, h1, h2):
                for j in range(NT):
                    e_tile(h0, j)

            def step(hs, ht, hn, hw, middle):
                t_copy(ht, 0)
                if hs:
                    e_tile(hs, 0)
                t_copy(ht, 2)
                if hs:
                    e_tile(hs, 1)
                middle()
                if hs:
                    e_tile(hs, 2)
                if ht.chunks > 4:
                    t_copy(ht, 4)
                if hs:
                    e_tile(hs, 3)

            run_attention(act, do, "X", X_HOOKS, prologue, step)
            f_gelu(0)
            f_gelu(1)
            follow(do, F_ITEMS)
            run_attention(act, do, "D", D_HOOKS, prologue, step)

            def m_gelu(i, n):
                g, m = m_at(i, n), n % NM
                if isinstance(i, int):
                    bias = M_b1[:, n:n + 1]
                else:
                    k = n // NM
                    bias = M_b1g[k][:, m:m + 1]
                    if m == 0:
                        act.wait_ge(m_bias[k], i * 16 - 16)
                gelu((n, g), ACT.Gelu, bias)
                if n % 2 == 0:
                    gelu_hi((n, g))

            act.wait_ge(ld["M_b1"], 16)
            do["chunk"] = lambda n: m_gelu(0, n + 2)
            m_gelu(0, 0)
            m_gelu(0, 1)
            follow(do, M_ITEMS)
            with act.Fori(2, GROUPS) as i:
                for n in range(GROUP_CHUNKS):
                    m_gelu(i, n)

        @block.vector
        def _(dve):
            v = nc.vector

            def ln_stats_of(stage, b):
                n = ln_index(stage, b)
                if stage == "A":
                    dve.wait_ge(ld[f"x{b}"], 16)
                elif stage in READ_BY_LN:
                    dve.wait_ge(x_written[b], READ_BY_LN[stage])
                else:
                    dve.wait_ge(o_added, (B * H if stage == "E" else 0) + H * (b + 1) + 1)
                for i in range(NT):
                    last = v.bn_stats(bn[:, b, i, :], x[b][:, i, :])
                last.then_inc(ln_bn, 1)
                dve.wait_ge(ln_bn, n + 1)
                for i in range(NT):
                    last = v.bn_aggr(mv[:, b, i, :], bn[:, b, i, :])
                last.then_inc(ln_stats, 1)

            def ln_hat_of(stage, b):
                dve.wait_ge(ln_rstd, ln_index(stage, b) + 1)
                for i in range(NT):
                    last = v.tensor_scalar(xhat[b][:, i, :], x[b][:, i, :], mv[:, b, i, 0:1], rstd[:, b, i:i + 1],
                                           ALU.subtract, ALU.mult)
                last.then_inc(ln_hat, 1)

            def split_z(stage, b):
                n = z_index(stage, b)
                dve.wait_ge(ln_xT, ln_index(stage, b) + 1)
                v.tensor_copy(z_hi[b][:], xT[b][:]).then_inc(z_hi_s, 1)
                dve.wait_ge(z_hi_s, n + 1)
                v.tensor_tensor(z_lo[b][:], xT[b][:], z_hi[b][:], ALU.subtract).then_inc(z_split, 1)

            def keys(kind, b):
                n = v_index(kind, b)
                full = xT[b][:]
                if kind == "D":
                    full = flat(xhat[b][:])
                    dve.wait_ge(d_k_mm, b + 1)
                    v.scalar_tensor_tensor(full, bank[2][:], col("D_bk"), const("peT", S), ALU.add,
                                           ALU.add).then_inc(d_k_full, 1)
                    dve.wait_ge(d_k_full, b + 1)
                v.tensor_scalar(k_hi[b][:], full, SCALE, None, ALU.mult).then_inc(k_hi_s, 1)
                dve.wait_ge(k_hi_s, n + 1)
                v.scalar_tensor_tensor(k_lo[b][:], full, SCALE, k_hi[b][:], ALU.mult,
                                       ALU.subtract).then_inc(keys_ready, 1)

            def vall_piece(kind, b, i):
                dve.wait_ge(vall_mm, 2 * NT * v_index(kind, b) + 2 * i + 2)
                v.tensor_copy(vall[b][:, i, S:2 * S], bank[V_BANK[f"{kind}{b}"][1]][:]).then_inc(vall_odd, 1)

            def f_gate(b):
                dve.wait_ge(f_lg_mm, b + 1)
                v.tensor_tensor(f_lg[:, b], bank[TR_BANK[f"F{b}"]][:, 0:NE], row("F_b_gate", NE),
                                ALU.add).then_inc(f_pick, 1)
                dve.wait_ge(f_pick, 4 * b + 1)
                v.max(f_max[:, b], f_lg[:, b]).then_inc(f_pick, 1)
                dve.wait_ge(f_pick, 4 * b + 2)
                v.max_index(f_idx[:, b], f_max[:, b], f_lg[:, b]).then_inc(f_idx_s, 1)
                v.tensor_scalar(f_nmax[:, b:b + 1], f_max[:, b, 0:1], -1.0, None, ALU.mult).then_inc(f_nmax_s, 1)

            def f_split(b, k):
                if k == 0:
                    dve.wait_ge(f_exp, b + 1)
                    v.reciprocal(f_ers[:, b:b + 1], f_es[:, b:b + 1]).then_inc(f_pick, 1)
                    dve.wait_ge(f_pick, 4 * b + 3)
                    v.tensor_scalar(f_g[:, b, :], f_e[:, b, :], f_ers[:, b:b + 1], f_1a[:], ALU.mult,
                                    ALU.mult).then_inc(f_pick, 1)
                    dve.wait_ge(f_pick, 4 * b + 4)
                dve.wait_ge(f_ld[b][k], 4 * 16)
                v.tensor_scalar(F_W2e[b][k][:], F_W2e[b][k][:], f_g[:, b, k:k + 1], None, ALU.mult).then_inc(f_w2, 1)
                if k == 0:
                    v.scalar_tensor_tensor(f_bias1[:, b:b + 1], F_b2e[:, b, 0:1], f_g[:, b, 0:1], f_bias0[:],
                                           ALU.mult, ALU.add).then_inc(f_bias_s, 1)
                else:
                    dve.wait_ge(f_bias_s, 2 * b + 1)
                    v.scalar_tensor_tensor(f_bias[:, b:b + 1], F_b2e[:, b, 1:2], f_g[:, b, 1:2],
                                           f_bias1[:, b:b + 1], ALU.mult, ALU.add).then_inc(f_bias_s, 1)

            def split_h(k, g, pairs):
                slot = k % 4
                if k % 2:
                    dve.wait_ge(h_gelu, g + 1)
                    if not (isinstance(g, int) and g < 4):
                        dve.wait_ge(y_mm, g - 3)
                    v.tensor_copy(h_hi[slot][:], h_full[slot][:]).then_inc(h_hi_odd, 1)
                elif not (isinstance(g, int) and g < 4):
                    dve.wait_ge(y_mm, g - 3)
                dve.wait_ge(h_hi_odd if k % 2 else h_hi_even, pairs + 1)
                v.tensor_tensor(h_lo[slot][:], h_full[slot][:], h_hi[slot][:], ALU.subtract).then_inc(h_split, 1)

            def f_split_h(n):
                if n < F_CHUNKS:
                    split_h(n, n, n // 2)

            def f_out(b):
                dve.wait_ge(f_out_mm, b + 1)
                v.tensor_tensor(x[b][:], tiled(bank[5 + b][:]), x[b][:], ALU.add).then_inc(x_written[b], 1)

            def e_s_piece(b):
                dve.wait_ge(e_s_mm, b + 1)
                v.tensor_tensor(flat(e_s[b][:]), bank[EB[b]][:, 0:NT * C],
                                e_lim[:, b * NT * C:(b + 1) * NT * C], ALU.min).then_inc(e_norm, 1)
                dve.wait_ge(e_norm, 6 * b + 1)
                v.tensor_reduce(e_nmax[:, b], e_s[b][:], AX, ALU.max, negate=True).then_inc(e_max, 1)

            def e_o_piece(b):
                dve.wait_ge(e_exp, b + 1)
                v.reciprocal(e_rsum[:, b], e_sum[:, b]).then_inc(e_norm, 1)
                dve.wait_ge(e_norm, 6 * b + 2)
                v.tensor_tensor(e_rsum2[:, b], e_rsum[:, b], e_rsum[:, b], ALU.mult).then_inc(e_norm, 1)
                dve.wait_ge(e_o_mm, b + 1)
                for i in range(NT):
                    last = v.bn_stats(bn[:, b, i, :], bank[EB[b]][:, i * P:(i + 1) * P])
                last.then_inc(e_norm, 1)
                dve.wait_ge(e_norm, 6 * b + 4)
                for i in range(NT):
                    last = v.bn_aggr(mv[:, b, i, :], bn[:, b, i, :])
                last.then_inc(e_st, 1)

            def e_ln_piece(b):
                dve.wait_ge(e_r, b + 1)
                for i in range(NT):
                    last = v.tensor_scalar(e_on[b][:, i, :], bank[EB[b]][:, i * P:(i + 1) * P], mv[:, b, i, 0:1],
                                           rstd[:, b, i:i + 1], ALU.subtract, ALU.mult)
                last.then_inc(e_norm, 1)
                dve.wait_ge(e_norm, 6 * b + 5)
                v.tensor_tensor(e_og[b][:], e_on[b][:], row("ln_gamma").unsqueeze(1).to_broadcast((P, NT, P)),
                                ALU.mult).then_inc(e_norm, 1)
                dve.wait_ge(e_norm, 6 * b + 6)
                dve.wait_ge(x_written[b], W_E_BETA)
                v.tensor_tensor(x[b][:], e_og[b][:], x[b][:], ALU.add).then_inc(x_written[b], 1)

            done = [0]

            def then(ins):
                done[0] += 1
                ins.then_inc(m_chain, 1)
                dve.wait_ge(m_chain, done[0])

            def m_router(b):
                tiles = (P, NT, NL)
                lang = m_lg[b][:, :, NE:NE + NL]
                dve.wait_ge(m_lg_mm, b + 1)
                then(v.tensor_tensor(m_lg[b][:],
                                     bank[EB[b]][:, 0:NT * (NE + NL)].rearrange("p (n e) -> p n e", n=NT),
                                     row("M_bias", NE + NL).unsqueeze(1).to_broadcast((P, NT, NE + NL)), ALU.add))
                then(v.tensor_reduce(m_lmax[:, b], lang, AX, ALU.max))
                then(v.tensor_tensor(m_ld[:, b], lang, m_lmax[:, b].unsqueeze(2).to_broadcast(tiles), ALU.subtract))

            def m_lang(b):
                tiles = (P, NT, NL)
                dve.wait_ge(m_lexp, b + 1)
                then(v.tensor_reduce(m_ls[:, b], m_le[:, b], AX, ALU.add))
                then(v.reciprocal(m_lr[:, b], m_ls[:, b]))
                then(v.tensor_tensor(m_lp[:, b, :, 0:NL], m_le[:, b], m_lr[:, b].unsqueeze(2).to_broadcast(tiles),
                                     ALU.mult))
                then(v.tensor_tensor(m_ew[:, b], m_lp[:, b, :, 0:NL], m_lp[:, b, :, 1:NL + 1], ALU.add))
                v.scalar_tensor_tensor(m_rl[b][:, :, 0:NL], m_ew[:, b], 0.1, m_lg[b][:, :, 0:NL], ALU.mult, ALU.add)
                then(v.scalar_tensor_tensor(m_rl[b][:, :, NL:NE], m_ew[:, b], 0.1, m_lg[b][:, :, NL:NE], ALU.mult,
                                            ALU.add))
                for i in range(NT):
                    last = v.max(m_max[:, b, i, :], m_rl[b][:, i, :])
                then(last)
                for i in range(NT):
                    last = v.max_index(m_idx[:, b, i, :], m_max[:, b, i, :], m_rl[b][:, i, :])
                then(last)
                then(v.tensor_tensor(m_d[:, b], m_max[:, b, :, 1], m_max[:, b, :, 0], ALU.subtract))
                assert done[0] == M_CHAIN * b + M_CHAIN_D

            def m_best(b):
                then(v.tensor_copy(m_idxf[:, b], m_idx[:, b, :, 0:2]))
                dve.wait_ge(m_exp, b + 1)
                then(v.tensor_scalar(m_s[:, b], m_e[:, b], 1.0, None, ALU.add))
                then(v.reciprocal(m_g0[:, b], m_s[:, b]))
                then(v.tensor_tensor(m_g1[:, b], m_g0[:, b], m_e[:, b], ALU.mult))
                for k, gk in enumerate((m_g0, m_g1)):
                    then(v.tensor_tensor(m_oh[:, b, k], const("iota", NE).unsqueeze(1).to_broadcast((P, NT, NE)),
                                         m_idxf[:, b, :, k:k + 1].to_broadcast((P, NT, NE)), ALU.is_equal))
                    then(v.tensor_tensor(m_og[:, b, k], m_oh[:, b, k],
                                         gk[:, b].unsqueeze(2).to_broadcast((P, NT, NE)), ALU.mult))
                assert done[0] == M_CHAIN * (b + 1)
                v.tensor_tensor(gates[b][:], m_og[:, b, 0], m_og[:, b, 1], ALU.add).then_inc(m_gates, 1)

            do = {"stats": ln_stats_of, "hat": ln_hat_of, "split": split_z, "keys": keys, "vall": vall_piece,
                  "F_gate": f_gate, "F_split": f_split, "chunk": lambda n: f_split_h(n + 1), "F_out": f_out, "E_s": e_s_piece,
                  "E_o": e_o_piece, "E_ln": e_ln_piece, "M_router": m_router, "M_lang": m_lang, "M_best": m_best}

            def q_copy(hd):
                p = hd.par
                dve.wait_ge(r_mm, hd.g + 1)
                src = bank[R_BANK][:]
                if not (hd.kind == "X" and hd.b == 0 and isinstance(hd.h, int) and hd.h < 2):
                    dve.wait_ge(q_ready, hd.g - 1)
                    dve.wait_ge(c_s_mm, hd.g - 1 if hd.kind == "X" else B * H)
                if hd.kind == "X":
                    v.tensor_scalar(q_full[p][:], src, X_r0[:, bass.ds(hd.h, 1)], None, ALU.add).then_inc(q_first, 1)
                else:
                    v.scalar_tensor_tensor(q_full[p][:], src, cols[:, bass.ds(hd.h + COLS["D_bq"], 1)],
                                           const("peT", S), ALU.add, ALU.add).then_inc(q_first, 1)
                dve.wait_ge(q_first, hd.g + 1)
                if not (hd.kind == "X" and hd.b == 0 and isinstance(hd.h, int) and hd.h < 2):
                    dve.wait_ge(s_mm, (hd.g - 1) * NT)
                v.tensor_copy(q_hi[p][:], q_full[p][:]).then_inc(q_hi_s, 1)

            ln_stats_of("A", 0)
            ln_stats_of("A", 1)
            ln_hat_of("A", 0)
            ln_hat_of("A", 1)
            dve.wait_ge(ld["consts"], 16)
            dve.wait_ge(ld["rows"], 16)
            v.tensor_copy(a_mask[:, 0:P], const("blocks", P)).then_inc(a_mask_ready, 1)
            v.tensor_tensor(a_mask[:, P:2 * P], const("blocks", P), row("norm_g"), ALU.mult).then_inc(a_mask_ready, 1)
            dve.wait_ge(a_mask_ready, 2)
            dve.wait_ge(ld["ctx"], 16)
            for b in range(B):
                last = v.bn_stats(c_bn[:, b, :], ctx_tok[:, b, :])
            last.then_inc(c_bn_s, 1)
            dve.wait_ge(c_bn_s, 1)
            for b in range(B):
                last = v.bn_aggr(c_mv[:, b, :], c_bn[:, b, :])
            last.then_inc(c_stats, 1)
            dve.wait_ge(c_rstd_s, 1)
            for b in range(B):
                last = v.tensor_scalar(c_hat[:, b, :], ctx_tok[:, b, :], c_mv[:, b, 0:1], c_rstd[:, b:b + 1],
                                       ALU.subtract, ALU.mult)
            last.then_inc(c_hat_s, 1)
            dve.wait_ge(ld["cols"], 16)
            for b in range(B):
                dve.wait_ge(a_kv_mm, b + 1)
                v.tensor_copy(kv[b][:, 0:S], bank[4 * b + 2][:])
                v.tensor_copy(kv[b][:, S:2 * S], bank[4 * b + 3][:]).then_inc(a_kv, 1)
            for b in range(B):
                dve.wait_ge(a_g_mm, b + 1)
                v.tensor_tensor(gm[b][:], bank[4 * b][:, 0:2 * P], a_mask[:], ALU.mult)
                v.tensor_tensor(vsum[:, b:b + 1], bank[4 * b][:, 2 * P:2 * P + 1], col("norm_b"),
                                ALU.mult).then_inc(a_g, 1)
            for b in range(B):
                dve.wait_ge(a_gq_mm, b + 1)
                dve.wait_ge(a_q, b + 1)
                v.tensor_tensor(t1[b][:], bank[4 * b + 1][:], qT[b][:], ALU.mult).then_inc(a_t1, 1)
            for b in range(B):
                dve.wait_ge(a_n2_mm, b + 1)
                v.tensor_scalar(norm2[:, b], bank[4 * b + 2][:, 0:NT * HA], NORM_EPS ** 2, None,
                                ALU.max).then_inc(a_n2, 1)
            dve.wait_ge(w_a_mm, 2)
            v.tensor_copy(flat(X_A[:, 4:8, :]), bank[5][:]).then_inc(w_a, 1)
            for b in range(B):
                dve.wait_ge(a_norm, b + 1)
                v.reciprocal(rnorm[:, b], norm1[:, b]).then_inc(a_rnorm, 1)
                dve.wait_ge(a_rnorm, b + 1)
                dve.wait_ge(a_o_mm, b + 1)
                heads = "p (g e) -> p g e"
                v.tensor_tensor(kv[b][:, 0:S].rearrange(heads, e=P // HA),
                                bank[4 * b + 3][:].rearrange(heads, e=P // HA),
                                rnorm[:, b].unsqueeze(2).to_broadcast((P, NT * HA, P // HA)),
                                ALU.mult).then_inc(a_o, 1)
            dve.wait_ge(c_zT, 1)
            dve.wait_ge(fills, 2)
            v.tensor_scalar(cz_scaled[:], czT[:], SCALE, None, ALU.mult).then_inc(c_scaled, 1)
            dve.wait_ge(w_v_mm, 2)
            v.tensor_copy(flat(X_V[:, 4:8, :]), bank[6][:]).then_inc(w_v, 1)
            for b in range(B):
                dve.wait_ge(a_y_mm, b + 1)
                dve.wait_ge(x_written[b], W_A_BIAS)
                v.tensor_tensor(x[b][:], tiled(bank[4 * b + 1][:]), x[b][:], ALU.add).then_inc(x_written[b], 1)
                ln_stats_of("X", b)
            ln_hat_of("X", 0)
            dve.wait_ge(w_b_mm, 1)
            v.tensor_copy(X_r0[:], bank[3][:, 0:H]).then_inc(w_bias, 1)
            v.tensor_tensor(X_bias[:], bank[7][:, 0:P], row("X_bo"), ALU.add).then_inc(w_bias, 1)
            ln_hat_of("X", 1)

            def context_values(b):
                dve.wait_ge(w_vc_mm, b + 1)
                for half in range(2):
                    last = v.tensor_copy(X_vc[:, b, half * S:(half + 1) * S], bank[VC_BANK[b][half]][0:C, :])
                last.then_inc(w_vc, 1)

            context_values(0)
            split_z("X", 0)
            keys("X", 0)
            q_copy(Head("X", 0, 0, 0))
            context_values(1)
            dve.wait_ge(e_kv_mm, 1)
            v.tensor_scalar(flat(e_kT[:]), bank[7][:, 0:B * C], col("E_bk"), SCALE, ALU.add, ALU.mult).then_inc(e_k_s, 1)
            v.tensor_tensor(e_v[:], bank[7][0:C, 2 * P:4 * P].rearrange("c (b d) -> c b d", b=B),
                            rows[0:C, ROWS["E_bv"]:ROWS["E_bv"] + P].unsqueeze(1).to_broadcast((C, B, P)),
                            ALU.add).then_inc(e_v_s, 1)
            for i in range(NT):
                vall_piece("X", 0, i)

            def limits_and_alpha():
                dve.wait_ge(ld["mask"], 16)
                v.tensor_scalar(e_tmp[:], mask[:].rearrange("p b n c -> p (b n c)"), 0.0, -2.0, ALU.is_equal,
                                ALU.mult).then_inc(e_lim_s, 1)
                dve.wait_ge(e_lim_s, 1)
                v.tensor_scalar(e_lim[:], e_tmp[:], 1.0, BIG, ALU.add, ALU.mult).then_inc(e_lim_s, 1)
                v.tensor_scalar(f_a[:], row("alpha", 1), 0.1, 1.0, ALU.max, ALU.min).then_inc(f_alpha, 1)
                dve.wait_ge(f_alpha, 1)
                v.tensor_scalar(f_1a[:], f_a[:], -1.0, 1.0, ALU.mult, ALU.add).then_inc(f_alpha, 1)
                dve.wait_ge(ld["F_W"], 3 * 16)
                v.tensor_scalar(F_W2m[:], F_W2m[:], f_a[:], None, ALU.mult).then_inc(f_w2, 1)
                v.tensor_tensor(f_bias0[:], col("F_b2m"), f_a[:], ALU.mult).then_inc(f_alpha, 1)
                dve.wait_ge(f_alpha, 3)

            def c_max(hd):
                if hd.kind == "X":
                    dve.wait_ge(c_s_mm, hd.g + 1)
                    v.tensor_reduce(neg_cmax[:, hd.par, :],
                                    bank[C_BANK][:, 0:NT * C].rearrange("p (n c) -> p n c", c=C),
                                    AX, ALU.max, negate=True).then_inc(cmax_ready, 1)
                    dve.wait_ge(cmax_ready, hd.g + 1)

            def x_max(hd, j):
                i, n = ORDER[j], hd.keys(ORDER[j])
                dve.wait_ge(s_mm, hd.g * NT + j + 1)
                scores = bank[S_BANK[i % 2]][:, 0:n]
                v.tensor_scalar(scores, scores, -1.0, neg_cmax[:, hd.par, i:i + 1] if hd.kind == "X" else None,
                                ALU.mult, ALU.min, accum_out=neg_max[:, hd.par, i:i + 1]).then_inc(max_ready, 1)

            def t_copy(hd, c):
                dve.wait_ge(t_mm, hd.c0 + c + 1)
                lo = 0 if hd.kind == "X" else c * P
                v.tensor_copy(pT[:, c, lo:S], bank[T_BANK[1]][:, lo:S]).then_inc(pT_odd, 1)

            def add_head(hd):
                p = hd.par
                dve.wait_ge(probs_ready, (hd.g + 1) * NT)
                if hd.kind == "X":
                    v.tensor_tensor(denom[:, p], sum_x[:, p], sum_c[:, p], ALU.add).then_inc(denom_ready, 1)
                    dve.wait_ge(denom_ready, hd.g + 1)
                    v.reciprocal(rdenom[:, p], denom[:, p]).then_inc(rdenom_ready, 1)
                else:
                    v.reciprocal(rdenom[:, p], sum_x[:, p]).then_inc(rdenom_ready, 1)
                dve.wait_ge(rdenom_ready, hd.g + 1)
                dve.wait_ge(o_mm, hd.g + 1)
                dve.wait_ge(x_written[hd.b], W_X_BIAS if hd.kind == "X" else W_F)
                dve.wait_ge(o_added, hd.g + 1)
                for i in range(NT):
                    last = v.scalar_tensor_tensor(x[hd.b][:, i, :], bank[O_BANK][:, i * P:(i + 1) * P],
                                                  rdenom[:, p, i:i + 1], x[hd.b][:, i, :], ALU.mult, ALU.add)
                last.then_inc(o_added, 1)

            def prologue(h0, h1, h2):
                if h0.kind == "X":
                    v.memset(o_start[:], 0.0).then_inc(o_added, 1)
                c_max(h0)
                for j in range(NT):
                    x_max(h0, j)
                q_copy(h1)
                if h0.kind == "X":
                    limits_and_alpha()

            def step(hs, ht, hn, hw, middle):
                if hs:
                    c_max(hs)
                    x_max(hs, 0)
                t_copy(ht, 1)
                if hn:
                    q_copy(hn)
                if hs:
                    x_max(hs, 1)
                middle()
                if hs:
                    x_max(hs, 2)
                t_copy(ht, 3)
                if hs:
                    x_max(hs, 3)
                add_head(ht)

            do["first_q"] = lambda kind: q_copy(Head(kind, 0, 0, 0))
            run_attention(dve, do, "X", X_HOOKS, prologue, step)
            f_split_h(0)
            follow(do, F_ITEMS)
            run_attention(dve, do, "D", D_HOOKS, prologue, step)

            def gate_unit(i, u):
                b = u // NE if isinstance(i, int) else 1
                gate = gates_bc[:, bass.ds(i * GROUP + u, 1), :].rearrange("p e s -> p (e s)")
                dve.wait_ge(m_gates_bc[b], 16 * NE)
                dve.wait_ge(y_mm, m_at(i, NM * (u + 1)))
                if not (isinstance(i, int) and u < 2):
                    dve.wait_ge(y_added, i * 4 + (u - 1))
                v.tensor_tensor(y_gated[u % 2][:], bank[Y_BANK[u % 2]][:], gate, ALU.mult).then_inc(y_gated_s, 1)

            def m_split_h(i, n):
                split_h(n, m_at(i, n), i * (GROUP_CHUNKS // 2) + (F_CHUNKS + n) // 2)
                if n % NM == 1 and not (isinstance(i, int) and n < NM):
                    gate_unit(i, n // NM - 1)

            def store_batch(b):
                dve.wait_ge(m_out_mm, b + 1)
                v.tensor_tensor(x[b][:], tiled(bank[5 + b][:]), x[b][:], ALU.add).then_inc(x_written[b], 1)

            do["chunk"] = lambda n: m_split_h(0, n + 1)
            m_split_h(0, 0)
            follow(do, M_ITEMS)
            m_split_h(0, 31)
            with dve.Fori(2, GROUPS) as i:
                for n in range(GROUP_CHUNKS):
                    m_split_h(i, n)
            dve.wait_ge(y_mm, m_at(GROUPS, 0))
            dve.wait_ge(y_added, B * NE - 2)
            v.tensor_tensor(y_gated[1][:], bank[Y_BANK[1]][:], gates_bc[:, B * NE - 1, :],
                            ALU.mult).then_inc(y_gated_s, 1)
            for b in range(B):
                store_batch(b)

        @block.tensor
        def _(pe):
            def mm(out, lhsT, rhs, start=True, stop=True):
                return nc.tensor.matmul(out, lhsT, rhs, start=start, stop=stop, skip_group_check=True)

            def mm3(out, l_hi, l_lo, r_hi, r_lo, start=True, stop=True):
                mm(out, l_hi, r_hi, start, False)
                mm(out, l_hi, r_lo, False, False)
                return mm(out, l_lo, r_hi, False, stop)

            def tile_of(bk, i, n=P):
                return bank[bk][:, i * n:(i + 1) * n]

            def turnx(stage, b):
                pe.wait_ge(ln_hat, ln_index(stage, b) + 1)
                for i in range(NT):
                    last = nc.tensor.transpose(tile_of(TR_BANK[f"{stage}{b}"], i), xhat[b][:, i, :], ident)
                last.then_inc(ln_mm, 1)

            def keys(kind, b):
                if kind == "D":
                    pe.wait_ge(ln_xT, ln_index("D", b) + 1)
                    mm(bank[2][:], D_Wkv[:, 0:P], xT[b][:]).then_inc(d_k_mm, 1)
                    mm(bank[6][:], D_Wkv[:, P:2 * P], xT[b][:]).then_inc(d_v_mm, 1)

            def vall_piece(kind, b, i):
                n0 = v_index(kind, b)
                w = X_V if kind == "X" else D_Wo
                if i == 0 and kind == "X":
                    pe.wait_ge(ln_xT, ln_index("X", b) + 1)
                    if b:
                        pe.wait_ge(q_first, H)
                elif i == 0:
                    pe.wait_ge(d_v_ready, b + 1)
                    pe.wait_ge(d_k_full, b + 1)
                src = xT[b] if kind == "X" else valuesT[b]
                for half in range(2):
                    if i:
                        pe.wait_ge((vall_even, vall_odd)[half], NT * n0 + i)
                    mm(bank[V_BANK[f"{kind}{b}"][half]][:], src[:, i * P:(i + 1) * P],
                       flat(w[:, 4 * half:4 * half + 4, :])).then_inc(vall_mm, 1)
                if i == NT - 1:
                    pe.wait_ge(vall_even, NT * (n0 + 1))
                    pe.wait_ge(vall_odd, NT * (n0 + 1))

            def f_gate(b):
                pe.wait_ge(f_mean, b + 1)
                mm(bank[TR_BANK[f"F{b}"]][:, 0:NE], mean_bc[:, b, :], F_w_gate[:]).then_inc(f_lg_mm, 1)

            def hidden(k, g, slot, b, m):
                if not (isinstance(g, int) and g < 2):
                    pe.wait_ge(h_gelu, g - 1)
                w = slice(m * P, (m + 1) * P)
                mm3(bank[k % 2][:], w1_hi[slot][:, w], w1_lo[slot][:, w], z_hi[b][:], z_lo[b][:]).then_inc(h_mm, 1)

            def output(k, g, slot, bk, m, start, stop):
                pe.wait_ge(h_split, g + 1)
                w = slice(m * P, (m + 1) * P)
                mm3(bank[bk][:], w2_hi[slot][:, w], w2_lo[slot][:, w], h_hi[k % 4][:], h_lo[k % 4][:], start,
                    stop).then_inc(y_mm, 1)

            def f_hidden(n):
                u = n // NM
                b, k = F_UNITS[u]
                if n % NM == 0:
                    if k is None:
                        pe.wait_ge(z_split, z_index("F", b) + 1)
                    pe.wait_ge(ws_ready, {None: 1}.get(k, 2 + 2 * b + (k or 0)))
                hidden(n, n, MAIN if k is None else k, b, n % NM)

            def f_chunk(n):
                if n + 2 < F_CHUNKS:
                    f_hidden(n + 2)
                b, k = F_UNITS[n // NM]
                output(n, n, MAIN if k is None else k, Y_BANK[b], n % NM, k is None and n % NM == 0,
                       k == 1 and n % NM == NM - 1)

            def turn_y(b, bk, s):
                for i in range(NT):
                    last = nc.tensor.transpose(tile_of(bk, i), yT[b][:, i * P:(i + 1) * P], ident)
                last.then_inc(s, 1)

            def f_out(b):
                pe.wait_ge(f_yT, b + 1)
                turn_y(b, 5 + b, f_out_mm)

            def e_q_piece(b):
                pe.wait_ge(ln_xT, ln_index("E", b) + 1)
                mm(bank[EA[b]][:], E_Wq[:], xT[b][:]).then_inc(e_q_mm, 1)

            def e_s_piece(b):
                pe.wait_ge(e_q, b + 1)
                for i in range(NT):
                    last = mm(bank[EB[b]][:, i * C:(i + 1) * C], e_qT[b][:, i, :], e_kT[:, b, :])
                last.then_inc(e_s_mm, 1)

            def e_t_piece(b):
                pe.wait_ge(e_exp, b + 1)
                for i in range(NT):
                    last = nc.tensor.transpose(bank[EA[b]][0:C, i * P:(i + 1) * P], e_p[b][:, i, :], ident)
                last.then_inc(e_t_mm, 1)

            def e_o_piece(b):
                pe.wait_ge(e_pT_s, b + 1)
                for i in range(NT):
                    last = mm(tile_of(EB[b], i), e_pT[b][:, i * P:(i + 1) * P], e_v[:, b, :])
                last.then_inc(e_o_mm, 1)

            def m_router(b):
                pe.wait_ge(ln_xT, ln_index("M", b) + 1)
                for i in range(NT):
                    last = mm(tile_of(EB[b], i, NE + NL), xT[b][:, i * P:(i + 1) * P], M_w[:])
                last.then_inc(m_lg_mm, 1)

            def m_gates_piece(b):
                pe.wait_ge(m_gates, b + 1)
                for i in range(NT):
                    last = nc.tensor.transpose(bank[EA[b]][0:NE, i * P:(i + 1) * P], gates[b][:, i, :], ident)
                last.then_inc(m_gT_mm, 1)

            def m_b2(b):
                pe.wait_ge(m_gT, b + 1)
                mm(bank[EB[b]][:], M_b2[:], gT[b][:]).then_inc(m_b_mm, 1)

            do = {"turnx": turnx, "keys": keys, "vall": vall_piece, "F_gate": f_gate, "chunk": f_chunk, "F_out": f_out,
                  "E_q": e_q_piece, "E_s": e_s_piece, "E_t": e_t_piece, "E_o": e_o_piece, "M_router": m_router,
                  "M_gates": m_gates_piece, "M_b2": m_b2}

            def queries(hd):
                pe.wait_ge(w_ready, hd.g + 1)
                if not hd.very_first:
                    pe.wait_ge(q_first, hd.g)
                mm3(bank[R_BANK][:], w_hi[hd.par][:], w_lo[hd.par][:], z_hi[hd.b][:], z_lo[hd.b][:]).then_inc(r_mm, 1)

            pe.wait_ge(ld["consts"], 16)
            pe.wait_ge(ld["A_wqkvT"], 16)
            for b in range(B):
                turnx("A", b)
            for b in range(B):
                k = 4 * b
                pe.wait_ge(ln_xT, b + 1)
                mm(bank[k + 1][:], A_wqkvT[:, 0:P], xT[b][:]).then_inc(a_q_mm, 1)
                for i in range(NT):
                    last = mm(bank[k + 2 + i // 2][:, (i % 2) * 2 * P:(i % 2 + 1) * 2 * P],
                              xT[b][:, i * P:(i + 1) * P], A_wqkvT[:, P:3 * P])
                last.then_inc(a_kv_mm, 1)
            for b in range(B):
                pe.wait_ge(a_kv, b + 1)
                k4 = kv[b][:].rearrange("p (n w) -> p n w", n=NT)
                for i in range(NT):
                    mm(bank[4 * b][:, 0:2 * P], k4[:, i, 0:P], k4[:, i, :], i == 0, i == NT - 1)
                for i in range(NT):
                    last = mm(bank[4 * b][:, 2 * P:2 * P + 1], k4[:, i, P:2 * P], const("ones", 1), False, i == NT - 1)
                last.then_inc(a_g_mm, 1)
            for b in range(B):
                pe.wait_ge(a_g, b + 1)
                pe.wait_ge(a_q, b + 1)
                mm(bank[4 * b + 1][:], gm[b][:, 0:P], qT[b][:]).then_inc(a_gq_mm, 1)
                for i in range(NT):
                    last = mm(tile_of(4 * b + 3, i), qT[b][:, i * P:(i + 1) * P], gm[b][:, P:2 * P])
                last.then_inc(a_o_mm, 1)
            for b in range(B):
                pe.wait_ge(a_t1, b + 1)
                for i in range(NT):
                    last = mm(tile_of(4 * b + 2, i, HA), t1[b][:, i * P:(i + 1) * P], const("head_sum", HA))
                last.then_inc(a_n2_mm, 1)
            pe.wait_ge(c_hat_s, 1)
            for b in range(B):
                last = nc.tensor.transpose(bank[0][:, b * C:(b + 1) * C], c_hat[:, b, :], ident[0:C, 0:C])
            last.then_inc(c_mm, 1)
            pe.wait_ge(ld["X_Wqk"], 2 * 16)
            for h in range(H):
                last = mm(tile_of((1, 5)[h // 4], h % 4), X_WqT[:, h, :], X_WkT[:, h, :])
                if h % 4 == 3:
                    last.then_inc(w_a_mm, 1)
            pe.wait_ge(c_zT, 1)
            for b in range(B):
                pe.wait_ge(a_o, b + 1)
                for i in range(NT):
                    last = nc.tensor.transpose(tile_of(4 * b, i), kv[b][:, i * P:(i + 1) * P], ident)
                last.then_inc(a_oT_mm, 1)
            pe.wait_ge(ld["X_Wvo"], 2 * 16)
            for h in range(H):
                last = mm(tile_of((2, 6)[h // 4], h % 4), X_WvT[:, h, :], X_Wo[:, h, :])
                if h % 4 == 3:
                    last.then_inc(w_v_mm, 1)
            pe.wait_ge(ld["A_woutT"], 16)
            pe.wait_ge(w_a, 2)
            for b in range(B):
                pe.wait_ge(a_oT, b + 1)
                for i in range(NT):
                    last = mm(tile_of(4 * b + 1, i), t1[b][:, i * P:(i + 1) * P], A_woutT[:])
                last.then_inc(a_y_mm, 1)
            pe.wait_ge(ld["cols"], 16)
            for h in range(H):
                mm(bank[3][:, h:h + 1], X_WkT[:, h, :], col("X_bq", 1, h))
            for h in range(H):
                last = mm(bank[7][:, 0:P], col("X_bv", 1, h).to_broadcast((P, P)), X_Wo[:, h, :], h == 0, h == H - 1)
            last.then_inc(w_b_mm, 1)

            def context_values(b):
                for half in range(2):
                    last = mm(bank[VC_BANK[b][half]][0:C, :], czT[:, b, :], flat(X_V[:, 4 * half:4 * half + 4, :]))
                last.then_inc(w_vc_mm, 1)

            pe.wait_ge(w_v, 2)
            context_values(0)
            turnx("X", 0)
            context_values(1)
            pe.wait_ge(ld["ctxT"], 16)
            pe.wait_ge(ld["E_W"], 3 * 16)
            pe.wait_ge(w_bias, 2)
            mm(bank[7][:, 0:B * C], E_Wk[:], flat(ctxT[:]))
            for b in range(B):
                last = mm(bank[7][0:C, (2 + b) * P:(3 + b) * P], ctxT[:, b, :], E_Wv[:])
            last.then_inc(e_kv_mm, 1)
            pe.wait_ge(x_written[1], W_A)
            pe.wait_ge(z_split, 1)
            queries(Head("X", 0, 0, 0))
            pe.wait_ge(w_vc, 1)
            for i in range(NT):
                vall_piece("X", 0, i)

            def scores_c(hd):
                pe.wait_ge(q_ready, hd.g + 1)
                if hd.kind == "X":
                    if not hd.very_first:
                        pe.wait_ge(probs_ready, hd.g * NT)
                    for i in range(NT):
                        last = mm(tile_of(C_BANK, i, C), q_full[hd.par][:, i * P:(i + 1) * P], cz_scaled[:, hd.b, :])
                    last.then_inc(c_s_mm, 1)

            def scores(hd, j):
                i, n = ORDER[j], hd.keys(ORDER[j])
                if not (hd.very_first and j < 2):
                    pe.wait_ge(probs_ready, hd.g * NT + j - 1)
                dst, w, b = bank[S_BANK[i % 2]], slice(i * P, (i + 1) * P), hd.b
                last = mm3(dst[:, 0:n], q_hi[hd.par][:, w], q_lo[hd.par][:, w], k_hi[b][:, 0:n], k_lo[b][:, 0:n],
                           True, hd.kind == "X")
                if hd.kind == "D":
                    last = mm(dst[:, n - P:n], ident_bf[:], causal_bf[:], False, True)
                last.then_inc(s_mm, 1)

            def turn(hd, c):
                if c == 0:
                    pe.wait_ge(probs_ready, (hd.g + 1) * NT)
                if c >= 2:
                    pe.wait_ge(pT_odd if c % 2 else pT_even, (hd.odd0 if c % 2 else hd.even0) + c // 2)
                k = C if c == NT else P
                for i in range(0 if hd.kind == "X" else c, NT):
                    last = nc.tensor.transpose(bank[T_BANK[c % 2]][0:k, i * P:(i + 1) * P],
                                               probs[hd.par][:, i, c * P:c * P + k], ident)
                last.then_inc(t_mm, 1)

            def weigh(hd, c):
                if c % 2 == 0:
                    pe.wait_ge(pT_even, hd.even0 + c // 2 + 1)
                else:
                    pe.wait_ge(pT_odd, hd.odd0 + c // 2 + 1)
                if c == 0:
                    pe.wait_ge(o_added, hd.g + 1)
                for i in range(0 if hd.kind == "X" else c, NT):
                    if c == NT:
                        l, r = pT[0:C, c, i * P:(i + 1) * P], X_vc[:, hd.b, bass.ds(hd.h * P, P)]
                    else:
                        l, r = pT[:, c, i * P:(i + 1) * P], vall[hd.b][:, c, bass.ds(hd.h * P, P)]
                    last = mm(tile_of(O_BANK, i), l, r, c == 0 and i == 0, c == hd.chunks - 1)
                if c == hd.chunks - 1:
                    last.then_inc(o_mm, 1)

            def prologue(h0, h1, h2):
                pe.wait_ge(z_split, z_index(h0.kind, 0) + 1)
                pe.wait_ge(keys_ready, v_index(h0.kind, 0) + 1)
                scores_c(h0)
                for j in range(NT):
                    scores(h0, j)
                queries(h1)

            def step(hs, ht, hn, hw, middle):
                if hs and hs.kind == "D":
                    scores_c(hs)
                    scores(hs, 0)
                turn(ht, 0)
                if hs and hs.kind == "X":
                    scores_c(hs)
                    scores(hs, 0)
                turn(ht, 1)
                if hn:
                    if isinstance(hn.h, int) and hn.h == 0:
                        pe.wait_ge(z_split, z_index(hn.kind, hn.b) + 1)
                        pe.wait_ge(keys_ready, v_index(hn.kind, hn.b) + 1)
                    queries(hn)
                weigh(ht, 0)
                if hs:
                    scores(hs, 1)
                middle()
                turn(ht, 2)
                weigh(ht, 1)
                if hs:
                    scores(hs, 2)
                turn(ht, 3)
                weigh(ht, 2)
                if hs:
                    scores(hs, 3)
                if ht.chunks > NT:
                    turn(ht, NT)
                weigh(ht, 3)
                if ht.chunks > NT:
                    weigh(ht, NT)

            pe.wait_ge(w_vc, B)
            pe.wait_ge(e_v_s, 1)
            def first_q(kind):
                pe.wait_ge(x_written[0], W_F)
                pe.wait_ge(z_split, z_index(kind, 0) + 1)
                queries(Head(kind, 0, 0, 0))

            do["first_q"] = first_q
            pe.wait_ge(c_scaled, 1)
            run_attention(pe, do, "X", X_HOOKS, prologue, step)
            pe.wait_ge(ld["F_W"], 3 * 16)
            pe.wait_ge(ld["D_W"], 3 * 16)
            pe.wait_ge(ld["M_W"], 2 * 16)
            f_hidden(0)
            f_hidden(1)
            follow(do, F_ITEMS)
            pe.wait_ge(bf_ready, 2)
            run_attention(pe, do, "D", D_HOOKS, prologue, step)

            def m_hidden(i, n):
                k = n // NM
                b = 0 if isinstance(i, int) else 1
                if n % NM == 0:
                    pe.wait_ge(ws_ready, i * 4 + (len(F_UNITS) + k) if b == 0 else i * 4 + (len(F_UNITS) - 4 + k))
                    if n == 0:
                        pe.wait_ge(z_split, z_index("M", b) + 1)
                hidden(n, m_at(i, n), k % 4, b, n % NM)

            def m_output(i, n):
                u = n // NM
                if n % NM == 0 and not (isinstance(i, int) and u < 2):
                    pe.wait_ge(y_gated_s, i * 4 + (u - 1))
                output(n, m_at(i, n), u % 4, Y_BANK[u % 2], n % NM, n % NM == 0, n % NM == NM - 1)

            def store_batch(b):
                pe.wait_ge(y_added, NE * (b + 1))
                turn_y(b, 5 + b, m_out_mm)

            do["chunk"] = lambda n: (m_hidden(0, n + 2), m_output(0, n))
            m_hidden(0, 0)
            m_hidden(0, 1)
            follow(do, M_ITEMS)
            with pe.Fori(2, GROUPS) as i:
                for n in range(GROUP_CHUNKS):
                    m_hidden(i, n)
                    m_output(i, n - 2)
            for n in (-2, -1):
                m_output(GROUPS, n)
            for b in range(B):
                store_batch(b)


M_CHAIN = 19
M_CHAIN_D = 11


def positions():
    pos = np.arange(S, dtype=np.float32)[:, None]
    inv_freq = np.exp(np.float32(-np.log(10000.0)) * np.arange(0, P, 2, dtype=np.float32) / np.float32(P))
    ang = (pos * inv_freq[None, :]).astype(np.float32)
    pe = np.zeros((S, P), np.float32)
    pe[:, 0::2] = np.sin(ang)
    pe[:, 1::2] = np.cos(ang)
    return pe.T


def constants():
    p = np.arange(P)
    blocks = (p[:, None] // (P // HA) == p[None, :] // (P // HA)).astype(np.float32)
    parts = {
        "ident": np.eye(P), "blocks": np.concatenate([blocks, blocks], 1),
        "head_sum": p[:, None] // (P // HA) == np.arange(HA)[None, :],
        "causal": np.where(p[None, :] <= p[:, None], 0.0, NEG),
        "iota": np.broadcast_to(np.arange(NE), (P, NE)), "ones": np.ones((P, 1)), "peT": positions()}
    return np.concatenate([np.asarray(parts[n], np.float32) for n in CONSTS], 1)


def kernel(**inputs):
    import concourse.bacc as bacc
    from concourse.bass_utils import run_bass_kernel_spmd

    w = {n: np.asarray(a) for n, a in inputs.items()}

    def as_cols(v):
        return np.reshape(v, (-1, P)).T

    per_head = P // HA
    bkv = w["L0_xattn_bkv"]
    cols = {
        "norm_b": np.repeat(w["L0_attn_norm_b"].reshape(HA), per_head),
        "gamma_media": w["L0_xattn_gamma_media"], "beta_media": w["L0_xattn_beta_media"],
        "gamma_lat": w["L0_xattn_gamma_lat"], "beta_lat": w["L0_xattn_beta_lat"],
        "X_bq": w["L0_xattn_bq"], "X_bv": bkv[H * P:],
        "F_b1m": w["L0_ffn_b1m"], "F_b2m": w["L0_ffn_b2m"], "D_bq": w["L1_attn_bq"],
        "D_bk": w["L1_attn_bkv"][:P], "D_bv": w["L1_attn_bkv"][P:],
        "E_bq": w["L1_xattn_bq"], "E_bk": w["L1_xattn_bk"]}
    rows = {
        "norm_g": np.repeat(w["L0_attn_norm_g"].reshape(HA), per_head), "A_b_out": w["L0_attn_b_out"],
        "X_bo": w["L0_xattn_bo"], "F_b_gate": w["L0_ffn_b_gate"], "alpha": w["L0_ffn_alpha"],
        "E_bv": w["L1_xattn_bv"], "ln_gamma": w["L1_xattn_ln_gamma"],
        "ln_beta": w["L1_xattn_ln_beta"], "M_bias": np.concatenate([w["L1_ffn_router_b"], w["L1_ffn_lang_b"]])}
    arrays = {
        "x": w["x"], "ctx": w["ctx_1024"], "mask": w["mask_BxSxS2_ik1"],
        "ctxT": w["ctx_1024"].transpose(2, 0, 1),
        "cols": np.concatenate([as_cols(cols[n]) for n in COLS], 1),
        "rows": np.concatenate([rows[n].reshape(1, -1) for n in ROWS], 1),
        "consts": constants(),
        "A_wqkvT": w["L0_attn_w_qkv"].T, "A_woutT": w["L0_attn_w_out"].T,
        "X_WqT": w["L0_xattn_Wq"].T, "X_WkvT": w["L0_xattn_Wkv"].T, "X_Wo": w["L0_xattn_Wo"],
        "F_w_gate": w["L0_ffn_w_gate"], "F_W1m": w["L0_ffn_W1m"], "F_W2m": w["L0_ffn_W2m"],
        "F_W1e": w["L0_ffn_W1e"], "F_W2e": w["L0_ffn_W2e"], "F_b2e": w["L0_ffn_b2e"],
        "F_b1eT": as_cols(w["L0_ffn_b1e"]),
        "D_Wq": w["L1_attn_Wq"], "D_Wkv": w["L1_attn_Wkv"], "D_Wo": w["L1_attn_Wo"],
        "E_Wq": w["L1_xattn_Wq"], "E_Wk": w["L1_xattn_Wk"], "E_Wv": w["L1_xattn_Wv"],
        "M_w": np.concatenate([w["L1_ffn_router_w"], w["L1_ffn_lang_w"]]).T, "M_b2": w["L1_ffn_b2"],
        "M_b1T": as_cols(w["L1_ffn_b1"]), "M_w1": w["L1_ffn_w1"], "M_w2": w["L1_ffn_w2"]}
    arrays = {n: np.ascontiguousarray(a) for n, a in arrays.items()}
    nc = bacc.Bacc("TRN2", target_bir_lowering=False, num_devices=1, dynamic_dma_scratch_size=1024)
    tensors = {n: nc.dram_tensor(n + "_dram", a.shape, mybir.dt.from_np(a.dtype), kind="ExternalInput").ap()
               for n, a in arrays.items()}
    tensors["out"] = nc.dram_tensor("out_dram", (B, S, P), F32, kind="ExternalOutput").ap()
    tensors["gates"] = nc.dram_tensor("gates_dram", (B, NE, S), F32, kind="Internal").ap()
    build(nc, tensors)
    result = run_bass_kernel_spmd(nc, [{n + "_dram": a for n, a in arrays.items()}], core_ids=[0])
    return result.results[0]["out_dram"]
```
